# Optimizing a Trainium2 kernel written in Bass

```python
import numpy as np
import jax
import jax.numpy as jnp

def _softmax(x, axis=-1):
    return jax.nn.softmax(x, axis=axis)

def _gelu(x):
    return jax.nn.gelu(x, approximate=True)

def _silu(x):
    return jax.nn.silu(x)

def _sigmoid(x):
    return jax.nn.sigmoid(x)

def _layernorm(x, axis=-1, eps=1e-05):
    m = jnp.mean(x, axis=axis, keepdims=True)
    v = jnp.var(x, axis=axis, keepdims=True)
    return (x - m) / jnp.sqrt(v + eps)

def _scatter_add(tgt, idx, src, axis=0):
    return tgt.at[idx].add(src)

def _segment_sum(src, seg, n):
    return jax.ops.segment_sum(src, seg, n)
kernel_name = 'mk_gnn_resnorm_d1_gnn_r64_d23efb'

def setup_inputs(seed: int=0):
    np.random.seed(seed)
    _w = jnp.asarray

    def _rec_inputs():
        import jax
        import jax.numpy as jnp
        _gk = jax.random.key(seed)
        x = -0.000202 + 1 * jax.random.normal(jax.random.fold_in(_gk, 1), (100000, 64), jnp.float32)
        src = jax.random.randint(jax.random.fold_in(_gk, 2), (50000,), 0, 100000, jnp.int32)
        dst = jax.random.randint(jax.random.fold_in(_gk, 3), (50000,), 0, 100000, jnp.int32)
        _o = jnp.argsort(dst, stable=True)
        src = src[_o]
        dst = dst[_o]
        edge_attr_32 = -8.62073e-06 + 0.999901 * jax.random.normal(jax.random.fold_in(_gk, 11), (50000, 32), jnp.float32)
        return (x, src, dst, edge_attr_32)
    x, src, dst, edge_attr_32 = _rec_inputs()

    def _L0_gnn_setup():
        import jax, jax.numpy as jnp
        import numpy as np
        N = 100000
        E = 15625
        HID = 64
        EDGE_DIM = 32
        N_STEPS = 4

        def _gru_cell(x, h, W_ih, b_ih, W_hh, b_hh):
            gi = x @ W_ih.T + b_ih
            gh = h @ W_hh.T + b_hh
            i_r, i_z, i_n = jnp.split(gi, 3, axis=-1)
            h_r, h_z, h_n = jnp.split(gh, 3, axis=-1)
            r = jax.nn.sigmoid(i_r + h_r)
            z = jax.nn.sigmoid(i_z + h_z)
            n = jnp.tanh(i_n + r * h_n)
            return (1.0 - z) * n + z * h
        key = jax.random.key(seed)
        ks = jax.random.split(key, 12)
        s = 0.05
        h = jax.random.normal(ks[0], (N, HID), dtype=jnp.float32)
        edge_attr = jax.random.normal(ks[1], (E, EDGE_DIM), dtype=jnp.float32)
        edge_index = jax.random.randint(ks[2], (2, E), 0, N, dtype=jnp.int64)
        W1 = jax.random.normal(ks[3], (HID, EDGE_DIM), dtype=jnp.float32) * s
        b1 = jax.random.normal(ks[4], (HID,), dtype=jnp.float32) * s
        W2 = jax.random.normal(ks[5], (HID, HID), dtype=jnp.float32) * s
        b2 = jax.random.normal(ks[6], (HID,), dtype=jnp.float32) * s
        W_ih = jax.random.normal(ks[7], (3 * HID, HID), dtype=jnp.float32) * s
        b_ih = jax.random.normal(ks[8], (3 * HID,), dtype=jnp.float32) * s
        W_hh = jax.random.normal(ks[9], (3 * HID, HID), dtype=jnp.float32) * s
        b_hh = jax.random.normal(ks[10], (3 * HID,), dtype=jnp.float32) * s
        return {'h': h, 'edge_attr': edge_attr, 'edge_index': edge_index, 'W1': W1, 'b1': b1, 'W2': W2, 'b2': b2, 'W_ih': W_ih, 'b_ih': b_ih, 'W_hh': W_hh, 'b_hh': b_hh}
    _L0_gnn_all = _L0_gnn_setup()
    _L0_gnn_in = {k: v for k, v in _L0_gnn_all.items() if k in ('W1', 'b1', 'W2', 'b2', 'W_ih', 'b_ih', 'W_hh', 'b_hh')}
    del _L0_gnn_all
    return {'x': x, 'src': src, 'dst': dst, 'edge_attr_32': edge_attr_32, 'L0_gnn_W1': _L0_gnn_in['W1'], 'L0_gnn_b1': _L0_gnn_in['b1'], 'L0_gnn_W2': _L0_gnn_in['W2'], 'L0_gnn_b2': _L0_gnn_in['b2'], 'L0_gnn_W_ih': _L0_gnn_in['W_ih'], 'L0_gnn_b_ih': _L0_gnn_in['b_ih'], 'L0_gnn_W_hh': _L0_gnn_in['W_hh'], 'L0_gnn_b_hh': _L0_gnn_in['b_hh']}

def reference(x, src, dst, edge_attr_32, L0_gnn_W1, L0_gnn_b1, L0_gnn_W2, L0_gnn_b2, L0_gnn_W_ih, L0_gnn_b_ih, L0_gnn_W_hh, L0_gnn_b_hh):
    import jax
    import jax.numpy as jnp

    def _L0_gnn_ref(h, edge_attr, edge_index, W1, b1, W2, b2, W_ih, b_ih, W_hh, b_hh):
        import jax, jax.numpy as jnp
        import numpy as np
        N = 100000
        E = 15625
        HID = 64
        EDGE_DIM = 32
        N_STEPS = 4

        def _gru_cell(x, h, W_ih, b_ih, W_hh, b_hh):
            gi = x @ W_ih.T + b_ih
            gh = h @ W_hh.T + b_hh
            i_r, i_z, i_n = jnp.split(gi, 3, axis=-1)
            h_r, h_z, h_n = jnp.split(gh, 3, axis=-1)
            r = jax.nn.sigmoid(i_r + h_r)
            z = jax.nn.sigmoid(i_z + h_z)
            n = jnp.tanh(i_n + r * h_n)
            return (1.0 - z) * n + z * h
        i, j = (edge_index[0], edge_index[1])
        msg_base = jax.nn.relu(edge_attr @ W1.T + b1) @ W2.T + b2
        for _ in range(N_STEPS):
            msg = msg_base * h[j]
            agg = jax.ops.segment_sum(msg, i, num_segments=N)
            h = _gru_cell(agg, h, W_ih, b_ih, W_hh, b_hh)
        return h
    edge_index = jnp.stack([src, dst])
    x = _layernorm(x + _L0_gnn_ref(x, edge_attr_32, edge_index, L0_gnn_W1, L0_gnn_b1, L0_gnn_W2, L0_gnn_b2, L0_gnn_W_ih, L0_gnn_b_ih, L0_gnn_W_hh, L0_gnn_b_hh), axis=-1)
    return x

_drawn_inputs = setup_inputs


def setup_inputs(seed=0):
    import zlib

    import numpy as np

    out = dict(_drawn_inputs(seed))
    spreads = {}
    factors = {'edge_attr_32': 8.0,
     'L0_gnn_W1': 8.0,
     'L0_gnn_b1': 8.0,
     'L0_gnn_W2': 8.0,
     'L0_gnn_b2': 8.0,
     'L0_gnn_W_ih': 7.885}
    for name, (base, spread) in spreads.items():
        noise = np.random.default_rng([zlib.crc32(name.encode()), seed]).standard_normal(out[name].shape)
        drawn = base * np.exp(spread * noise) if base else spread * noise
        out[name] = jnp.asarray(drawn.astype(out[name].dtype))
    for name, factor in factors.items():
        out[name] = (out[name] * factor).astype(out[name].dtype)
    return out
```

```python
from contextlib import ExitStack

import concourse.bass as bass
from concourse import mybir

ALU = mybir.AluOpType
ACT = mybir.ActivationFunctionType
F32 = mybir.dt.float32
BF16 = mybir.dt.bfloat16
I32 = mybir.dt.int32
AX_X = mybir.AxisListType.X

P = 128
N = 100000
E = 50000
HID = 64
ED = 32
STEPS = 4
EPS = 1e-5

SORT_COLS = 512
BLOCKS = 4
BLOCK_E = E // BLOCKS
LOAD_P = 125
LOAD_F = BLOCK_E // LOAD_P
LOCAL_BITS = 14
KEY_SHIFT = 512
PAD_KEY = N + 351

GT = 8
GROUPS = (E + GT * P - 1) // (GT * P)
TILES = GROUPS * GT
SLOTS = TILES * P
ROW = ED + 1

NU = 4
NODE_TILE = P * NU
NODE_TILES = (N + NODE_TILE - 1) // NODE_TILE
JT = 4
ITERS = NODE_TILES // JT
UNITS = JT * STEPS
LAST_BASE = N - NODE_TILE
LAST_NEW_P = (NODE_TILES * NODE_TILE - N) // NU
MAP_COLS = (N + P - 1) // P
assert NODE_TILES == ITERS * JT and ITERS == GROUPS and ITERS % 2 == 1
NEWTON = 4
NEWTON_OPS = 4 + 3 * NEWTON


def gnn_program(nc, x, src, dst, attr, w1t, b1, w2t, b2, wit, bih, wht, bhh, out):
    edge_rows = nc.dram_tensor("edge_rows", (E, ROW), F32, kind="Internal").ap()
    row_map = nc.dram_tensor("row_map", (P * MAP_COLS, 1), I32, kind="Internal").ap()
    table = [None] + [nc.dram_tensor(f"table{t}", (N + SLOTS, HID), F32, kind="Internal").ap() for t in range(1, STEPS)]
    slot_x = nc.dram_tensor("slot_x", (SLOTS, HID), F32, kind="Internal").ap()
    slot_src = nc.dram_tensor("slot_src", (SLOTS, HID), F32, kind="Internal").ap()

    def slot_rows(ap, g):
        return ap.rearrange("(g p u) f -> g p (u f)", p=P, u=GT)[bass.ds(g, 1), :, :].rearrange("o p f -> (o p) f")

    slot_table = [slot_x] + [table[t][N:N + SLOTS, :] for t in range(1, STEPS)]

    def node_rows(ap, tile):
        full = ap[0:(NODE_TILES - 1) * NODE_TILE, :].rearrange("(t p u) f -> t p (u f)", p=P, u=NU)
        return full[bass.ds(tile, 1), :, :].rearrange("o p f -> (o p) f")

    with ExitStack() as ctx:
        def sb(name, shape, dt=F32):
            return ctx.enter_context(nc.sbuf_tensor(name, list(shape), dt))

        def ps(name, shape):
            return ctx.enter_context(nc.psum_tensor(name, list(shape), F32))

        def sem(name):
            return ctx.enter_context(nc.semaphore(name))

        ident = sb("ident", [P, P])
        shift_t = sb("shift_t", [P, P])
        wrap_t = sb("wrap_t", [P, P])
        is_last_p = sb("is_last_p", [P, 1])
        p_col = sb("p_col", [P, 8], I32)
        p_bit = sb("p_bit", [P, 8], I32)
        sign = sb("sign", [P, 8])
        slot_row_id = sb("slot_row_id", [P, TILES], I32)
        ones_bf = sb("ones_bf", [P, P], BF16)
        gate_w = sb("gate_w", [P, 4 * HID])
        gate_wh = sb("gate_wh", [HID, 3 * HID])
        w1_t = sb("w1_t", [ED, HID])
        w2_b = sb("w2_b", [HID + 1, HID])
        b1_col = sb("b1_col", [HID, 1])
        bi3 = sb("bi3", [3, 3 * HID])
        bh3 = sb("bh3", [3, 3 * HID])
        b3 = sb("b3", [3, 4 * HID])
        bias_rest = sb("bias_rest", [3, 4 * HID])
        bias_part = sb("bias_part", [3, 3, 4 * HID], BF16)
        bias_acc = sb("bias_acc", [3, 4 * HID])
        bias_rows = sb("bias_rows", [P, 8 * HID], BF16)

        target = sb("target", [P, TILES + 1])
        prev_last = sb("prev_last", [P, TILES])
        target_idx = sb("target_idx", [P, TILES], I32)
        edge_idx = sb("edge_idx", [P, TILES], I32)
        rep_idx = sb("rep_idx", [P, TILES], I32)
        src_node = sb("src_node", [P, TILES], I32)
        src_row = sb("src_row", [P, TILES], I32)

        msg_base = sb("msg_base", [P, TILES * HID])
        idx_g = {name: [sb(f"{name}_idx{b}", [P, GT], I32) for b in range(2)] for name in ("rows", "xj", "xi", "map", "node", "src", "y")}
        map_row_g = [sb(f"map_row_g{b}", [P, GT], I32) for b in range(2)]
        src_row_g = [sb(f"src_row_g{b}", [P, GT], I32) for b in range(2)]
        run_end = sb("run_end", [P, TILES])
        dst_stage = sb("dst_stage", [LOAD_P, E // LOAD_P], I32)[:, :]
        attr_stage = msg_base[0:LOAD_P, 0:E // LOAD_P * ED]
        scratch = [E // LOAD_P * ED]

        def square(cols=SORT_COLS, dt=F32):
            a = msg_base[:, scratch[0]:scratch[0] + cols]
            scratch[0] += cols
            assert scratch[0] <= TILES * HID
            return a.bitcast(dt) if dt != F32 else a

        key_i = square(dt=I32)
        local_e = square(dt=I32)
        block_e = square()
        kk = [square(), square()]
        pp = [square(), square()]
        swap = square(SORT_COLS // 2)
        delta = square(SORT_COLS // 2)
        node_id = square(MAP_COLS, I32)

        RZ = [sb(f"rz{b}", [P, NU, 2 * HID]) for b in range(2)]
        pre = [sb(f"pre{b}", [P, NU, HID]) for b in range(2)]
        cand = [sb(f"cand{b}", [P, NU, HID]) for b in range(2)]
        dif = [sb(f"dif{b}", [P, NU, HID]) for b in range(2)]
        xt = [sb(f"xt{b}", [P, 4 * P]) for b in range(2)]
        var = sb("var", [P, 16])
        vhalf = sb("vhalf", [P, 16])
        rstd = sb("rstd", [P, 16])
        nt1 = sb("nt1", [P, 16])
        nt2 = sb("nt2", [P, 16])

        ARENA = E // LOAD_P * ROW
        arena = sb("arena", [P, ARENA])
        at = [0]

        def carve(cols):
            a = arena[:, at[0]:at[0] + cols]
            at[0] += cols
            assert at[0] <= ARENA, at[0]
            return a

        def v3(a, u):
            return a.rearrange("p (u f) -> p u f", u=u)

        edge_stage = arena[0:LOAD_P, :].rearrange("p (r d) -> p r d", d=ROW)
        TW = NU * HID
        x_t = [[v3(carve(TW), NU) for j in range(JT)] for b in range(2)]
        h_t = [[v3(carve(TW), NU) for b in range(2)] for j in range(JT)]
        y_t = [v3(carve(TW), NU) for j in range(JT)]
        sq = v3(carve(TW), NU)
        rows_g = [v3(carve(GT * ROW), GT) for b in range(2)]
        xj_g = [v3(carve(GT * HID), GT) for b in range(2)]
        xi_g = [v3(carve(GT * HID), GT) for b in range(2)]
        attr_t = carve(4 * P)
        hidden = carve(4 * P)
        ln_sum = carve(8)
        at[0] = 0
        xc = [v3(carve(GT * 2 * HID), GT) for b in range(2)]
        g_c = [v3(carve(GT * HID), GT) for b in range(2)]
        msg = [v3(carve(GT * HID), GT) for b in range(2)]
        same = [v3(carve(4 * P), 4) for h in range(2)]
        same_prev = [v3(carve(4 * P), 4) for h in range(2)]
        h_c = [v3(carve(GT * HID), GT) for b in range(2)]
        xi_c = [v3(carve(GT * HID), GT) for b in range(2)]
        y_c = [v3(carve(GT * HID), GT) for b in range(2)]
        sq_c = v3(carve(TW), NU)
        tgt_g = [carve(GT) for b in range(2)]
        ln_sum_c = carve(8)

        gates = [ps(f"gates{b}", [P, NU, 4 * HID]) for b in range(2)]
        xt_ps = [ps(f"xt_ps{b}", [P, 4 * P]) for b in range(2)]
        bank_a = ps("bank_a", [P, 4 * P])
        bank_b = ps("bank_b", [P, 4 * P])

        S = {}
        for name in (
            "pad_set", "keys_loaded", "weights_loaded", "attr_loaded", "dst_loaded", "zero_set", "consts_set", "masks_set",
            "rows_made", "rows_stored", "map_stored", "sort_step", "flipped", "unflipped", "sorted_", "shifted", "columns_set",
            "setup_step", "bias_set",
            "x_loaded0", "x_loaded1", "xt_ready", "xt_copied", "gates_ready", "rz_ready", "r_hn_ready", "pre_tanh_ready",
            "n_ready", "diff_ready", "gated_ready", "h_ready", "resid_ready", "sum_ready", "center_ready", "square_ready",
            "var_ready", "newton_step", "y_ready",
            "rows_got0", "rows_got1", "xj_got0", "xj_got1", "xi_got0", "xi_got1", "map_put", "xj_stored0", "xj_stored1",
            "xi_stored0", "xi_stored1", "src_saved", "attr_turned", "attr_t_copied", "hidden_summed", "hidden_ready", "base_summed", "base_copied",
            "src_row_got", "rows_idx_set", "xj_idx_set", "xi_idx_set", "map_idx_set", "node_idx_set", "src_idx_set", "y_idx_set", "pool_passed", "map_rows_set", "src_rows_saved",
            "tgt_copied", "bcast_ready", "same_ready", "msg_ready", "agg_summed", "agg_copied", "g_got0", "g_got1",
            "g_loaded0", "g_loaded1", "xc_loaded0", "xc_loaded1", "xi_loaded0", "xi_loaded1", "hc_stored0", "hc_stored1",
            "c_xt_ready", "c_xt_copied", "c_gates_ready", "c_rz_ready", "c_r_hn_ready", "c_pre_tanh_ready",
            "c_n_ready", "c_diff_ready", "c_gated_ready", "c_h_ready", "c_resid_ready", "c_sum_ready", "c_center_ready",
            "c_square_ready", "c_var_ready", "c_newton_step", "c_y_ready", "y_put0", "y_put1",
        ):
            S[name] = sem(name)
        h_stored = [[sem(f"h_stored_{j}_{b}") for b in range(2)] for j in range(JT)]
        y_stored = [sem(f"y_stored_{j}") for j in range(JT)]

        turn_asked = sem("turn_asked")
        turned = sem("turned")

        block = ctx.enter_context(nc.Block())

        WEIGHT_DMAS = 14
        MLP_TICKS = {6: (0, 0), 7: (0, 1), 9: (0, 2), 10: (1, 0), 12: (1, 1), 14: (1, 2)}

        def run_iterations(eng, body, count):
            body(0, 0, 0)
            with eng.Fori(0, (count - 3) // 2) as m:
                body(m * 2 + 1, 1, m)
                body(m * 2 + 2, 0, m + 1)
            body(count - 2, 1, (count - 3) // 2)
            body(count - 1, 0, (count - 1) // 2)

        def run_groups(eng, body):
            for g in range(3):
                body(g, g % 2, g // 2)
            with eng.Fori(1, (GROUPS - 3) // 2) as m:
                body(m * 2 + 1, 1, m)
                body(m * 2 + 2, 0, m + 1)
            body(GROUPS - 2, 1, (GROUPS - 3) // 2)
            body(GROUPS - 1, 0, (GROUPS - 1) // 2)

        def is_first(i):
            return isinstance(i, int) and i == 0

        def is_end(i, count):
            return isinstance(i, int) and i == count - 1

        def phases():
            res = []
            for m in range(1, 17):
                high = [l for l in range(m - 1, -1, -1) if l >= 14 or 7 <= l]
                low = [l for l in range(m - 1, -1, -1) if l < 7]
                if high:
                    res.append(("N", m, high))
                res.append(("T", m, low))
            return res

        def turn_list():
            res, lay, k, p = [], "T", 0, 0
            for L, m, ls in phases():
                if L != lay:
                    res.append(kk[k])
                    k ^= 1
                    if m >= 15:
                        res.append(pp[p])
                        p ^= 1
                    lay = L
                k ^= len(ls) & 1
                if m >= 15:
                    p ^= len(ls) & 1
                if L == "T" and m == 14:
                    k ^= 1
            return res + [kk[k], pp[p]]

        TURNS = turn_list()

        @block.sync
        def _(sp):
            sp.wait_ge(S["pad_set"], 1)
            with nc.allow_non_contiguous_dma(reason="small loads"):
                sp.dma_start(key_i[0:LOAD_P, :].rearrange("p (q f) -> p q f", q=BLOCKS)[:, :, 0:LOAD_F],
                             src.rearrange("(q p f) -> p q f", q=BLOCKS, p=LOAD_P)).then_inc(S["keys_loaded"], 16)
                sp.dma_start(attr_stage, attr.rearrange("(p r) d -> p (r d)", p=LOAD_P)).then_inc(S["attr_loaded"], 16)
                sp.dma_start(dst_stage, dst.rearrange("(p r) -> p r", p=LOAD_P)).then_inc(S["dst_loaded"], 16)
                sp.wait_ge(S["zero_set"], 4)
                w = S["weights_loaded"]
                sp.dma_start(gate_w[0:HID, 0:2 * HID], wit[:, 0:2 * HID]).then_inc(w, 16)
                sp.dma_start(gate_w[0:HID, 3 * HID:4 * HID], wit[:, 2 * HID:3 * HID]).then_inc(w, 16)
                sp.dma_start(gate_w[HID:P, 0:3 * HID], wht).then_inc(w, 16)
                sp.dma_start(gate_wh[:, :], wht).then_inc(w, 16)
                sp.dma_start(w1_t[:, :], w1t).then_inc(w, 16)
                sp.dma_start(w2_b[0:HID, :], w2t).then_inc(w, 16)
                sp.dma_start(w2_b[HID:HID + 1, :], b2.rearrange("(o f) -> o f", o=1)).then_inc(w, 16)
                sp.dma_start(b1_col[:, :], b1.rearrange("(f o) -> f o", o=1)).then_inc(w, 16)
                for k in range(3):
                    sp.dma_start(bi3[k:k + 1, :], bih.rearrange("(o f) -> o f", o=1)).then_inc(w, 16)
                    sp.dma_start(bh3[k:k + 1, :], bhh.rearrange("(o f) -> o f", o=1)).then_inc(w, 16)
            sp.wait_ge(S["consts_set"], 1)
            sp.dma_start(row_map.rearrange("(p c) o -> p (c o)", p=P), node_id[:, :]).then_inc(S["map_stored"], 16)
            sp.wait_ge(S["rows_made"], 2)
            sp.dma_start(edge_rows.rearrange("(p r) d -> p (r d)", p=LOAD_P),
                         edge_stage[:, :, :].rearrange("p r d -> p (r d)")).then_inc(S["rows_stored"], 16)

            def load_x(i, par):
                for j in range(JT):
                    if is_end(i, ITERS) and j == JT - 1:
                        rows = x[LAST_BASE:N, :].rearrange("(p u) f -> p (u f)", p=P)
                    else:
                        rows = node_rows(x, i * JT + j)
                    sp.dma_start(x_t[par][j].rearrange("p u f -> p (u f)"), rows).then_inc(S[f"x_loaded{par}"], 16)

            def store_tile(dram, i, j, tile):
                if is_end(i, ITERS) and j == JT - 1:
                    return (dram[LAST_BASE + NU * LAST_NEW_P:N, :].rearrange("(p u) f -> p (u f)", u=NU),
                            tile[LAST_NEW_P:P].rearrange("p u f -> p (u f)"))
                return node_rows(dram, i * JT + j), tile.rearrange("p u f -> p (u f)")

            def store_y(i, j):
                sp.wait_ge(S["y_ready"], i * JT + j + 1)
                d, s = store_tile(out, i, j, y_t[j])
                sp.dma_start(d, s).then_inc(y_stored[j], 16)

            def store_gathers(i, par, uses):
                sp.wait_ge(S[f"xj_got{par}"], (uses + 1) * (16 * GT))
                sp.dma_start(slot_rows(slot_src, i), xj_g[par].rearrange("p u f -> p (u f)")).then_inc(S[f"xj_stored{par}"], 16)
                sp.wait_ge(S[f"xi_got{par}"], (uses + 1) * (16 * GT))
                sp.dma_start(slot_rows(slot_x, i), xi_g[par].rearrange("p u f -> p (u f)")).then_inc(S[f"xi_stored{par}"], 16)

            def dense(i, par, uses):
                for k in range(3 * JT):
                    j, t = k % JT, k // JT
                    if k == 1 and not is_end(i, ITERS):
                        if not is_first(i):
                            sp.wait_ge(S["resid_ready"], i * JT)
                        load_x(i + 1, 1 - par)
                    if 1 <= k <= JT and not is_first(i):
                        store_y(i - 1, k - 1)
                    if k == 6 and not is_first(i):
                        store_gathers(i - 1, 1 - par, uses - par_uses(par))
                    sp.wait_ge(S["h_ready"], i * UNITS + k + 1)
                    d, s = store_tile(table[t + 1], i, j, h_t[j][t % 2])
                    sp.dma_start(d, s).then_inc(h_stored[j][t % 2], 16)

            def par_uses(par):
                return 0 if par == 1 else 1

            sp.wait_ge(S["rows_stored"], 16)
            load_x(0, 0)
            run_iterations(sp, dense, ITERS)
            for j in range(JT):
                store_y(ITERS - 1, j)
            store_gathers(ITERS - 1, 0, (ITERS - 1) // 2)

            def slot_loads(t):
                def f(g, par, uses):
                    gg = g + t * GROUPS
                    n = uses + t * (25 if par == 0 else 24)
                    early = isinstance(g, int) and g < 2
                    if t == 0:
                        if not early:
                            sp.wait_ge(S["msg_ready"], gg - 1)
                        sp.dma_start(g_c[par].rearrange("p u f -> p (u f)"), slot_rows(slot_src, g)).then_inc(S[f"g_loaded{par}"], 16)
                    if t == STEPS - 1 and not early:
                        sp.wait_ge(S["c_resid_ready"], (g - 1) * 2)
                    elif not (early and t == 0):
                        sp.wait_ge(S["c_diff_ready"], t * GROUPS * 2 if early else (gg - 1) * 2)
                    sp.dma_start(xc[par][:, :, HID:2 * HID],
                                 slot_rows(slot_table[t], g).rearrange("p (u f) -> p u f", u=GT)).then_inc(S[f"xc_loaded{par}"], 16)
                    if t == STEPS - 1:
                        sp.dma_start(xi_c[par].rearrange("p u f -> p (u f)"), slot_rows(slot_x, g)).then_inc(S[f"xi_loaded{par}"], 16)
                return f

            def slot_store(t, g, par):
                sp.wait_ge(S["c_h_ready"], (g + t * GROUPS) * 2 + 2)
                sp.dma_start(slot_rows(slot_table[t + 1], g), h_c[par].rearrange("p u f -> p (u f)")).then_inc(S[f"hc_stored{par}"], 16)

            for j in range(JT):
                sp.wait_ge(h_stored[j][0], 16 * 2 * ITERS)
                sp.wait_ge(h_stored[j][1], 16 * ITERS)
                sp.wait_ge(y_stored[j], 16 * ITERS)
            sp.wait_ge(S["xj_stored0"], 16 * 25)
            sp.wait_ge(S["xj_stored1"], 16 * 24)
            sp.wait_ge(S["xi_stored0"], 16 * 25)
            sp.wait_ge(S["xi_stored1"], 16 * 24)
            sp.wait_ge(S["base_copied"], 2 * GROUPS)
            sp.wait_ge(S["src_saved"], GROUPS)
            for t in range(STEPS):
                ld = slot_loads(t)

                def both(g, par, uses, ld=ld, t=t):
                    if not is_end(g, GROUPS):
                        ld(g + 1, 1 - par, uses if par == 0 else uses + 1)
                    if not is_first(g) and t < STEPS - 1:
                        slot_store(t, g - 1, 1 - par)

                ld(0, 0, 0)
                run_groups(sp, both)
                if t < STEPS - 1:
                    slot_store(t, GROUPS - 1, 0)
                    sp.wait_ge(S["hc_stored0"], 16 * 25 * (t + 1))
                    sp.wait_ge(S["hc_stored1"], 16 * 24 * (t + 1))

        @block.gpsimd
        def _(pool):
            pool.memset(key_i[:, :], PAD_KEY).then_inc(S["pad_set"], 1)
            pool.memset(gate_w[:, :], 0.0).then_inc(S["zero_set"], 1)
            pool.memset(bias_rows[:, :], 0.0).then_inc(S["zero_set"], 1)
            pool.memset(ones_bf[:, :], 1.0).then_inc(S["zero_set"], 1)
            pool.memset(w2_b[:, :], 0.0).then_inc(S["zero_set"], 1)
            for n, (tile, base, cm) in enumerate(((ident, 0, 1), (shift_t, -1, 1), (wrap_t, P - 1, P))):
                pool.memset(tile[:, :], 0.0).then_inc(S["masks_set"], 1)
                pool.wait_ge(S["masks_set"], 2 * n + 1)
                pool.affine_select(out=tile[:, :], in_=tile[:, :], pattern=[[-1, P]], compare_op=ALU.not_equal,
                                   fill=1.0, base=base, channel_multiplier=cm).then_inc(S["masks_set"], 1)
            pool.memset(is_last_p[:, :], 0.0).then_inc(S["masks_set"], 1)
            pool.wait_ge(S["masks_set"], 7)
            pool.affine_select(out=is_last_p[:, :], in_=is_last_p[:, :], pattern=[[0, 1]], compare_op=ALU.not_equal,
                               fill=1.0, base=-(P - 1), channel_multiplier=1).then_inc(S["masks_set"], 1)
            pool.iota(local_e[:, :], [[0, BLOCKS], [1, P]], base=0, channel_multiplier=LOAD_F).then_inc(S["masks_set"], 1)
            pool.iota(p_col[:, :], [[0, 8]], base=0, channel_multiplier=1).then_inc(S["masks_set"], 1)
            pool.iota(block_e[:, :], [[BLOCK_E, BLOCKS], [0, P]], base=0, channel_multiplier=0,
                      allow_small_or_imprecise_dtypes=True).then_inc(S["masks_set"], 1)
            pool.iota(node_id[:, :], [[1, MAP_COLS]], base=0, channel_multiplier=MAP_COLS).then_inc(S["consts_set"], 1)
            pool.iota(slot_row_id[:, :], [[GT * P, GROUPS], [1, GT]], base=N, channel_multiplier=GT).then_inc(S["consts_set"], 1)
            pool.wait_ge(S["dst_loaded"], 16)
            pool.tensor_copy(edge_stage[:, :, ED:ROW].bitcast(I32).rearrange("p r o -> p (r o)"), dst_stage).then_inc(S["rows_made"], 1)

            def gather(o, table_ap, idx, bound, s):
                pool.indirect_dma_start(out=o, out_offset=None, in_=table_ap,
                                        in_offset=bass.IndirectOffsetOnAxis(ap=idx, axis=0),
                                        bounds_check=bound).then_inc(s, 16)

            def column(tile, g, u):
                return tile[:, bass.ds(g * GT + u, 1)]

            def take_indices(name, tile, g, par, count):
                pool.tensor_copy(idx_g[name][par][:, :], tile[:, bass.ds(g * GT, GT)]).then_inc(S[name + "_idx_set"], 1)
                pool.wait_ge(S[name + "_idx_set"], count + 1)
                pool.sem_inc(S["pool_passed"], 1)
                return lambda u: idx_g[name][par][:, u:u + 1]

            def get_rows(i, par):
                idx = take_indices("rows", edge_idx, i, par, i)
                for u in range(GT):
                    gather(rows_g[par][:, u, :], edge_rows, idx(u), E - 1, S[f"rows_got{par}"])

            def setup(i, par, uses):
                if not is_end(i, ITERS):
                    if not is_first(i):
                        pool.wait_ge(S["attr_turned"], i * 2)
                        pool.sem_inc(S["pool_passed"], 1)
                        pool.wait_ge(S["src_saved"], i)
                        pool.sem_inc(S["pool_passed"], 1)
                    get_rows(i + 1, 1 - par)
                pool.wait_ge(S[f"rows_got{par}"], (uses + 1) * (16 * GT))
                pool.sem_inc(S["pool_passed"], 1)
                if not (isinstance(i, int) and i < 2):
                    pool.wait_ge(S[f"xj_stored{par}"], uses * 16)
                    pool.sem_inc(S["pool_passed"], 1)
                    pool.wait_ge(S[f"xi_stored{par}"], uses * 16)
                    pool.sem_inc(S["pool_passed"], 1)
                pool.tensor_copy(idx_g["xj"][par][:, :], rows_g[par][:, :, ED:ROW].bitcast(I32).rearrange("p u o -> p (u o)")).then_inc(S["xj_idx_set"], 1)
                pool.wait_ge(S["xj_idx_set"], i + 1)
                pool.sem_inc(S["pool_passed"], 1)
                for u in range(GT):
                    gather(xj_g[par][:, u, :], x, idx_g["xj"][par][:, u:u + 1], N - 1, S[f"xj_got{par}"])
                idx = take_indices("xi", target_idx, i, par, i)
                for u in range(GT):
                    gather(xi_g[par][:, u, :], x, idx(u), N - 1, S[f"xi_got{par}"])
                if not (isinstance(i, int) and i < 2):
                    pool.wait_ge(S["map_put"], (i - 1) * (16 * GT))
                    pool.sem_inc(S["pool_passed"], 1)
                idx = take_indices("map", rep_idx, i, par, i)
                pool.tensor_copy(map_row_g[par][:, :], slot_row_id[:, bass.ds(i * GT, GT)]).then_inc(S["map_rows_set"], 1)
                pool.wait_ge(S["map_rows_set"], i + 1)
                pool.sem_inc(S["pool_passed"], 1)
                for u in range(GT):
                    pool.indirect_dma_start(out=row_map, out_offset=bass.IndirectOffsetOnAxis(ap=idx(u), axis=0),
                                            in_=map_row_g[par][:, u:u + 1], in_offset=None,
                                            bounds_check=N - 1, oob_is_err=False).then_inc(S["map_put"], 16)

            pool.wait_ge(S["rows_stored"], 16)
            pool.wait_ge(S["map_stored"], 16)
            pool.wait_ge(S["columns_set"], 4)
            get_rows(0, 0)
            run_groups(pool, setup)

            pool.wait_ge(S["map_put"], 16 * TILES)
            pool.wait_ge(S["src_saved"], GROUPS)

            def get_src_rows(g, par, uses):
                if not (isinstance(g, int) and g < 2):
                    save_src_rows(g - 2, par)
                idx = take_indices("node", src_node, g, par, g)
                for u in range(GT):
                    gather(src_row_g[par][:, u:u + 1], row_map, idx(u), N - 1, S["src_row_got"])

            def save_src_rows(g, par):
                pool.wait_ge(S["src_row_got"], (g + 2) * (16 * GT))
                pool.sem_inc(S["pool_passed"], 1)
                pool.tensor_copy(src_row[:, bass.ds(g * GT, GT)], src_row_g[par][:, :]).then_inc(S["src_rows_saved"], 1)
                pool.wait_ge(S["src_rows_saved"], g + 1)
                pool.sem_inc(S["pool_passed"], 1)

            run_groups(pool, get_src_rows)
            pool.wait_ge(S["src_row_got"], 16 * TILES)
            for g in (GROUPS - 2, GROUPS - 1):
                pool.tensor_copy(src_row[:, g * GT:(g + 1) * GT], src_row_g[g % 2][:, :]).then_inc(S["src_rows_saved"], 1)
            pool.wait_ge(S["src_rows_saved"], GROUPS)

            def put_y(g, par, uses):
                pool.wait_ge(S["c_y_ready"], g * 2 + 2)
                pool.sem_inc(S["pool_passed"], 1)
                if not (isinstance(g, int) and g < 2):
                    pool.wait_ge(S[f"y_put{par}"], uses * (16 * GT))
                    pool.sem_inc(S["pool_passed"], 1)
                idx = take_indices("y", rep_idx, g, par, g)
                for u in range(GT):
                    pool.indirect_dma_start(out=out, out_offset=bass.IndirectOffsetOnAxis(ap=idx(u), axis=0),
                                            in_=y_c[par][:, u, :], in_offset=None,
                                            bounds_check=N - 1, oob_is_err=False).then_inc(S[f"y_put{par}"], 16)

            for j in range(JT):
                pool.wait_ge(h_stored[j][0], 16 * 2 * ITERS)
                pool.wait_ge(h_stored[j][1], 16 * ITERS)
                pool.wait_ge(y_stored[j], 16 * ITERS)
            for t in range(1, STEPS):
                def get(g, par, uses, t=t):
                    gg = g + t * GROUPS
                    if is_first(g):
                        pool.wait_ge(S["hc_stored0"], 16 * 25 * t)
                        pool.wait_ge(S["hc_stored1"], 16 * 24 * t)
                    early = isinstance(g, int) and g < 2
                    pool.wait_ge(S["msg_ready"], t * GROUPS if early else gg - 1)
                    pool.sem_inc(S["pool_passed"], 1)
                    idx = take_indices("src", src_row, g, par, gg - GROUPS)
                    for u in range(GT):
                        gather(g_c[par][:, u, :], table[t], idx(u), N + SLOTS - 1, S[f"g_got{par}"])
                    if t == STEPS - 1 and not early:
                        put_y(g - 2, par, uses - 1)

                run_groups(pool, get)
            put_y(GROUPS - 2, 1, 23)
            put_y(GROUPS - 1, 0, 24)
            pool.wait_ge(S["y_put0"], 16 * GT * 25)
            pool.wait_ge(S["y_put1"], 16 * GT * 24)

        def gate_matmuls_bias(k2):
            for b in range(2):
                nc.tensor.matmul(gates[k2][:, 2 * b:2 * b + 2, :].rearrange("p u f -> p (u f)"), ones_bf[:, :], bias_rows[:, :],
                                 start=True, stop=False, skip_group_check=True)

        def sigmoid_unit(act, c, k, k2):
            act.wait_ge(S[c + "gates_ready"], k + 1)
            if not (isinstance(k, int) and k < 2):
                act.wait_ge(S[c + "gated_ready"], k - 1)
            nc.scalar.activation(RZ[k2][:, :, :], gates[k2][:, :, 0:2 * HID], ACT.Sigmoid).then_inc(S[c + "rz_ready"], 1)

        def tanh_unit(act, c, k, k2):
            act.wait_ge(S[c + "pre_tanh_ready"], k + 1)
            if not (isinstance(k, int) and k < 2):
                act.wait_ge(S[c + "h_ready"], k - 1)
            nc.scalar.activation(cand[k2][:, :, :], pre[k2][:, :, :], ACT.Tanh).then_inc(S[c + "n_ready"], 1)

        def vec_r_hn(dve, c, k, k2):
            dve.wait_ge(S[c + "rz_ready"], k + 1)
            if not (isinstance(k, int) and k < 2):
                dve.wait_ge(S[c + "n_ready"], k - 1)
            nc.vector.tensor_tensor(pre[k2][:, :, :], gates[k2][:, :, 2 * HID:3 * HID], RZ[k2][:, :, 0:HID],
                                    ALU.mult).then_inc(S[c + "r_hn_ready"], 1)

        def vec_pre(dve, c, k, k2):
            dve.wait_ge(S[c + "r_hn_ready"], k + 1)
            nc.vector.tensor_tensor(pre[k2][:, :, :], pre[k2][:, :, :], gates[k2][:, :, 3 * HID:4 * HID],
                                    ALU.add).then_inc(S[c + "pre_tanh_ready"], 1)

        def unit_view(tile, c):
            return tile.rearrange("p (b s) f -> p b s f", b=2) if c == "" else tile

        def state_view(tile, c):
            return tile.rearrange("p (s b) f -> p b s f", b=2) if c == "" else tile

        def vec_diff(dve, c, k, k2, h):
            dve.wait_ge(S[c + "n_ready"], k + 1)
            nc.vector.tensor_tensor(unit_view(dif[k2][:, :, :], c), state_view(h, c), unit_view(cand[k2][:, :, :], c),
                                    ALU.subtract).then_inc(S[c + "diff_ready"], 1)

        def vec_gate(dve, c, k, k2):
            dve.wait_ge(S[c + "diff_ready"], k + 1)
            nc.vector.tensor_tensor(dif[k2][:, :, :], dif[k2][:, :, :], RZ[k2][:, :, HID:2 * HID],
                                    ALU.mult).then_inc(S[c + "gated_ready"], 1)

        def vec_h(dve, c, k, k2, h_new):
            dve.wait_ge(S[c + "gated_ready"], k + 1)
            nc.vector.tensor_tensor(state_view(h_new, c), unit_view(dif[k2][:, :, :], c), unit_view(cand[k2][:, :, :], c),
                                    ALU.add).then_inc(S[c + "h_ready"], 1)

        def norm_stats(dve, c, n, h_k, xx, hh, y, sqt, sums, v4):
            dve.wait_ge(S[c + "h_ready"], h_k + 1)
            nc.vector.tensor_tensor(y, xx, hh, ALU.add).then_inc(S[c + "resid_ready"], 1)
            dve.wait_ge(S[c + "resid_ready"], n + 1)
            nc.vector.tensor_reduce(sums, y, AX_X, ALU.add).then_inc(S[c + "sum_ready"], 1)
            dve.wait_ge(S[c + "sum_ready"], n + 1)
            nc.vector.scalar_tensor_tensor(out=y, in0=sums.unsqueeze(2).to_broadcast([P, NU, HID]), scalar=-1.0 / HID, in1=y,
                                           op0=ALU.mult, op1=ALU.add).then_inc(S[c + "center_ready"], 1)
            dve.wait_ge(S[c + "center_ready"], n + 1)
            nc.vector.tensor_tensor(sqt, y, y, ALU.mult).then_inc(S[c + "square_ready"], 1)
            dve.wait_ge(S[c + "square_ready"], n + 1)
            nc.vector.tensor_reduce(v4, sqt, AX_X, ALU.add).then_inc(S[c + "var_ready"], 1)

        def newton(dve, c, done, stats, w):
            s = S[c + "newton_step"]
            cnt = [0]

            def step(ins):
                ins.then_inc(s, 1)
                cnt[0] += 1
                dve.wait_ge(s, done + cnt[0])

            dve.wait_ge(S[c + "var_ready"], stats)
            v, hf, r, a, b = (q[:, 0:w] for q in (var, vhalf, rstd, nt1, nt2))
            step(nc.vector.tensor_scalar(v, v, 1.0 / HID, EPS, ALU.mult, ALU.add))
            step(nc.vector.tensor_scalar(hf, v, 0.5, None, ALU.mult))
            step(nc.vector.tensor_scalar(a.bitcast(I32), v.bitcast(I32), 1, None, ALU.logical_shift_right))
            step(nc.vector.tensor_scalar(r.bitcast(I32), a.bitcast(I32), -1.0, float(0x5F3759DF), ALU.mult, ALU.add))
            for _ in range(NEWTON):
                step(nc.vector.tensor_tensor(a, r, r, ALU.mult))
                step(nc.vector.tensor_tensor(b, a, hf, ALU.mult))
                step(nc.vector.scalar_tensor_tensor(out=r, in0=b, scalar=1.5, in1=r, op0=ALU.subtract, op1=ALU.mult))
            assert cnt[0] == NEWTON_OPS

        @block.tensor
        def _(pe):
            pe.wait_ge(S["masks_set"], 2)
            for n, square_in in enumerate(TURNS):
                pe.wait_ge(turn_asked, n + 1)
                for q in range(BLOCKS):
                    mm = nc.tensor.transpose(xt_ps[0][:, q * P:(q + 1) * P], square_in[:, q * P:(q + 1) * P], ident[:, :])
                mm.then_inc(turned, 1)
            pe.wait_ge(S["sorted_"], 1)
            pe.wait_ge(S["masks_set"], 6)
            nc.tensor.matmul(bank_a[:, 0:TILES], shift_t[:, :], target[:, 0:TILES], start=True, stop=False)
            nc.tensor.matmul(bank_a[:, 0:TILES], wrap_t[:, :], target[:, 1:TILES + 1], start=False, stop=True).then_inc(S["shifted"], 1)

            pe.wait_ge(S["weights_loaded"], 16 * WEIGHT_DMAS)
            pe.wait_ge(S["zero_set"], 4)
            pe.wait_ge(S["bias_set"], 1)

            def turn_states(i, k, par, uses):
                j, t = k % JT, k // JT
                kk_ = i * UNITS + k
                if t == 0:
                    if k == 0:
                        pe.wait_ge(S[f"x_loaded{par}"], (uses + 1) * (16 * JT))
                    hsrc = x_t[par][j]
                else:
                    pe.wait_ge(S["h_ready"], kk_ - JT + 1)
                    hsrc = h_t[j][(t - 1) % 2]
                if not (is_first(i) and k < 2):
                    pe.wait_ge(S["xt_copied"], kk_ - 1)
                for a in range(2):
                    mm = nc.tensor.transpose(xt_ps[k % 2][:, a * P:(a + 1) * P],
                                             hsrc[:, 2 * a:2 * a + 2, :].rearrange("p u f -> p (u f)"), ident[:, :])
                mm.then_inc(S["xt_ready"], 1)

            def gate_unit(i, k):
                kk_ = i * UNITS + k
                k2 = k % 2
                if not (is_first(i) and k < 2):
                    pe.wait_ge(S["pre_tanh_ready"], kk_ - 1)
                gate_matmuls_bias(k2)
                pe.wait_ge(S["xt_copied"], kk_ + 1)
                for a in range(2):
                    nc.tensor.matmul(gates[k2][:, a, 0:3 * HID], xt[k2][0:HID, a * P:(a + 1) * P], gate_wh[:, :],
                                     start=False, stop=False, skip_group_check=True)
                    mm = nc.tensor.matmul(gates[k2][:, 2 + a, 0:3 * HID], xt[k2][HID:P, a * P:(a + 1) * P], gate_w[HID:P, 0:3 * HID],
                                          start=False, stop=(a == 1), skip_group_check=True)
                mm.then_inc(S["gates_ready"], 1)

            def mlp(i, par, uses, half, stage):
                n = i * 2 + half
                if stage == 0:
                    if half == 0:
                        pe.wait_ge(S[f"rows_got{par}"], (uses + 1) * (16 * GT))
                    if not (is_first(i) and half == 0):
                        pe.wait_ge(S["base_copied"], n)
                    for u in range(4):
                        mm = nc.tensor.transpose(bank_a[0:ED, u * P:(u + 1) * P], rows_g[par][:, 4 * half + u, 0:ED], ident[:, :])
                    mm.then_inc(S["attr_turned"], 1)
                elif stage == 1:
                    pe.wait_ge(S["attr_t_copied"], n + 1)
                    nc.tensor.matmul(bank_b[0:HID, :], w1_t[:, :], attr_t[0:ED, :], start=True, stop=True).then_inc(S["hidden_summed"], 1)
                else:
                    pe.wait_ge(S["hidden_ready"], n + 1)
                    for u in range(4):
                        mm = nc.tensor.matmul(bank_a[:, u * HID:(u + 1) * HID], hidden[0:HID + 1, u * P:(u + 1) * P], w2_b[:, :],
                                              start=True, stop=True)
                    mm.then_inc(S["base_summed"], 1)

            def dense(i, par, uses):
                for k in range(UNITS):
                    gate_unit(i, k)
                    if k + 2 < UNITS:
                        turn_states(i, k + 2, par, uses)
                    elif not is_end(i, ITERS):
                        turn_states(i + 1, k + 2 - UNITS, 1 - par, uses if par == 0 else uses + 1)
                    if k in MLP_TICKS:
                        half, stage = MLP_TICKS[k]
                        mlp(i, par, uses, half, stage)

            turn_states(0, 0, 0, 0)
            turn_states(0, 1, 0, 0)
            run_iterations(pe, dense, ITERS)

            pe.wait_ge(S["base_copied"], 2 * GROUPS)
            pe.wait_ge(S["pre_tanh_ready"], ITERS * UNITS)

            for t in range(STEPS):
                def bcast(g, par, half, t=t):
                    gg = g + t * GROUPS
                    if half == 0:
                        pe.wait_ge(S["tgt_copied"], gg + 1)
                    if not (t == 0 and is_first(g) and half == 0):
                        pe.wait_ge(S["same_ready"], gg * 2 + half)
                    for u in range(4):
                        col = tgt_g[par][:, 4 * half + u:4 * half + u + 1].to_broadcast([P, P])
                        mm = nc.tensor.matmul(bank_b[:, u * P:(u + 1) * P], col, ident[:, :], start=True, stop=True)
                    mm.then_inc(S["bcast_ready"], 1)

                def turn_slots(g, par, uses, b, t=t):
                    gg = g + t * GROUPS
                    n = gg * 2 + b
                    if b == 0:
                        pe.wait_ge(S[f"xc_loaded{par}"], (uses + t * (25 if par == 0 else 24) + 1) * 16)
                    pe.wait_ge(S["agg_copied"], gg * GT + 4 * b + 4)
                    if not (t == 0 and is_first(g)):
                        pe.wait_ge(S["c_xt_copied"], n - 1)
                    for u in range(4):
                        mm = nc.tensor.transpose(xt_ps[b][:, u * P:(u + 1) * P], xc[par][:, 4 * b + u, :], ident[:, :])
                    mm.then_inc(S["c_xt_ready"], 1)

                def gate_bias(g, b, t=t):
                    n = (g + t * GROUPS) * 2 + b
                    if not (t == 0 and is_first(g)):
                        pe.wait_ge(S["c_pre_tanh_ready"], n - 1)
                    gate_matmuls_bias(b)
                    pe.wait_ge(S["c_xt_copied"], n + 1)

                def gate_part(b, u):
                    mm = nc.tensor.matmul(gates[b][:, u, :], xt[b][:, u * P:(u + 1) * P], gate_w[:, :],
                                          start=False, stop=(u == 3), skip_group_check=True)
                    if u == 3:
                        mm.then_inc(S["c_gates_ready"], 1)

                def slots(g, par, uses, t=t):
                    gg = g + t * GROUPS
                    prev = not is_first(g)
                    if prev:
                        pu = uses if par == 1 else uses - 1
                        turn_slots(g - 1, 1 - par, pu, 0)
                        turn_slots(g - 1, 1 - par, pu, 1)
                    for u in range(GT):
                        if u % 4 == 0:
                            pe.wait_ge(S["same_ready"], gg * 2 + u // 4 + 1)
                            if prev:
                                gate_bias(g - 1, u // 4)
                        if u == 0:
                            pe.wait_ge(S["msg_ready"], gg + 1)
                        first = not prev and u == 0
                        if not (first and t == 0):
                            pe.wait_ge(S["agg_copied"], gg * GT + u)
                        mm = nc.tensor.matmul(bank_a[:, u * HID:(u + 1) * HID], same[u // 4][:, u % 4, :], msg[par][:, u, :],
                                              start=True, stop=first)
                        if not first:
                            carry = xc[par][:, u - 1, 0:HID] if u else xc[1 - par][:, GT - 1, 0:HID]
                            mm = nc.tensor.matmul(bank_a[:, u * HID:(u + 1) * HID], same_prev[u // 4][:, u % 4, :], carry,
                                                  start=False, stop=True)
                        mm.then_inc(S["agg_summed"], 1)
                        if prev:
                            gate_part(u // 4, u % 4)
                        if u == 1:
                            bcast(g, par, 1)
                        if u == 5 and not is_end(g, GROUPS):
                            bcast(g + 1, 1 - par, 0)

                bcast(0, 0, 0)
                run_groups(pe, slots)
                for b in range(2):
                    turn_slots(GROUPS - 1, 0, 24, b)
                for b in range(2):
                    gate_bias(GROUPS - 1, b)
                    for u in range(4):
                        gate_part(b, u)

        @block.scalar
        def _(act):
            act.wait_ge(S["attr_loaded"], 16)
            nc.scalar.copy(edge_stage[:, :, 0:ED], attr_stage.rearrange("p (r d) -> p r d", d=ED)).then_inc(S["rows_made"], 1)
            act.wait_ge(S["weights_loaded"], 16 * WEIGHT_DMAS)
            act.wait_ge(S["columns_set"], 4)

            def copy_xt(i, k):
                kk_ = i * UNITS + k
                act.wait_ge(S["xt_ready"], kk_ + 1)
                if not (is_first(i) and k < 2):
                    act.wait_ge(S["gates_ready"], kk_ - 1)
                nc.scalar.copy(xt[k % 2][:, 0:2 * P], xt_ps[k % 2][:, 0:2 * P]).then_inc(S["xt_copied"], 1)

            def mlp(i, half, stage):
                n = i * 2 + half
                if stage == 0:
                    act.wait_ge(S["attr_turned"], n + 1)
                    if not (is_first(i) and half == 0):
                        act.wait_ge(S["hidden_summed"], n)
                    nc.scalar.copy(attr_t[0:ED, :], bank_a[0:ED, :]).then_inc(S["attr_t_copied"], 1)
                elif stage == 1:
                    act.wait_ge(S["hidden_summed"], n + 1)
                    if not (is_first(i) and half == 0):
                        act.wait_ge(S["base_summed"], n)
                    nc.scalar.activation(hidden[0:HID, :], bank_b[0:HID, :], ACT.Relu, bias=b1_col[:, :]).then_inc(S["hidden_ready"], 1)
                else:
                    act.wait_ge(S["base_summed"], n + 1)
                    nc.scalar.copy(msg_base[:, bass.ds(i * (GT * HID) + half * 4 * HID, 4 * HID)],
                                   bank_a[:, 0:4 * HID]).then_inc(S["base_copied"], 1)

            def dense(i, par, uses):
                for k in range(UNITS):
                    kk_ = i * UNITS + k
                    sigmoid_unit(act, "", kk_, k % 2)
                    if not (is_first(i) and k == 0):
                        tanh_unit(act, "", kk_ - 1, (k - 1) % 2)
                    if k + 2 < UNITS:
                        copy_xt(i, k + 2)
                    elif not is_end(i, ITERS):
                        copy_xt(i + 1, k + 2 - UNITS)
                    if k in MLP_TICKS:
                        half, stage = MLP_TICKS[k]
                        mlp(i, half, stage)

            act.wait_ge(S["rows_stored"], 16)
            copy_xt(0, 0)
            copy_xt(0, 1)
            run_iterations(act, dense, ITERS)
            tanh_unit(act, "", ITERS * UNITS - 1, 1)
            for q in ("xj_stored", "xi_stored"):
                act.wait_ge(S[q + "0"], 16 * 25)
                act.wait_ge(S[q + "1"], 16 * 24)
            act.wait_ge(S["src_saved"], GROUPS)
            for j in range(JT):
                act.wait_ge(h_stored[j][0], 16 * 2 * ITERS)
                act.wait_ge(h_stored[j][1], 16 * ITERS)
                act.wait_ge(y_stored[j], 16 * ITERS)
            act.wait_ge(S["base_summed"], 2 * GROUPS)

            for t in range(STEPS):
                def copy_agg(g, par, u, t=t):
                    gg = g + t * GROUPS
                    act.wait_ge(S["agg_summed"], gg * GT + u + 1)
                    if u == 0 and not (t == 0 and isinstance(g, int) and g < 2):
                        act.wait_ge(S["c_xt_ready"], gg * 2 - 2)
                    nc.scalar.copy(xc[par][:, u, 0:HID], bank_a[:, u * HID:(u + 1) * HID]).then_inc(S["agg_copied"], 1)

                def copy_xt_c(g, b, t=t):
                    n = (g + t * GROUPS) * 2 + b
                    act.wait_ge(S["c_xt_ready"], n + 1)
                    if not (t == 0 and is_first(g)):
                        act.wait_ge(S["c_gates_ready"], n - 1)
                    nc.scalar.copy(xt[b][:, :], xt_ps[b][:, :]).then_inc(S["c_xt_copied"], 1)

                def slots(g, par, uses, t=t):
                    prev = not is_first(g)
                    if prev:
                        k = (g + (t * GROUPS - 1)) * 2
                        copy_xt_c(g - 1, 0)
                        copy_xt_c(g - 1, 1)
                    for u in range(GT):
                        copy_agg(g, par, u)
                        if prev and u == 4:
                            sigmoid_unit(act, "c_", k, 0)
                        if prev and u == 6:
                            tanh_unit(act, "c_", k, 0)
                    if prev:
                        sigmoid_unit(act, "c_", k + 1, 1)
                        tanh_unit(act, "c_", k + 1, 1)

                run_groups(act, slots)
                k = (t * GROUPS + GROUPS - 1) * 2
                for b in range(2):
                    copy_xt_c(GROUPS - 1, b)
                for b in range(2):
                    sigmoid_unit(act, "c_", k + b, b)
                    tanh_unit(act, "c_", k + b, b)

        @block.vector
        def _(dve):
            sstep = [0]

            def step(ins):
                ins.then_inc(S["sort_step"], 1)
                sstep[0] += 1
                dve.wait_ge(S["sort_step"], sstep[0])

            TT = nc.vector.tensor_tensor
            TS = nc.vector.tensor_scalar
            dve.wait_ge(S["keys_loaded"], 16)
            dve.wait_ge(S["masks_set"], 11)
            cur, oth = kk[0], kk[1]
            step(TS(key_i[:, :], key_i[:, :], float(KEY_SHIFT), None, ALU.add))
            step(TS(key_i[:, :], key_i[:, :], LOCAL_BITS, None, ALU.logical_shift_left))
            step(TT(cur[:, :].bitcast(I32), key_i[:, :], local_e[:, :], ALU.bitwise_or))
            for b in range(7):
                step(TS(p_bit[:, b:b + 1], p_col[:, b:b + 1], b, 1, ALU.logical_shift_right, ALU.bitwise_and))
            step(TS(sign[:, 0:7], p_bit[:, 0:7], -2.0, 1.0, ALU.mult, ALU.add))

            def free_bit(lay, b):
                if lay == "N":
                    return b - 7
                return b if b < 7 else (b - 7 if b >= 14 else None)

            def halves(tile, lay, m, l):
                fl = free_bit(lay, l)
                fm = free_bit(lay, m) if m < 16 else None
                w = tile.shape[1]
                if fm is None:
                    v = tile[:, :].rearrange("p (h t l) -> p t h l", t=2, l=1 << fl)
                    return [(v[:, 0], v[:, 1], False)]
                v = tile[:, :].rearrange("p (h d m t l) -> p d t h m l", d=2, t=2, l=1 << fl, m=1 << (fm - fl - 1))
                return [(v[:, d, 0], v[:, d, 1], d == 1) for d in range(2)]

            def pair_view(tile, lay, m, l):
                fl = free_bit(lay, l)
                fm = free_bit(lay, m) if m < 16 else None
                if fm is None:
                    return [tile[:, :].rearrange("p (h l) -> p h l", l=1 << fl)]
                v = tile[:, :].rearrange("p (h d m l) -> p d h m l", d=2, l=1 << fl, m=1 << (fm - fl - 1))
                return [v[:, 0], v[:, 1]]

            lay = "T"
            cp, op = pp[0], pp[1]
            nturn = [0]

            def turn(tile, dest):
                assert tile is TURNS[nturn[0]]
                dve.sem_inc(turn_asked, 1)
                nturn[0] += 1
                dve.wait_ge(turned, nturn[0])
                step(nc.vector.tensor_copy(dest[:, :], xt_ps[0][:, :]))

            todo = phases()
            for n, (L, m, ls) in enumerate(todo):
                payload = m >= 15
                if L != lay:
                    turn(cur, oth)
                    cur, oth = oth, cur
                    if payload:
                        turn(cp, op)
                        cp, op = op, cp
                    lay = L
                flip = L == "T" and 7 <= m <= 13
                if flip:
                    step(TS(oth[:, :], cur[:, :], sign[:, m - 7:m - 6], None, ALU.mult))
                    cur, oth = oth, cur
                for l in ls:
                    c2, o2 = halves(cur, L, m, l), halves(oth, L, m, l)
                    if payload:
                        sw = pair_view(swap, L, m, l)
                        for (a, b, desc), s_ in zip(c2, sw):
                            TT(s_, a, b, ALU.is_lt if desc else ALU.is_gt)
                        pa, pb = halves(cp, L, 16, l)[0][0:2]
                        qa, qb = halves(op, L, 16, l)[0][0:2]
                        dl = pair_view(delta, L, 16, l)[0]
                        sf = pair_view(swap, L, 16, l)[0]
                        step(TT(dl, pb, pa, ALU.subtract))
                        ins = TT(dl, dl, sf, ALU.mult)
                        ins.then_inc(S["sort_step"], 1)
                        sstep[0] += 1
                    for n2, ((a, b, desc), (oa, ob, _)) in enumerate(zip(c2, o2)):
                        TT(oa, a, b, ALU.max if desc else ALU.min)
                        ins = TT(ob, a, b, ALU.min if desc else ALU.max)
                    step(ins)
                    cur, oth = oth, cur
                    if payload:
                        TT(qa, pa, dl, ALU.add)
                        step(TT(qb, pb, dl, ALU.subtract))
                        cp, op = op, cp
                if flip:
                    step(TS(oth[:, :], cur[:, :], sign[:, m - 7:m - 6], None, ALU.mult))
                    cur, oth = oth, cur
                if L == "T" and m == 14:
                    step(TS(key_i[:, :], cur[:, :].bitcast(I32), (1 << LOCAL_BITS) - 1, None, ALU.bitwise_and))
                    step(TT(cp[:, :], key_i[:, :], block_e[:, :], ALU.add))
                    step(TS(key_i[:, :], cur[:, :].bitcast(I32), LOCAL_BITS, None, ALU.logical_shift_right))
                    step(TS(oth[:, :], key_i[:, :], -float(KEY_SHIFT), None, ALU.add))
                    cur, oth = oth, cur
            turn(cur, oth)
            cur, oth = oth, cur
            turn(cp, op)
            cp, op = op, cp
            nc.vector.tensor_copy(target[:, :], cur[:, 0:TILES + 1]).then_inc(S["sorted_"], 1)
            dve.wait_ge(S["sorted_"], 1)
            TS(edge_idx[:, :], cp[:, 0:TILES], float(E - 1), None, ALU.min).then_inc(S["columns_set"], 1)
            TS(target_idx[:, :], target[:, 0:TILES], float(N - 1), None, ALU.min).then_inc(S["columns_set"], 1)
            nc.vector.memset(prev_last[:, 0:1], -1.0)
            step(TS(prev_last[:, 1:TILES], target[:, 0:TILES - 1], 1.0, is_last_p[:, :], ALU.add, ALU.mult))
            TS(prev_last[:, 1:TILES], prev_last[:, 1:TILES], -1.0, None, ALU.add).then_inc(S["columns_set"], 1)
            dve.wait_ge(S["shifted"], 1)
            step(TT(run_end[:, :], target[:, 0:TILES], bank_a[:, 0:TILES], ALU.is_equal))
            nc.vector.scalar_tensor_tensor(out=rep_idx[:, :], in0=run_end[:, :], scalar=float(1 << 20), in1=target[:, 0:TILES],
                                           op0=ALU.mult, op1=ALU.add).then_inc(S["columns_set"], 1)
            dve.wait_ge(S["weights_loaded"], 16 * WEIGHT_DMAS)
            dve.wait_ge(S["zero_set"], 4)
            TT(b3[:, 0:2 * HID], bi3[:, 0:2 * HID], bh3[:, 0:2 * HID], ALU.add)
            nc.vector.tensor_copy(b3[:, 2 * HID:3 * HID], bh3[:, 2 * HID:3 * HID])
            step(nc.vector.tensor_copy(b3[:, 3 * HID:4 * HID], bi3[:, 2 * HID:3 * HID]))
            step(nc.vector.tensor_copy(bias_part[:, 0, :], b3[:, :]))
            step(TT(bias_rest[:, :], b3[:, :], bias_part[:, 0, :], ALU.subtract))
            step(nc.vector.tensor_copy(bias_part[:, 1, :], bias_rest[:, :]))
            step(TT(b3[:, :], bias_rest[:, :], bias_part[:, 1, :], ALU.subtract))
            step(nc.vector.tensor_copy(bias_part[:, 2, :], b3[:, :]))
            step(TS(bias_acc[:, :], bias_part[:, 0, :], ident[0:3, 0:1], None, ALU.mult))
            step(nc.vector.scalar_tensor_tensor(out=bias_acc[:, :], in0=bias_part[:, 1, :], scalar=ident[0:3, 1:2],
                                                in1=bias_acc[:, :], op0=ALU.mult, op1=ALU.add))
            for hlf in range(2):
                ins = nc.vector.scalar_tensor_tensor(out=bias_rows[0:3, 4 * HID * hlf:4 * HID * (hlf + 1)], in0=bias_part[:, 2, :],
                                                     scalar=ident[0:3, 2:3], in1=bias_acc[:, :], op0=ALU.mult, op1=ALU.add)
            dve.wait_ge(S["rows_stored"], 16)
            nc.vector.memset(hidden[HID:HID + 1, :], 1.0).then_inc(S["bias_set"], 1)

            def finish(i, j, par):
                if not is_first(i):
                    dve.wait_ge(y_stored[j], i * 16)
                norm_stats(dve, "", i * JT + j, i * UNITS + 3 * JT + j, x_t[par][j], h_t[j][1], y_t[j], sq,
                           ln_sum[:, 0:NU], var[:, NU * j:NU * j + NU])

            def update(i, k, par):
                j, t = k % JT, k // JT
                kk_ = i * UNITS + k
                h = x_t[par][j] if t == 0 else h_t[j][(t - 1) % 2]

                def last():
                    if t == 0 and not is_first(i):
                        dve.wait_ge(h_stored[j][0], i * 32)
                    if t == 2:
                        dve.wait_ge(h_stored[j][0], i * 32 + 16)
                    if t == 3:
                        dve.wait_ge(h_stored[j][1], i * 16 + 16)
                    vec_h(dve, "", kk_, k % 2, h_t[j][t % 2])
                return (lambda: vec_diff(dve, "", kk_, k % 2, h), lambda: vec_gate(dve, "", kk_, k % 2), last)

            def dense(i, par, uses):
                for k in range(UNITS):
                    kk_ = i * UNITS + k
                    if k == 0:
                        up = None if is_first(i) else update(i - 1, UNITS - 1, 1 - par)
                    else:
                        up = update(i, k - 1, par)
                    vec_r_hn(dve, "", kk_, k % 2)
                    if up:
                        up[0]()
                    vec_pre(dve, "", kk_, k % 2)
                    if up:
                        up[1]()
                        up[2]()
                    if k == 0 and not is_first(i):
                        finish(i - 1, JT - 1, 1 - par)
                    if k > 3 * JT:
                        finish(i, k - 1 - 3 * JT, par)
                    if k == 1 and not is_first(i):
                        newton(dve, "", (i - 1) * NEWTON_OPS, i * JT, 16)
                    if 2 <= k < 2 + JT and not is_first(i):
                        scale_y(i - 1, k - 2)
                    if k == 7:
                        dve.wait_ge(S[f"rows_got{par}"], (uses + 1) * (16 * GT))
                        nc.vector.tensor_copy(src_node[:, bass.ds(i * GT, GT)],
                                              rows_g[par][:, :, ED:ROW].bitcast(I32).rearrange("p u o -> p (u o)")).then_inc(S["src_saved"], 1)

            def scale_y(i, j):
                nc.vector.tensor_tensor(y_t[j], y_t[j], rstd[:, NU * j:NU * j + NU].unsqueeze(2).to_broadcast([P, NU, HID]),
                                        ALU.mult).then_inc(S["y_ready"], 1)

            run_iterations(dve, dense, ITERS)
            for f in update(ITERS - 1, UNITS - 1, 0):
                f()
            finish(ITERS - 1, JT - 1, 0)
            newton(dve, "", (ITERS - 1) * NEWTON_OPS, ITERS * JT, 16)
            for j in range(JT):
                scale_y(ITERS - 1, j)

            for j in range(JT):
                dve.wait_ge(h_stored[j][0], 16 * 2 * ITERS)
                dve.wait_ge(h_stored[j][1], 16 * ITERS)
                dve.wait_ge(y_stored[j], 16 * ITERS)
            dve.wait_ge(S["xj_stored0"], 16 * 25)
            dve.wait_ge(S["xj_stored1"], 16 * 24)
            dve.wait_ge(S["xi_stored0"], 16 * 25)
            dve.wait_ge(S["xi_stored1"], 16 * 24)
            dve.wait_ge(S["base_copied"], 2 * GROUPS)
            for t in range(STEPS):
                def copy_targets(g, par, t=t):
                    gg = g + t * GROUPS
                    if not (t == 0 and isinstance(g, int) and g < 2):
                        dve.wait_ge(S["bcast_ready"], gg * 2 - 2)
                    nc.vector.tensor_copy(tgt_g[par], target[:, bass.ds(g * GT, GT)]).then_inc(S["tgt_copied"], 1)

                def make_same(g, half, t=t):
                    gg = g + t * GROUPS
                    dve.wait_ge(S["bcast_ready"], gg * 2 + half + 1)
                    if not (t == 0 and is_first(g)):
                        dve.wait_ge(S["agg_summed"], gg * GT - GT + 4 * half + 4)
                    rows = bank_b[:, :].rearrange("p (u s) -> p u s", u=4)
                    for o, cols in ((same[half], target), (same_prev[half], prev_last)):
                        c = cols[:, bass.ds(g * GT + 4 * half, 4)].unsqueeze(2).to_broadcast([P, 4, P])
                        ins = nc.vector.tensor_tensor(o, rows, c, ALU.is_equal)
                    ins.then_inc(S["same_ready"], 1)

                def make_msg(g, par, uses, t=t):
                    gg = g + t * GROUPS
                    if t == 0:
                        dve.wait_ge(S[f"g_loaded{par}"], (uses + 1) * 16)
                    else:
                        dve.wait_ge(S[f"g_got{par}"], (uses + (t - 1) * (25 if par == 0 else 24) + 1) * (16 * GT))
                    if not (t == 0 and isinstance(g, int) and g < 2):
                        dve.wait_ge(S["agg_summed"], gg * GT - GT)
                    nc.vector.tensor_tensor(msg[par].rearrange("p u f -> p (u f)"), g_c[par].rearrange("p u f -> p (u f)"),
                                            msg_base[:, bass.ds(g * (GT * HID), GT * HID)], ALU.mult).then_inc(S["msg_ready"], 1)

                def unit(g, par, uses, b, t=t):
                    n = (g + t * GROUPS) * 2 + b
                    hb = h_c[par][:, 4 * b:4 * b + 4, :]
                    vec_r_hn(dve, "c_", n, b)
                    vec_pre(dve, "c_", n, b)

                def unit_end(g, par, uses, b, t=t):
                    n = (g + t * GROUPS) * 2 + b
                    hb = h_c[par][:, 4 * b:4 * b + 4, :]
                    vec_diff(dve, "c_", n, b, xc[par][:, 4 * b:4 * b + 4, HID:2 * HID])
                    vec_gate(dve, "c_", n, b)
                    if b == 0 and not (t == 0 and isinstance(g, int) and g < 2) and t < STEPS - 1:
                        dve.wait_ge(S[f"hc_stored{par}"], (uses + t * (25 if par == 0 else 24)) * 16)
                    vec_h(dve, "c_", n, b, hb)
                    if t == STEPS - 1:
                        if b == 0:
                            dve.wait_ge(S[f"xi_loaded{par}"], (uses + 1) * 16)
                            if not (isinstance(g, int) and g < 2):
                                dve.wait_ge(S[f"y_put{par}"], uses * (16 * GT))
                        yb = y_c[par][:, 4 * b:4 * b + 4, :]
                        norm_stats(dve, "c_", g * 2 + b, n, xi_c[par][:, 4 * b:4 * b + 4, :], hb, yb, sq_c,
                                   ln_sum_c[:, 0:NU], var[:, NU * b:NU * b + NU])
                        if b == 1:
                            newton(dve, "c_", g * NEWTON_OPS, g * 2 + 2, 8)
                            for c in range(2):
                                yc = y_c[par][:, 4 * c:4 * c + 4, :]
                                nc.vector.tensor_tensor(yc, yc, rstd[:, NU * c:NU * c + NU].unsqueeze(2).to_broadcast([P, NU, HID]),
                                                        ALU.mult).then_inc(S["c_y_ready"], 1)

                def slots(g, par, uses, t=t):
                    prev = not is_first(g)
                    pu = uses if par == 1 else uses - 1
                    make_same(g, 1)
                    if not is_end(g, GROUPS):
                        copy_targets(g + 1, 1 - par)
                    if prev:
                        unit(g - 1, 1 - par, pu, 0)
                        unit_end(g - 1, 1 - par, pu, 0)
                    if not is_end(g, GROUPS):
                        make_same(g + 1, 0)
                        make_msg(g + 1, 1 - par, uses if par == 0 else uses + 1)
                    if prev:
                        unit(g - 1, 1 - par, pu, 1)
                        unit_end(g - 1, 1 - par, pu, 1)

                copy_targets(0, 0)
                make_same(0, 0)
                make_msg(0, 0, 0)
                run_groups(dve, slots)
                for b in range(2):
                    unit(GROUPS - 1, 0, 24, b)
                    unit_end(GROUPS - 1, 0, 24, b)


def kernel(**inputs):
    import numpy as np
    import concourse.bacc as bacc
    from concourse.bass_utils import run_bass_kernel_spmd

    nc = bacc.Bacc("TRN2", target_bir_lowering=False, num_devices=1)
    g = {k: np.asarray(v) for k, v in inputs.items()}
    arrays = {
        "x": g["x"], "src": g["src"], "dst": g["dst"], "attr": g["edge_attr_32"],
        "w1t": g["L0_gnn_W1"].T, "b1": g["L0_gnn_b1"], "w2t": g["L0_gnn_W2"].T, "b2": g["L0_gnn_b2"],
        "wit": g["L0_gnn_W_ih"].T, "bih": g["L0_gnn_b_ih"], "wht": g["L0_gnn_W_hh"].T, "bhh": g["L0_gnn_b_hh"],
    }
    arrays = {k + "_dram": np.ascontiguousarray(v) for k, v in arrays.items()}
    args = [nc.dram_tensor(k, v.shape, mybir.dt.from_np(v.dtype), kind="ExternalInput").ap() for k, v in arrays.items()]
    out = nc.dram_tensor("out_0_dram", (N, HID), F32, kind="ExternalOutput").ap()
    gnn_program(nc, *args, out)
    r = run_bass_kernel_spmd(nc, [arrays], core_ids=[0])
    return r.results[0]["out_0_dram"]
```

```python
from contextlib import ExitStack

import concourse.bass as bass
from concourse import mybir

ALU = mybir.AluOpType
ACT = mybir.ActivationFunctionType
F32 = mybir.dt.float32
BF16 = mybir.dt.bfloat16
I32 = mybir.dt.int32
AX_X = mybir.AxisListType.X

P = 128
N = 100000
E = 50000
HID = 64
ED = 32
STEPS = 4
EPS = 1e-5

SORT_COLS = 512
BLOCKS = 4
BLOCK_E = E // BLOCKS
LOAD_P = 125
LOAD_F = BLOCK_E // LOAD_P
LOCAL_BITS = 14
KEY_SHIFT = 512
PAD_KEY = N + 351

GT = 8
GROUPS = (E + GT * P - 1) // (GT * P)
TILES = GROUPS * GT
SLOTS = TILES * P
ROW = ED + 1

NU = 4
NODE_TILE = P * NU
NODE_TILES = (N + NODE_TILE - 1) // NODE_TILE
JT = 4
ITERS = NODE_TILES // JT
UNITS = JT * STEPS
LAST_BASE = N - NODE_TILE
LAST_NEW_P = (NODE_TILES * NODE_TILE - N) // NU
MAP_COLS = (N + P - 1) // P
assert NODE_TILES == ITERS * JT and ITERS == GROUPS and ITERS % 2 == 1
NEWTON = 4
NEWTON_OPS = 4 + 3 * NEWTON


def gnn_program(nc, x, src, dst, attr, w1t, b1, w2t, b2, wit, bih, wht, bhh, out):
    edge_rows = nc.dram_tensor("edge_rows", (E, ROW), F32, kind="Internal").ap()
    row_map = nc.dram_tensor("row_map", (P * MAP_COLS, 1), I32, kind="Internal").ap()
    table = [None] + [nc.dram_tensor(f"table{t}", (N + SLOTS, HID), F32, kind="Internal").ap() for t in range(1, STEPS)]
    slot_x = nc.dram_tensor("slot_x", (SLOTS, HID), F32, kind="Internal").ap()
    slot_src = nc.dram_tensor("slot_src", (SLOTS, HID), F32, kind="Internal").ap()

    def slot_rows(ap, g):
        return ap.rearrange("(g p u) f -> g p (u f)", p=P, u=GT)[bass.ds(g, 1), :, :].rearrange("o p f -> (o p) f")

    slot_table = [slot_x] + [table[t][N:N + SLOTS, :] for t in range(1, STEPS)]

    def node_rows(ap, tile):
        full = ap[0:(NODE_TILES - 1) * NODE_TILE, :].rearrange("(t p u) f -> t p (u f)", p=P, u=NU)
        return full[bass.ds(tile, 1), :, :].rearrange("o p f -> (o p) f")

    with ExitStack() as ctx:
        def sb(name, shape, dt=F32):
            return ctx.enter_context(nc.sbuf_tensor(name, list(shape), dt))

        def ps(name, shape):
            return ctx.enter_context(nc.psum_tensor(name, list(shape), F32))

        def sem(name):
            return ctx.enter_context(nc.semaphore(name))

        ident = sb("ident", [P, P])
        shift_t = sb("shift_t", [P, P])
        wrap_t = sb("wrap_t", [P, P])
        before_t = sb("before_t", [P, P])
        ident_bf = sb("ident_bf", [P, P], BF16)
        is_last_p = sb("is_last_p", [P, 1])
        p_col = sb("p_col", [P, 8], I32)
        p_bit = sb("p_bit", [P, 8], I32)
        sign = sb("sign", [P, 8])
        slot_row_id = sb("slot_row_id", [P, TILES], I32)
        ones_bf = sb("ones_bf", [P, P], BF16)
        gate_w = sb("gate_w", [P, 4 * HID])
        gate_pair = sb("gate_pair", [P, 3 * P])
        bi_col = sb("bi_col", [P, 3])
        bh_col = sb("bh_col", [P, 3])
        b_rz = sb("b_rz", [P, 2])
        w1_t = sb("w1_t", [ED, HID])
        w2_b = sb("w2_b", [HID + 1, HID])
        b1_col = sb("b1_col", [HID, 1])
        bi3 = sb("bi3", [3, 3 * HID])
        bh3 = sb("bh3", [3, 3 * HID])
        b3 = sb("b3", [3, 4 * HID])
        bias_rest = sb("bias_rest", [3, 4 * HID])
        bias_part = sb("bias_part", [3, 3, 4 * HID], BF16)
        bias_acc = sb("bias_acc", [3, 4 * HID])
        bias_rows = sb("bias_rows", [P, 8 * HID], BF16)

        target = sb("target", [P, TILES + 1])
        rank = sb("rank", [P, TILES])
        prev_run = sb("prev_run", [P, TILES])
        target_idx = sb("target_idx", [P, TILES], I32)
        edge_idx = sb("edge_idx", [P, TILES], I32)
        rep_idx = sb("rep_idx", [P, TILES], I32)
        src_node = sb("src_node", [P, TILES], I32)
        src_row = sb("src_row", [P, TILES], I32)

        msg_base = sb("msg_base", [P, TILES * HID])
        idx_g = {name: [sb(f"{name}_idx{b}", [P, GT], I32) for b in range(2)] for name in ("rows", "xj", "xi", "map", "node", "src", "y")}
        map_row_g = [sb(f"map_row_g{b}", [P, GT], I32) for b in range(2)]
        src_row_g = [sb(f"src_row_g{b}", [P, GT], I32) for b in range(2)]
        run_on = sb("run_on", [P, TILES])
        run_end = sb("run_end", [P, TILES])
        dst_stage = sb("dst_stage", [LOAD_P, E // LOAD_P], I32)[:, :]
        attr_stage = msg_base[0:LOAD_P, 0:E // LOAD_P * ED]
        scratch = [E // LOAD_P * ED]

        def square(cols=SORT_COLS, dt=F32):
            a = msg_base[:, scratch[0]:scratch[0] + cols]
            scratch[0] += cols
            assert scratch[0] <= TILES * HID
            return a.bitcast(dt) if dt != F32 else a

        key_i = square(dt=I32)
        local_e = square(dt=I32)
        block_e = square()
        kk = [square(), square()]
        pp = [square(), square()]
        swap = square(SORT_COLS // 2)
        delta = square(SORT_COLS // 2)
        node_id = square(MAP_COLS, I32)

        RZ = [sb(f"rz{b}", [P, NU, 2 * HID]) for b in range(2)]
        pre = [sb(f"pre{b}", [P, NU, HID]) for b in range(2)]
        cand = [sb(f"cand{b}", [P, NU, HID]) for b in range(2)]
        dif = [sb(f"dif{b}", [P, NU, HID]) for b in range(2)]
        xt = [sb(f"xt{b}", [P, 4 * P]) for b in range(2)]
        var = sb("var", [P, 16])
        vhalf = sb("vhalf", [P, 16])
        rstd = sb("rstd", [P, 16])
        nt1 = sb("nt1", [P, 16])
        nt2 = sb("nt2", [P, 16])

        ARENA = E // LOAD_P * ROW
        arena = sb("arena", [P, ARENA])
        at = [0]

        def carve(cols):
            a = arena[:, at[0]:at[0] + cols]
            at[0] += cols
            assert at[0] <= ARENA, at[0]
            return a

        def v3(a, u):
            return a.rearrange("p (u f) -> p u f", u=u)

        edge_stage = arena[0:LOAD_P, :].rearrange("p (r d) -> p r d", d=ROW)
        TW = NU * HID
        x_t = [[v3(carve(TW), NU) for j in range(JT)] for b in range(2)]
        h_t = [[v3(carve(TW), NU) for b in range(2)] for j in range(JT)]
        x_turn = [carve(TW) for j in range(JT)]
        h_turn = [carve(TW) for j in range(JT)]
        y_t = [v3(carve(TW), NU) for j in range(JT)]
        sq = v3(carve(TW), NU)
        rows_g = [v3(carve(GT * ROW), GT) for b in range(2)]
        xj_g = [v3(carve(GT * HID), GT) for b in range(2)]
        xi_g = [v3(carve(GT * HID), GT) for b in range(2)]
        attr_t = carve(4 * P)
        hidden = carve(4 * P)
        ln_sum = carve(8)
        at[0] = 0
        xc = [v3(carve(GT * 2 * HID), GT) for b in range(2)]
        g_c = [v3(carve(GT * HID), GT) for b in range(2)]
        msg = [v3(carve(GT * HID), GT) for b in range(2)]
        same = [v3(carve(4 * P), 4) for h in range(2)]
        same_prev = [v3(carve(4 * P), 4) for h in range(2)]
        h_c = [v3(carve(GT * HID), GT) for b in range(2)]
        xi_c = [v3(carve(GT * HID), GT) for b in range(2)]
        y_c = [v3(carve(GT * HID), GT) for b in range(2)]
        sq_c = v3(carve(TW), NU)
        rank_g = [carve(GT // 2).bitcast(BF16) for b in range(2)]
        ln_sum_c = carve(8)

        gates = [ps(f"gates{b}", [P, NU, 4 * HID]) for b in range(2)]
        xt_ps = [ps(f"xt_ps{b}", [P, 4 * P]) for b in range(2)]
        bank_a = ps("bank_a", [P, 4 * P])
        bank_b = ps("bank_b", [P, 4 * P])

        def dense_gate(k2, g):
            return gates[k2][:, :, :].rearrange("p u f -> p (u f)")[:, g * TW:(g + 1) * TW]

        def flat(tile):
            return tile[:, :, :].rearrange("p u f -> p (u f)")

        S = {}
        for name in (
            "pad_set", "keys_loaded", "weights_loaded", "attr_loaded", "dst_loaded", "zero_set", "consts_set", "masks_set",
            "rows_made", "rows_stored", "map_stored", "sort_step", "flipped", "unflipped", "sorted_", "shifted", "columns_set", "before_set", "ends_set", "ranked", "ranks_set",
            "setup_step", "bias_set",
            "x_loaded0", "x_loaded1", "x_turned", "x_turn_copied", "back_turned", "rows_ready", "gates_ready", "r_ready", "z_ready", "pre_tanh_ready",
            "n_ready", "diff_ready", "gated_ready", "h_ready", "resid_ready", "sum_ready", "center_ready", "square_ready",
            "var_ready", "newton_step", "y_ready",
            "rows_got0", "rows_got1", "xj_got0", "xj_got1", "xi_got0", "xi_got1", "map_put", "xj_stored0", "xj_stored1",
            "xi_stored0", "xi_stored1", "src_saved", "attr_turned", "attr_t_copied", "hidden_summed", "hidden_ready", "base_summed", "base_copied",
            "src_row_got", "rows_idx_set", "xj_idx_set", "xi_idx_set", "map_idx_set", "node_idx_set", "src_idx_set", "y_idx_set", "pool_passed", "map_rows_set", "src_rows_saved",
            "rank_copied", "bcast_ready", "same_ready", "msg_ready", "agg_summed", "agg_copied", "g_got0", "g_got1",
            "g_loaded0", "g_loaded1", "xc_loaded0", "xc_loaded1", "xi_loaded0", "xi_loaded1", "hc_stored0", "hc_stored1",
            "c_xt_ready", "c_xt_copied", "c_gates_ready", "c_rz_ready", "c_r_hn_ready", "c_pre_tanh_ready",
            "c_n_ready", "c_diff_ready", "c_gated_ready", "c_h_ready", "c_resid_ready", "c_sum_ready", "c_center_ready",
            "c_square_ready", "c_var_ready", "c_newton_step", "c_y_ready", "y_put0", "y_put1",
        ):
            S[name] = sem(name)
        h_stored = [[sem(f"h_stored_{j}_{b}") for b in range(2)] for j in range(JT)]
        y_stored = [sem(f"y_stored_{j}") for j in range(JT)]

        turn_asked = sem("turn_asked")
        turned = sem("turned")

        block = ctx.enter_context(nc.Block())

        WEIGHT_DMAS = 23
        BACK_LAG = 3
        X_TICKS = {10: 0, 11: 1, 12: 2, 13: 3}
        NORM_TICKS = {1: ((0, 0), (0, 1)), 2: ((1, 0), (0, 2), (0, 3)), 3: ((2, 0), (0, 4), (1, 1)), 4: ((3, 0), (1, 2), (1, 3)),
                      5: ((1, 4), (2, 1), (2, 2)), 6: ((2, 3), (2, 4), (3, 1)), 7: ((3, 2), (3, 3), (3, 4))}
        NEWTON_TICKS = {8: 0, 9: 1, 10: 2}
        SCALE_TICKS = {11: (0, 1), 12: (2, 3)}
        MLP_TICKS = {6: (0, 0), 7: (0, 1), 9: (0, 2), 10: (1, 0), 12: (1, 1), 14: (1, 2)}

        def run_iterations(eng, body, count):
            body(0, 0, 0)
            with eng.Fori(0, (count - 3) // 2) as m:
                body(m * 2 + 1, 1, m)
                body(m * 2 + 2, 0, m + 1)
            body(count - 2, 1, (count - 3) // 2)
            body(count - 1, 0, (count - 1) // 2)

        def run_groups(eng, body, peel=3):
            for g in range(peel):
                body(g, g % 2, g // 2)
            with eng.Fori((peel - 1) // 2, (GROUPS - 3) // 2) as m:
                body(m * 2 + 1, 1, m)
                body(m * 2 + 2, 0, m + 1)
            body(GROUPS - 2, 1, (GROUPS - 3) // 2)
            body(GROUPS - 1, 0, (GROUPS - 1) // 2)

        def is_first(i):
            return isinstance(i, int) and i == 0

        def is_end(i, count):
            return isinstance(i, int) and i == count - 1

        def phases():
            res = []
            for m in range(1, 17):
                high = [l for l in range(m - 1, -1, -1) if l >= 14 or 7 <= l]
                low = [l for l in range(m - 1, -1, -1) if l < 7]
                if high:
                    res.append(("N", m, high))
                res.append(("T", m, low))
            return res

        def turn_list():
            res, lay, k, p = [], "T", 0, 0
            for L, m, ls in phases():
                if L != lay:
                    res.append(kk[k])
                    k ^= 1
                    if m >= 15:
                        res.append(pp[p])
                        p ^= 1
                    lay = L
                k ^= len(ls) & 1
                if m >= 15:
                    p ^= len(ls) & 1
                if L == "T" and m == 14:
                    k ^= 1
            return res + [kk[k], pp[p]]

        TURNS = turn_list()

        @block.sync
        def _(sp):
            sp.wait_ge(S["pad_set"], 1)
            with nc.allow_non_contiguous_dma(reason="small loads"):
                sp.dma_start(key_i[0:LOAD_P, :].rearrange("p (q f) -> p q f", q=BLOCKS)[:, :, 0:LOAD_F],
                             src.rearrange("(q p f) -> p q f", q=BLOCKS, p=LOAD_P)).then_inc(S["keys_loaded"], 16)
                sp.dma_start(attr_stage, attr.rearrange("(p r) d -> p (r d)", p=LOAD_P)).then_inc(S["attr_loaded"], 16)
                sp.dma_start(dst_stage, dst.rearrange("(p r) -> p r", p=LOAD_P)).then_inc(S["dst_loaded"], 16)
                sp.wait_ge(S["zero_set"], 5)
                w = S["weights_loaded"]
                sp.dma_start(gate_w[0:HID, 0:2 * HID], wit[:, 0:2 * HID]).then_inc(w, 16)
                sp.dma_start(gate_w[0:HID, 3 * HID:4 * HID], wit[:, 2 * HID:3 * HID]).then_inc(w, 16)
                sp.dma_start(gate_w[HID:P, 0:3 * HID], wht).then_inc(w, 16)
                for hf in range(2):
                    rows = slice(hf * HID, (hf + 1) * HID)
                    for g in range(3):
                        sp.dma_start(gate_pair[rows, g * P + hf * HID:g * P + (hf + 1) * HID], wht[:, g * HID:(g + 1) * HID]).then_inc(w, 16)
                    sp.dma_start(bi_col[rows, :], bih.rearrange("(g f) -> f g", g=3)).then_inc(w, 16)
                    sp.dma_start(bh_col[rows, :], bhh.rearrange("(g f) -> f g", g=3)).then_inc(w, 16)
                sp.dma_start(w1_t[:, :], w1t).then_inc(w, 16)
                sp.dma_start(w2_b[0:HID, :], w2t).then_inc(w, 16)
                sp.dma_start(w2_b[HID:HID + 1, :], b2.rearrange("(o f) -> o f", o=1)).then_inc(w, 16)
                sp.dma_start(b1_col[:, :], b1.rearrange("(f o) -> f o", o=1)).then_inc(w, 16)
                for k in range(3):
                    sp.dma_start(bi3[k:k + 1, :], bih.rearrange("(o f) -> o f", o=1)).then_inc(w, 16)
                    sp.dma_start(bh3[k:k + 1, :], bhh.rearrange("(o f) -> o f", o=1)).then_inc(w, 16)
            sp.wait_ge(S["consts_set"], 1)
            sp.dma_start(row_map.rearrange("(p c) o -> p (c o)", p=P), node_id[:, :]).then_inc(S["map_stored"], 16)
            sp.wait_ge(S["rows_made"], 2)
            sp.dma_start(edge_rows.rearrange("(p r) d -> p (r d)", p=LOAD_P),
                         edge_stage[:, :, :].rearrange("p r d -> p (r d)")).then_inc(S["rows_stored"], 16)

            def load_x(i, par):
                for j in range(JT):
                    if is_end(i, ITERS) and j == JT - 1:
                        rows = x[LAST_BASE:N, :].rearrange("(p u) f -> p (u f)", p=P)
                    else:
                        rows = node_rows(x, i * JT + j)
                    sp.dma_start(x_t[par][j].rearrange("p u f -> p (u f)"), rows).then_inc(S[f"x_loaded{par}"], 16)

            def store_tile(dram, i, j, tile):
                if is_end(i, ITERS) and j == JT - 1:
                    return (dram[LAST_BASE + NU * LAST_NEW_P:N, :].rearrange("(p u) f -> p (u f)", u=NU),
                            tile[LAST_NEW_P:P].rearrange("p u f -> p (u f)"))
                return node_rows(dram, i * JT + j), tile.rearrange("p u f -> p (u f)")

            def store_y(i, j):
                sp.wait_ge(S["y_ready"], i * JT + j + 1)
                d, s = store_tile(out, i, j, y_t[j])
                sp.dma_start(d, s).then_inc(y_stored[j], 16)

            def store_gathers(i, par, uses):
                sp.wait_ge(S[f"xj_got{par}"], (uses + 1) * (16 * GT))
                sp.dma_start(slot_rows(slot_src, i), xj_g[par].rearrange("p u f -> p (u f)")).then_inc(S[f"xj_stored{par}"], 16)
                sp.wait_ge(S[f"xi_got{par}"], (uses + 1) * (16 * GT))
                sp.dma_start(slot_rows(slot_x, i), xi_g[par].rearrange("p u f -> p (u f)")).then_inc(S[f"xi_stored{par}"], 16)

            def dense(i, par, uses):
                for k in range(3 * JT):
                    j, t = k % JT, k // JT
                    if k == 2 and not is_end(i, ITERS):
                        if not is_first(i):
                            sp.wait_ge(S["resid_ready"], i * JT)
                        load_x(i + 1, 1 - par)
                    if k == 6 and not is_first(i):
                        store_gathers(i - 1, 1 - par, uses - par_uses(par))
                    if k >= 10 and not is_first(i):
                        store_y(i - 1, 2 * (k - 10))
                        store_y(i - 1, 2 * (k - 10) + 1)
                    sp.wait_ge(S["rows_ready"], i * UNITS + k + 1)
                    d, s = store_tile(table[t + 1], i, j, h_t[j][t % 2])
                    sp.dma_start(d, s).then_inc(h_stored[j][t % 2], 16)

            def par_uses(par):
                return 0 if par == 1 else 1

            sp.wait_ge(S["rows_stored"], 16)
            load_x(0, 0)
            run_iterations(sp, dense, ITERS)
            for j in range(JT):
                store_y(ITERS - 1, j)
            store_gathers(ITERS - 1, 0, (ITERS - 1) // 2)

            def load_g(g, par):
                if not (isinstance(g, int) and g < 2):
                    sp.wait_ge(S["msg_ready"], g - 1)
                sp.dma_start(g_c[par].rearrange("p u f -> p (u f)"), slot_rows(slot_src, g)).then_inc(S[f"g_loaded{par}"], 16)

            def load_states(t, g, par):
                early = isinstance(g, int) and g < 2
                if t == STEPS - 1 and not early:
                    sp.wait_ge(S["c_resid_ready"], (g - 1) * 2)
                elif not (early and t == 0):
                    sp.wait_ge(S["c_diff_ready"], t * GROUPS * 2 if early else (g + t * GROUPS - 1) * 2)
                sp.dma_start(xc[par][:, :, HID:2 * HID],
                             slot_rows(slot_table[t], g).rearrange("p (u f) -> p u f", u=GT)).then_inc(S[f"xc_loaded{par}"], 16)
                if t == STEPS - 1:
                    sp.dma_start(xi_c[par].rearrange("p u f -> p (u f)"), slot_rows(slot_x, g)).then_inc(S[f"xi_loaded{par}"], 16)

            def slot_store(t, g, par):
                sp.wait_ge(S["c_h_ready"], (g + t * GROUPS) * 2 + 2)
                sp.dma_start(slot_rows(slot_table[t + 1], g), h_c[par].rearrange("p u f -> p (u f)")).then_inc(S[f"hc_stored{par}"], 16)

            for j in range(JT):
                sp.wait_ge(h_stored[j][0], 16 * 2 * ITERS)
                sp.wait_ge(h_stored[j][1], 16 * ITERS)
                sp.wait_ge(y_stored[j], 16 * ITERS)
            sp.wait_ge(S["xj_stored0"], 16 * 25)
            sp.wait_ge(S["xj_stored1"], 16 * 24)
            sp.wait_ge(S["xi_stored0"], 16 * 25)
            sp.wait_ge(S["xi_stored1"], 16 * 24)
            sp.wait_ge(S["base_copied"], 2 * GROUPS)
            sp.wait_ge(S["src_saved"], GROUPS)
            for t in range(STEPS):
                def both(g, par, uses, t=t):
                    if t == 0 and not (isinstance(g, int) and g >= GROUPS - 2):
                        load_g(g + 2, par)
                    if not is_end(g, GROUPS):
                        load_states(t, g + 1, 1 - par)
                    if not is_first(g) and t < STEPS - 1:
                        slot_store(t, g - 1, 1 - par)

                if t == 0:
                    load_g(0, 0)
                    load_g(1, 1)
                load_states(t, 0, 0)
                run_groups(sp, both)
                if t < STEPS - 1:
                    slot_store(t, GROUPS - 1, 0)
                    sp.wait_ge(S["hc_stored0"], 16 * 25 * (t + 1))
                    sp.wait_ge(S["hc_stored1"], 16 * 24 * (t + 1))

        @block.gpsimd
        def _(pool):
            pool.memset(key_i[:, :], PAD_KEY).then_inc(S["pad_set"], 1)
            pool.memset(gate_w[:, :], 0.0).then_inc(S["zero_set"], 1)
            pool.memset(gate_pair[:, :], 0.0).then_inc(S["zero_set"], 1)
            pool.memset(bias_rows[:, :], 0.0).then_inc(S["zero_set"], 1)
            pool.memset(ones_bf[:, :], 1.0).then_inc(S["zero_set"], 1)
            pool.memset(w2_b[:, :], 0.0).then_inc(S["zero_set"], 1)
            pool.memset(before_t[:, :], 1.0).then_inc(S["before_set"], 1)
            pool.wait_ge(S["before_set"], 1)
            pool.affine_select(out=before_t[:, :], in_=before_t[:, :], pattern=[[1, P]], compare_op=ALU.is_gt,
                               fill=0.0, base=0, channel_multiplier=-1).then_inc(S["before_set"], 1)
            for n, (tile, base, cm) in enumerate(((ident, 0, 1), (shift_t, -1, 1), (wrap_t, P - 1, P))):
                pool.memset(tile[:, :], 0.0).then_inc(S["masks_set"], 1)
                pool.wait_ge(S["masks_set"], 2 * n + 1)
                pool.affine_select(out=tile[:, :], in_=tile[:, :], pattern=[[-1, P]], compare_op=ALU.not_equal,
                                   fill=1.0, base=base, channel_multiplier=cm).then_inc(S["masks_set"], 1)
            pool.memset(is_last_p[:, :], 0.0).then_inc(S["masks_set"], 1)
            pool.wait_ge(S["masks_set"], 7)
            pool.affine_select(out=is_last_p[:, :], in_=is_last_p[:, :], pattern=[[0, 1]], compare_op=ALU.not_equal,
                               fill=1.0, base=-(P - 1), channel_multiplier=1).then_inc(S["masks_set"], 1)
            pool.iota(local_e[:, :], [[0, BLOCKS], [1, P]], base=0, channel_multiplier=LOAD_F).then_inc(S["masks_set"], 1)
            pool.iota(p_col[:, :], [[0, 8]], base=0, channel_multiplier=1).then_inc(S["masks_set"], 1)
            pool.iota(block_e[:, :], [[BLOCK_E, BLOCKS], [0, P]], base=0, channel_multiplier=0,
                      allow_small_or_imprecise_dtypes=True).then_inc(S["masks_set"], 1)
            pool.iota(node_id[:, :], [[1, MAP_COLS]], base=0, channel_multiplier=MAP_COLS).then_inc(S["consts_set"], 1)
            pool.iota(slot_row_id[:, :], [[GT * P, GROUPS], [1, GT]], base=N, channel_multiplier=GT).then_inc(S["consts_set"], 1)
            pool.wait_ge(S["dst_loaded"], 16)
            pool.tensor_copy(edge_stage[:, :, ED:ROW].bitcast(I32).rearrange("p r o -> p (r o)"), dst_stage).then_inc(S["rows_made"], 1)

            def gather(o, table_ap, idx, bound, s):
                pool.indirect_dma_start(out=o, out_offset=None, in_=table_ap,
                                        in_offset=bass.IndirectOffsetOnAxis(ap=idx, axis=0),
                                        bounds_check=bound).then_inc(s, 16)

            def column(tile, g, u):
                return tile[:, bass.ds(g * GT + u, 1)]

            def take_indices(name, tile, g, par, count):
                pool.tensor_copy(idx_g[name][par][:, :], tile[:, bass.ds(g * GT, GT)]).then_inc(S[name + "_idx_set"], 1)
                pool.wait_ge(S[name + "_idx_set"], count + 1)
                pool.sem_inc(S["pool_passed"], 1)
                return lambda u: idx_g[name][par][:, u:u + 1]

            def get_rows(i, par):
                idx = take_indices("rows", edge_idx, i, par, i)
                for u in range(GT):
                    gather(rows_g[par][:, u, :], edge_rows, idx(u), E - 1, S[f"rows_got{par}"])

            def setup(i, par, uses):
                if not is_end(i, ITERS):
                    if not is_first(i):
                        pool.wait_ge(S["attr_turned"], i * 2)
                        pool.sem_inc(S["pool_passed"], 1)
                        pool.wait_ge(S["src_saved"], i)
                        pool.sem_inc(S["pool_passed"], 1)
                    get_rows(i + 1, 1 - par)
                pool.wait_ge(S[f"rows_got{par}"], (uses + 1) * (16 * GT))
                pool.sem_inc(S["pool_passed"], 1)
                if not (isinstance(i, int) and i < 2):
                    pool.wait_ge(S[f"xj_stored{par}"], uses * 16)
                    pool.sem_inc(S["pool_passed"], 1)
                    pool.wait_ge(S[f"xi_stored{par}"], uses * 16)
                    pool.sem_inc(S["pool_passed"], 1)
                pool.tensor_copy(idx_g["xj"][par][:, :], rows_g[par][:, :, ED:ROW].bitcast(I32).rearrange("p u o -> p (u o)")).then_inc(S["xj_idx_set"], 1)
                pool.wait_ge(S["xj_idx_set"], i + 1)
                pool.sem_inc(S["pool_passed"], 1)
                for u in range(GT):
                    gather(xj_g[par][:, u, :], x, idx_g["xj"][par][:, u:u + 1], N - 1, S[f"xj_got{par}"])
                idx = take_indices("xi", target_idx, i, par, i)
                for u in range(GT):
                    gather(xi_g[par][:, u, :], x, idx(u), N - 1, S[f"xi_got{par}"])
                if not (isinstance(i, int) and i < 2):
                    pool.wait_ge(S["map_put"], (i - 1) * (16 * GT))
                    pool.sem_inc(S["pool_passed"], 1)
                idx = take_indices("map", rep_idx, i, par, i)
                pool.tensor_copy(map_row_g[par][:, :], slot_row_id[:, bass.ds(i * GT, GT)]).then_inc(S["map_rows_set"], 1)
                pool.wait_ge(S["map_rows_set"], i + 1)
                pool.sem_inc(S["pool_passed"], 1)
                for u in range(GT):
                    pool.indirect_dma_start(out=row_map, out_offset=bass.IndirectOffsetOnAxis(ap=idx(u), axis=0),
                                            in_=map_row_g[par][:, u:u + 1], in_offset=None,
                                            bounds_check=N - 1, oob_is_err=False).then_inc(S["map_put"], 16)

            pool.wait_ge(S["rows_stored"], 16)
            pool.wait_ge(S["map_stored"], 16)
            pool.wait_ge(S["columns_set"], 3)
            get_rows(0, 0)
            run_groups(pool, setup)

            pool.wait_ge(S["map_put"], 16 * TILES)
            pool.wait_ge(S["src_saved"], GROUPS)

            def get_src_rows(g, par, uses):
                if not (isinstance(g, int) and g < 2):
                    save_src_rows(g - 2, par)
                idx = take_indices("node", src_node, g, par, g)
                for u in range(GT):
                    gather(src_row_g[par][:, u:u + 1], row_map, idx(u), N - 1, S["src_row_got"])

            def save_src_rows(g, par):
                pool.wait_ge(S["src_row_got"], (g + 2) * (16 * GT))
                pool.sem_inc(S["pool_passed"], 1)
                pool.tensor_copy(src_row[:, bass.ds(g * GT, GT)], src_row_g[par][:, :]).then_inc(S["src_rows_saved"], 1)
                pool.wait_ge(S["src_rows_saved"], g + 1)
                pool.sem_inc(S["pool_passed"], 1)

            run_groups(pool, get_src_rows)
            pool.wait_ge(S["src_row_got"], 16 * TILES)
            for g in (GROUPS - 2, GROUPS - 1):
                pool.tensor_copy(src_row[:, g * GT:(g + 1) * GT], src_row_g[g % 2][:, :]).then_inc(S["src_rows_saved"], 1)
            pool.wait_ge(S["src_rows_saved"], GROUPS)

            def put_y(g, par, uses):
                pool.wait_ge(S["c_y_ready"], g * 2 + 2)
                pool.sem_inc(S["pool_passed"], 1)
                if not (isinstance(g, int) and g < 2):
                    pool.wait_ge(S[f"y_put{par}"], uses * (16 * GT))
                    pool.sem_inc(S["pool_passed"], 1)
                idx = take_indices("y", rep_idx, g, par, g)
                for u in range(GT):
                    pool.indirect_dma_start(out=out, out_offset=bass.IndirectOffsetOnAxis(ap=idx(u), axis=0),
                                            in_=y_c[par][:, u, :], in_offset=None,
                                            bounds_check=N - 1, oob_is_err=False).then_inc(S[f"y_put{par}"], 16)

            for j in range(JT):
                pool.wait_ge(h_stored[j][0], 16 * 2 * ITERS)
                pool.wait_ge(h_stored[j][1], 16 * ITERS)
                pool.wait_ge(y_stored[j], 16 * ITERS)
            for t in range(1, STEPS):
                def get(g, par, uses, t=t):
                    gg = g + t * GROUPS
                    if is_first(g):
                        pool.wait_ge(S["hc_stored0"], 16 * 25 * t)
                        pool.wait_ge(S["hc_stored1"], 16 * 24 * t)
                    early = isinstance(g, int) and g < 2
                    pool.wait_ge(S["msg_ready"], t * GROUPS if early else gg - 1)
                    pool.sem_inc(S["pool_passed"], 1)
                    idx = take_indices("src", src_row, g, par, gg - GROUPS)
                    for u in range(GT):
                        gather(g_c[par][:, u, :], table[t], idx(u), N + SLOTS - 1, S[f"g_got{par}"])
                    if t == STEPS - 1 and not (isinstance(g, int) and g < 3):
                        put_y(g - 3, 1 - par, uses - 1 if par == 1 else uses - 2)

                run_groups(pool, get, 5 if t == STEPS - 1 else 3)
            put_y(GROUPS - 3, 0, 23)
            put_y(GROUPS - 2, 1, 23)
            put_y(GROUPS - 1, 0, 24)
            pool.wait_ge(S["y_put0"], 16 * GT * 25)
            pool.wait_ge(S["y_put1"], 16 * GT * 24)

        def gate_matmuls_bias(k2):
            for b in range(2):
                nc.tensor.matmul(gates[k2][:, 2 * b:2 * b + 2, :].rearrange("p u f -> p (u f)"), ones_bf[:, :], bias_rows[:, :],
                                 start=True, stop=False, skip_group_check=True)

        def sigmoid_unit(act, c, k, k2):
            act.wait_ge(S[c + "gates_ready"], k + 1)
            if not (isinstance(k, int) and k < 2):
                act.wait_ge(S[c + "gated_ready"], k - 1)
            nc.scalar.activation(RZ[k2][:, :, :], gates[k2][:, :, 0:2 * HID], ACT.Sigmoid).then_inc(S[c + "rz_ready"], 1)

        def tanh_unit(act, c, k, k2):
            act.wait_ge(S[c + "pre_tanh_ready"], k + 1)
            if not (isinstance(k, int) and k < 2):
                act.wait_ge(S[c + "h_ready"], k - 1)
            nc.scalar.activation(cand[k2][:, :, :], pre[k2][:, :, :], ACT.Tanh).then_inc(S[c + "n_ready"], 1)

        def vec_r_hn(dve, c, k, k2):
            dve.wait_ge(S[c + "rz_ready"], k + 1)
            if not (isinstance(k, int) and k < 2):
                dve.wait_ge(S[c + "n_ready"], k - 1)
            nc.vector.tensor_tensor(pre[k2][:, :, :], gates[k2][:, :, 2 * HID:3 * HID], RZ[k2][:, :, 0:HID],
                                    ALU.mult).then_inc(S[c + "r_hn_ready"], 1)

        def vec_pre(dve, c, k, k2):
            dve.wait_ge(S[c + "r_hn_ready"], k + 1)
            nc.vector.tensor_tensor(pre[k2][:, :, :], pre[k2][:, :, :], gates[k2][:, :, 3 * HID:4 * HID],
                                    ALU.add).then_inc(S[c + "pre_tanh_ready"], 1)

        def vec_diff(dve, c, k, k2, h):
            dve.wait_ge(S[c + "n_ready"], k + 1)
            nc.vector.tensor_tensor(dif[k2][:, :, :], h, cand[k2][:, :, :],
                                    ALU.subtract).then_inc(S[c + "diff_ready"], 1)

        def vec_gate(dve, c, k, k2):
            dve.wait_ge(S[c + "diff_ready"], k + 1)
            nc.vector.tensor_tensor(dif[k2][:, :, :], dif[k2][:, :, :], RZ[k2][:, :, HID:2 * HID],
                                    ALU.mult).then_inc(S[c + "gated_ready"], 1)

        def vec_h(dve, c, k, k2, h_new):
            dve.wait_ge(S[c + "gated_ready"], k + 1)
            nc.vector.tensor_tensor(h_new, dif[k2][:, :, :], cand[k2][:, :, :],
                                    ALU.add).then_inc(S[c + "h_ready"], 1)

        def norm_stage(dve, c, stage, n, inputs, xx, hh, y, sqt, sums, v4):
            if stage == 0:
                inputs()
                nc.vector.tensor_tensor(y, xx, hh, ALU.add).then_inc(S[c + "resid_ready"], 1)
            elif stage == 1:
                dve.wait_ge(S[c + "resid_ready"], n + 1)
                nc.vector.tensor_reduce(sums, y, AX_X, ALU.add).then_inc(S[c + "sum_ready"], 1)
            elif stage == 2:
                dve.wait_ge(S[c + "sum_ready"], n + 1)
                nc.vector.scalar_tensor_tensor(out=y, in0=sums.unsqueeze(2).to_broadcast([P, NU, HID]), scalar=-1.0 / HID, in1=y,
                                               op0=ALU.mult, op1=ALU.add).then_inc(S[c + "center_ready"], 1)
            elif stage == 3:
                dve.wait_ge(S[c + "center_ready"], n + 1)
                nc.vector.tensor_tensor(sqt, y, y, ALU.mult).then_inc(S[c + "square_ready"], 1)
            else:
                dve.wait_ge(S[c + "square_ready"], n + 1)
                nc.vector.tensor_reduce(v4, sqt, AX_X, ALU.add).then_inc(S[c + "var_ready"], 1)

        def newton(dve, c, done, stats, w, parts=(0, 1, 2)):
            s = S[c + "newton_step"]
            starts = (0, 4, 4 + 3 * (NEWTON // 2))
            cnt = [starts[parts[0]]]

            def step(ins):
                ins.then_inc(s, 1)
                cnt[0] += 1
                dve.wait_ge(s, done + cnt[0])

            v, hf, r, a, b = (q[:, 0:w] for q in (var, vhalf, rstd, nt1, nt2))
            if 0 in parts:
                dve.wait_ge(S[c + "var_ready"], stats)
                step(nc.vector.tensor_scalar(v, v, 1.0 / HID, EPS, ALU.mult, ALU.add))
                step(nc.vector.tensor_scalar(hf, v, 0.5, None, ALU.mult))
                step(nc.vector.tensor_scalar(a.bitcast(I32), v.bitcast(I32), 1, None, ALU.logical_shift_right))
                step(nc.vector.tensor_scalar(r.bitcast(I32), a.bitcast(I32), -1.0, float(0x5F3759DF), ALU.mult, ALU.add))
            for part in (1, 2):
                if part in parts:
                    for _ in range(NEWTON // 2):
                        step(nc.vector.tensor_tensor(a, r, r, ALU.mult))
                        step(nc.vector.tensor_tensor(b, a, hf, ALU.mult))
                        step(nc.vector.scalar_tensor_tensor(out=r, in0=b, scalar=1.5, in1=r, op0=ALU.subtract, op1=ALU.mult))

        @block.tensor
        def _(pe):
            pe.wait_ge(S["masks_set"], 2)
            for n, square_in in enumerate(TURNS):
                pe.wait_ge(turn_asked, n + 1)
                for q in range(BLOCKS):
                    mm = nc.tensor.transpose(xt_ps[0][:, q * P:(q + 1) * P], square_in[:, q * P:(q + 1) * P], ident[:, :])
                mm.then_inc(turned, 1)
            pe.wait_ge(S["sorted_"], 1)
            pe.wait_ge(S["masks_set"], 6)
            nc.tensor.matmul(bank_a[:, 0:TILES], shift_t[:, :], target[:, 0:TILES], start=True, stop=False)
            nc.tensor.matmul(bank_a[:, 0:TILES], wrap_t[:, :], target[:, 1:TILES + 1], start=False, stop=True).then_inc(S["shifted"], 1)
            pe.wait_ge(S["ends_set"], 1)
            pe.wait_ge(S["before_set"], 2)
            nc.tensor.matmul(bank_b[:, 0:TILES], before_t[:, :], run_end[:, :], start=True, stop=True).then_inc(S["ranked"], 1)

            pe.wait_ge(S["weights_loaded"], 16 * WEIGHT_DMAS)
            pe.wait_ge(S["zero_set"], 5)
            pe.wait_ge(S["bias_set"], 1)

            def turn_x(i, j, par, uses):
                if j == 0:
                    pe.wait_ge(S[f"x_loaded{par}"], (uses + 1) * (16 * JT))
                if not (is_first(i) and j == 0):
                    pe.wait_ge(S["x_turn_copied"], i * JT + j)
                for a in range(2):
                    mm = nc.tensor.transpose(xt_ps[1][:, a * P:(a + 1) * P],
                                             x_t[par][j][:, 2 * a:2 * a + 2, :].rearrange("p u f -> p (u f)"), ident[:, :])
                mm.then_inc(S["x_turned"], 1)

            def turn_back(i, k):
                kk_ = i * UNITS + k
                pe.wait_ge(S["h_ready"], kk_ + 1)
                if not (is_first(i) and k == 0):
                    pe.wait_ge(S["rows_ready"], kk_)
                for a in range(2):
                    mm = nc.tensor.transpose(xt_ps[0][:, a * P:(a + 1) * P], h_turn[k % JT][:, a * P:(a + 1) * P], ident[:, :])
                mm.then_inc(S["back_turned"], 1)

            def gate_unit(i, k):
                kk_ = i * UNITS + k
                k2, j = k % 2, k % JT
                if not (is_first(i) and k < 2):
                    pe.wait_ge(S["pre_tanh_ready"], kk_ - 1)
                    pe.wait_ge(S["z_ready"], kk_ - 1)
                if k < JT:
                    pe.wait_ge(S["x_turn_copied"], i * JT + j + 1)
                else:
                    pe.wait_ge(S["h_ready"], kk_ - JT + 1)
                h = x_turn[j] if k < JT else h_turn[j]
                for g in range(3):
                    mm = nc.tensor.matmul(dense_gate(k2, g), gate_pair[:, g * P:(g + 1) * P], h, start=True, stop=True)
                mm.then_inc(S["gates_ready"], 1)

            def mlp(i, par, uses, half, stage):
                n = i * 2 + half
                if stage == 0:
                    if half == 0:
                        pe.wait_ge(S[f"rows_got{par}"], (uses + 1) * (16 * GT))
                    if not (is_first(i) and half == 0):
                        pe.wait_ge(S["base_copied"], n)
                    for u in range(4):
                        mm = nc.tensor.transpose(bank_a[0:ED, u * P:(u + 1) * P], rows_g[par][:, 4 * half + u, 0:ED], ident[:, :])
                    mm.then_inc(S["attr_turned"], 1)
                elif stage == 1:
                    pe.wait_ge(S["attr_t_copied"], n + 1)
                    nc.tensor.matmul(bank_b[0:HID, :], w1_t[:, :], attr_t[0:ED, :], start=True, stop=True).then_inc(S["hidden_summed"], 1)
                else:
                    pe.wait_ge(S["hidden_ready"], n + 1)
                    for u in range(4):
                        mm = nc.tensor.matmul(bank_a[:, u * HID:(u + 1) * HID], hidden[0:HID + 1, u * P:(u + 1) * P], w2_b[:, :],
                                              start=True, stop=True)
                    mm.then_inc(S["base_summed"], 1)

            def dense(i, par, uses):
                for k in range(UNITS):
                    gate_unit(i, k)
                    if k >= BACK_LAG:
                        turn_back(i, k - BACK_LAG)
                    elif not is_first(i):
                        turn_back(i - 1, k - BACK_LAG + UNITS)
                    if k in X_TICKS and not is_end(i, ITERS):
                        turn_x(i + 1, X_TICKS[k], 1 - par, uses if par == 0 else uses + 1)
                    if k in MLP_TICKS:
                        half, stage = MLP_TICKS[k]
                        mlp(i, par, uses, half, stage)

            for j in range(JT):
                turn_x(0, j, 0, 0)
            run_iterations(pe, dense, ITERS)
            for k in range(UNITS - BACK_LAG, UNITS):
                turn_back(ITERS - 1, k)

            pe.wait_ge(S["base_copied"], 2 * GROUPS)
            pe.wait_ge(S["rows_ready"], ITERS * UNITS)

            for t in range(STEPS):
                def bcast(g, par, half, t=t):
                    gg = g + t * GROUPS
                    if half == 0:
                        pe.wait_ge(S["rank_copied"], gg + 1)
                    if not (t == 0 and is_first(g) and half == 0):
                        pe.wait_ge(S["same_ready"], gg * 2 + half)
                    for u in range(4):
                        col = rank_g[par][:, 4 * half + u:4 * half + u + 1].to_broadcast([P, P])
                        mm = nc.tensor.matmul(bank_b[:, u * P:(u + 1) * P], col, ident_bf[:, :], start=True, stop=True)
                    mm.then_inc(S["bcast_ready"], 1)

                def turn_slots(g, par, uses, b, t=t):
                    gg = g + t * GROUPS
                    n = gg * 2 + b
                    if b == 0:
                        pe.wait_ge(S[f"xc_loaded{par}"], (uses + t * (25 if par == 0 else 24) + 1) * 16)
                    pe.wait_ge(S["agg_copied"], gg * GT + 4 * b + 4)
                    if not (t == 0 and is_first(g)):
                        pe.wait_ge(S["c_xt_copied"], n - 1)
                    for u in range(4):
                        mm = nc.tensor.transpose(xt_ps[b][:, u * P:(u + 1) * P], xc[par][:, 4 * b + u, :], ident[:, :])
                    mm.then_inc(S["c_xt_ready"], 1)

                def gate_bias(g, b, t=t):
                    n = (g + t * GROUPS) * 2 + b
                    if not (t == 0 and is_first(g)):
                        pe.wait_ge(S["c_pre_tanh_ready"], n - 1)
                    gate_matmuls_bias(b)

                def gate_part(g, b, u, t=t):
                    if u == 0:
                        pe.wait_ge(S["c_xt_copied"], (g + t * GROUPS) * 2 + b + 1)
                    mm = nc.tensor.matmul(gates[b][:, u, :], xt[b][:, u * P:(u + 1) * P], gate_w[:, :],
                                          start=False, stop=(u == 3), skip_group_check=True)
                    if u == 3:
                        mm.then_inc(S["c_gates_ready"], 1)

                def slots(g, par, uses, t=t):
                    gg = g + t * GROUPS
                    prev = not is_first(g)
                    if prev:
                        pu = uses if par == 1 else uses - 1
                        turn_slots(g - 1, 1 - par, pu, 0)
                    for u in range(GT):
                        if u % 4 == 0:
                            pe.wait_ge(S["same_ready"], gg * 2 + u // 4 + 1)
                            if prev:
                                gate_bias(g - 1, u // 4)
                        if u == 0:
                            pe.wait_ge(S["msg_ready"], gg + 1)
                        first = not prev and u == 0
                        if not (first and t == 0):
                            pe.wait_ge(S["agg_copied"], gg * GT + u)
                        mm = nc.tensor.matmul(bank_a[:, u * HID:(u + 1) * HID], same[u // 4][:, u % 4, :], msg[par][:, u, :],
                                              start=True, stop=first)
                        if not first:
                            carry = xc[par][:, u - 1, 0:HID] if u else xc[1 - par][:, GT - 1, 0:HID]
                            mm = nc.tensor.matmul(bank_a[:, u * HID:(u + 1) * HID], same_prev[u // 4][:, u % 4, :], carry,
                                                  start=False, stop=True)
                        mm.then_inc(S["agg_summed"], 1)
                        if prev and u == 1:
                            turn_slots(g - 1, 1 - par, pu, 1)
                        if prev:
                            gate_part(g - 1, u // 4, u % 4)
                        if u == 0:
                            bcast(g, par, 1)
                        if u == 4 and not is_end(g, GROUPS):
                            bcast(g + 1, 1 - par, 0)

                bcast(0, 0, 0)
                run_groups(pe, slots)
                for b in range(2):
                    turn_slots(GROUPS - 1, 0, 24, b)
                for b in range(2):
                    gate_bias(GROUPS - 1, b)
                    for u in range(4):
                        gate_part(GROUPS - 1, b, u)

        @block.scalar
        def _(act):
            act.wait_ge(S["attr_loaded"], 16)
            nc.scalar.copy(edge_stage[:, :, 0:ED], attr_stage.rearrange("p (r d) -> p r d", d=ED)).then_inc(S["rows_made"], 1)
            act.wait_ge(S["weights_loaded"], 16 * WEIGHT_DMAS)
            act.wait_ge(S["columns_set"], 3)

            def copy_x(i, j):
                act.wait_ge(S["x_turned"], i * JT + j + 1)
                if not is_first(i):
                    act.wait_ge(S["diff_ready"], (i - 1) * UNITS + j + 1)
                nc.scalar.copy(x_turn[j], xt_ps[1][:, 0:TW]).then_inc(S["x_turn_copied"], 1)

            def copy_back(i, k):
                j, t = k % JT, k // JT
                act.wait_ge(S["back_turned"], i * UNITS + k + 1)
                if t == 0 and not is_first(i):
                    act.wait_ge(h_stored[j][0], i * 32)
                if t == 1 and not is_first(i):
                    act.wait_ge(S["resid_ready"], (i - 1) * JT + j + 1)
                if t == 2:
                    act.wait_ge(h_stored[j][0], i * 32 + 16)
                if t == 3:
                    act.wait_ge(h_stored[j][1], i * 16 + 16)
                nc.scalar.copy(h_t[j][t % 2].rearrange("p u f -> p (u f)"), xt_ps[0][:, 0:TW]).then_inc(S["rows_ready"], 1)

            def dense_sigmoid(i, k, g):
                kk_, k2 = i * UNITS + k, k % 2
                if g == 0:
                    act.wait_ge(S["gates_ready"], kk_ + 1)
                    if not (is_first(i) and k < 2):
                        act.wait_ge(S["pre_tanh_ready"], kk_ - 1)
                elif not (is_first(i) and k < 2):
                    act.wait_ge(S["gated_ready"], kk_ - 1)
                nc.scalar.activation(flat(RZ[k2])[:, g * TW:(g + 1) * TW], dense_gate(k2, g), ACT.Sigmoid,
                                     bias=b_rz[:, g:g + 1]).then_inc(S["r_ready" if g == 0 else "z_ready"], 1)

            def dense_tanh(kk_, k2, first):
                act.wait_ge(S["pre_tanh_ready"], kk_ + 1)
                if not first:
                    act.wait_ge(S["h_ready"], kk_ - 1)
                nc.scalar.activation(flat(cand[k2]), flat(pre[k2]), ACT.Tanh, bias=bi_col[:, 2:3]).then_inc(S["n_ready"], 1)

            def mlp(i, half, stage):
                n = i * 2 + half
                if stage == 0:
                    act.wait_ge(S["attr_turned"], n + 1)
                    if not (is_first(i) and half == 0):
                        act.wait_ge(S["hidden_summed"], n)
                    nc.scalar.copy(attr_t[0:ED, :], bank_a[0:ED, :]).then_inc(S["attr_t_copied"], 1)
                elif stage == 1:
                    act.wait_ge(S["hidden_summed"], n + 1)
                    if not (is_first(i) and half == 0):
                        act.wait_ge(S["base_summed"], n)
                    nc.scalar.activation(hidden[0:HID, :], bank_b[0:HID, :], ACT.Relu, bias=b1_col[:, :]).then_inc(S["hidden_ready"], 1)
                else:
                    act.wait_ge(S["base_summed"], n + 1)
                    nc.scalar.copy(msg_base[:, bass.ds(i * (GT * HID) + half * 4 * HID, 4 * HID)],
                                   bank_a[:, 0:4 * HID]).then_inc(S["base_copied"], 1)

            def dense(i, par, uses):
                for k in range(UNITS):
                    dense_sigmoid(i, k, 0)
                    if not (is_first(i) and k == 0):
                        dense_tanh(i * UNITS + k - 1, (k - 1) % 2, is_first(i) and k < 3)
                    dense_sigmoid(i, k, 1)
                    if k >= BACK_LAG:
                        copy_back(i, k - BACK_LAG)
                    elif not is_first(i):
                        copy_back(i - 1, k - BACK_LAG + UNITS)
                    if k in X_TICKS and not is_end(i, ITERS):
                        copy_x(i + 1, X_TICKS[k])
                    if k in MLP_TICKS:
                        half, stage = MLP_TICKS[k]
                        mlp(i, half, stage)

            act.wait_ge(S["rows_stored"], 16)
            act.wait_ge(S["bias_set"], 1)
            for j in range(JT):
                copy_x(0, j)
            run_iterations(act, dense, ITERS)
            dense_tanh(ITERS * UNITS - 1, 1, False)
            for k in range(UNITS - BACK_LAG, UNITS):
                copy_back(ITERS - 1, k)
            for q in ("xj_stored", "xi_stored"):
                act.wait_ge(S[q + "0"], 16 * 25)
                act.wait_ge(S[q + "1"], 16 * 24)
            act.wait_ge(S["src_saved"], GROUPS)
            for j in range(JT):
                act.wait_ge(h_stored[j][0], 16 * 2 * ITERS)
                act.wait_ge(h_stored[j][1], 16 * ITERS)
                act.wait_ge(y_stored[j], 16 * ITERS)
            act.wait_ge(S["base_summed"], 2 * GROUPS)

            for t in range(STEPS):
                def copy_agg(g, par, u, t=t):
                    gg = g + t * GROUPS
                    act.wait_ge(S["agg_summed"], gg * GT + u + 1)
                    if u == 0 and not (t == 0 and isinstance(g, int) and g < 2):
                        act.wait_ge(S["c_xt_ready"], gg * 2 - 2)
                    nc.scalar.copy(xc[par][:, u, 0:HID], bank_a[:, u * HID:(u + 1) * HID]).then_inc(S["agg_copied"], 1)

                def copy_xt_c(g, b, t=t):
                    n = (g + t * GROUPS) * 2 + b
                    act.wait_ge(S["c_xt_ready"], n + 1)
                    if not (t == 0 and is_first(g)):
                        act.wait_ge(S["c_gates_ready"], n - 1)
                    nc.scalar.copy(xt[b][:, :], xt_ps[b][:, :]).then_inc(S["c_xt_copied"], 1)

                def slots(g, par, uses, t=t):
                    prev = not is_first(g)
                    prev2 = not (isinstance(g, int) and g < 2)
                    k = (g + (t * GROUPS - 1)) * 2
                    if prev:
                        copy_xt_c(g - 1, 0)
                    for u in range(GT):
                        copy_agg(g, par, u)
                        if prev2 and u == 0:
                            sigmoid_unit(act, "c_", k - 1, 1)
                        if prev and u == 1:
                            copy_xt_c(g - 1, 1)
                        if prev2 and u == 3:
                            tanh_unit(act, "c_", k - 1, 1)
                        if prev and u == 4:
                            sigmoid_unit(act, "c_", k, 0)
                        if prev and u == 6:
                            tanh_unit(act, "c_", k, 0)

                run_groups(act, slots)
                k = (t * GROUPS + GROUPS - 1) * 2
                copy_xt_c(GROUPS - 1, 0)
                sigmoid_unit(act, "c_", k - 1, 1)
                copy_xt_c(GROUPS - 1, 1)
                tanh_unit(act, "c_", k - 1, 1)
                for b in range(2):
                    sigmoid_unit(act, "c_", k + b, b)
                    tanh_unit(act, "c_", k + b, b)

        @block.vector
        def _(dve):
            sstep = [0]

            def step(ins):
                ins.then_inc(S["sort_step"], 1)
                sstep[0] += 1
                dve.wait_ge(S["sort_step"], sstep[0])

            TT = nc.vector.tensor_tensor
            TS = nc.vector.tensor_scalar
            dve.wait_ge(S["keys_loaded"], 16)
            dve.wait_ge(S["masks_set"], 11)
            cur, oth = kk[0], kk[1]
            step(TS(key_i[:, :], key_i[:, :], float(KEY_SHIFT), None, ALU.add))
            step(TS(key_i[:, :], key_i[:, :], LOCAL_BITS, None, ALU.logical_shift_left))
            step(TT(cur[:, :].bitcast(I32), key_i[:, :], local_e[:, :], ALU.bitwise_or))
            for b in range(7):
                step(TS(p_bit[:, b:b + 1], p_col[:, b:b + 1], b, 1, ALU.logical_shift_right, ALU.bitwise_and))
            step(TS(sign[:, 0:7], p_bit[:, 0:7], -2.0, 1.0, ALU.mult, ALU.add))

            def free_bit(lay, b):
                if lay == "N":
                    return b - 7
                return b if b < 7 else (b - 7 if b >= 14 else None)

            def halves(tile, lay, m, l):
                fl = free_bit(lay, l)
                fm = free_bit(lay, m) if m < 16 else None
                w = tile.shape[1]
                if fm is None:
                    v = tile[:, :].rearrange("p (h t l) -> p t h l", t=2, l=1 << fl)
                    return [(v[:, 0], v[:, 1], False)]
                v = tile[:, :].rearrange("p (h d m t l) -> p d t h m l", d=2, t=2, l=1 << fl, m=1 << (fm - fl - 1))
                return [(v[:, d, 0], v[:, d, 1], d == 1) for d in range(2)]

            def pair_view(tile, lay, m, l):
                fl = free_bit(lay, l)
                fm = free_bit(lay, m) if m < 16 else None
                if fm is None:
                    return [tile[:, :].rearrange("p (h l) -> p h l", l=1 << fl)]
                v = tile[:, :].rearrange("p (h d m l) -> p d h m l", d=2, l=1 << fl, m=1 << (fm - fl - 1))
                return [v[:, 0], v[:, 1]]

            lay = "T"
            cp, op = pp[0], pp[1]
            nturn = [0]

            def turn(tile, dest):
                assert tile is TURNS[nturn[0]]
                dve.sem_inc(turn_asked, 1)
                nturn[0] += 1
                dve.wait_ge(turned, nturn[0])
                step(nc.vector.tensor_copy(dest[:, :], xt_ps[0][:, :]))

            todo = phases()
            for n, (L, m, ls) in enumerate(todo):
                payload = m >= 15
                if L != lay:
                    turn(cur, oth)
                    cur, oth = oth, cur
                    if payload:
                        turn(cp, op)
                        cp, op = op, cp
                    lay = L
                flip = L == "T" and 7 <= m <= 13
                if flip:
                    step(TS(oth[:, :], cur[:, :], sign[:, m - 7:m - 6], None, ALU.mult))
                    cur, oth = oth, cur
                for l in ls:
                    c2, o2 = halves(cur, L, m, l), halves(oth, L, m, l)
                    if payload:
                        sw = pair_view(swap, L, m, l)
                        for (a, b, desc), s_ in zip(c2, sw):
                            TT(s_, a, b, ALU.is_lt if desc else ALU.is_gt)
                        pa, pb = halves(cp, L, 16, l)[0][0:2]
                        qa, qb = halves(op, L, 16, l)[0][0:2]
                        dl = pair_view(delta, L, 16, l)[0]
                        sf = pair_view(swap, L, 16, l)[0]
                        step(TT(dl, pb, pa, ALU.subtract))
                        ins = TT(dl, dl, sf, ALU.mult)
                        ins.then_inc(S["sort_step"], 1)
                        sstep[0] += 1
                    for n2, ((a, b, desc), (oa, ob, _)) in enumerate(zip(c2, o2)):
                        TT(oa, a, b, ALU.max if desc else ALU.min)
                        ins = TT(ob, a, b, ALU.min if desc else ALU.max)
                    step(ins)
                    cur, oth = oth, cur
                    if payload:
                        TT(qa, pa, dl, ALU.add)
                        step(TT(qb, pb, dl, ALU.subtract))
                        cp, op = op, cp
                if flip:
                    step(TS(oth[:, :], cur[:, :], sign[:, m - 7:m - 6], None, ALU.mult))
                    cur, oth = oth, cur
                if L == "T" and m == 14:
                    step(TS(key_i[:, :], cur[:, :].bitcast(I32), (1 << LOCAL_BITS) - 1, None, ALU.bitwise_and))
                    step(TT(cp[:, :], key_i[:, :], block_e[:, :], ALU.add))
                    step(TS(key_i[:, :], cur[:, :].bitcast(I32), LOCAL_BITS, None, ALU.logical_shift_right))
                    step(TS(oth[:, :], key_i[:, :], -float(KEY_SHIFT), None, ALU.add))
                    cur, oth = oth, cur
            turn(cur, oth)
            cur, oth = oth, cur
            turn(cp, op)
            cp, op = op, cp
            nc.vector.tensor_copy(target[:, :], cur[:, 0:TILES + 1]).then_inc(S["sorted_"], 1)
            dve.wait_ge(S["sorted_"], 1)
            TS(edge_idx[:, :], cp[:, 0:TILES], float(E - 1), None, ALU.min).then_inc(S["columns_set"], 1)
            TS(target_idx[:, :], target[:, 0:TILES], float(N - 1), None, ALU.min).then_inc(S["columns_set"], 1)
            dve.wait_ge(S["shifted"], 1)
            step(TT(run_on[:, :], target[:, 0:TILES], bank_a[:, 0:TILES], ALU.is_equal))
            TS(run_end[:, :], run_on[:, :], -1.0, 1.0, ALU.mult, ALU.add).then_inc(S["ends_set"], 1)
            nc.vector.scalar_tensor_tensor(out=rep_idx[:, :], in0=run_on[:, :], scalar=float(1 << 20), in1=target[:, 0:TILES],
                                           op0=ALU.mult, op1=ALU.add).then_inc(S["columns_set"], 1)
            nc.vector.memset(prev_run[:, 0:1], -1.0)
            TS(prev_run[:, 1:TILES], run_on[:, 0:TILES - 1], is_last_p[:, :], -1.0, ALU.mult, ALU.add).then_inc(S["ranks_set"], 1)
            dve.wait_ge(S["ranked"], 1)
            nc.vector.tensor_copy(rank[:, :], bank_b[:, 0:TILES]).then_inc(S["ranks_set"], 1)
            nc.vector.tensor_copy(ident_bf[:, :], ident[:, :]).then_inc(S["ranks_set"], 1)
            dve.wait_ge(S["ranks_set"], 3)
            dve.wait_ge(S["weights_loaded"], 16 * WEIGHT_DMAS)
            dve.wait_ge(S["zero_set"], 5)
            TT(b_rz[:, :], bi_col[:, 0:2], bh_col[:, 0:2], ALU.add)
            TT(b3[:, 0:2 * HID], bi3[:, 0:2 * HID], bh3[:, 0:2 * HID], ALU.add)
            nc.vector.tensor_copy(b3[:, 2 * HID:3 * HID], bh3[:, 2 * HID:3 * HID])
            step(nc.vector.tensor_copy(b3[:, 3 * HID:4 * HID], bi3[:, 2 * HID:3 * HID]))
            step(nc.vector.tensor_copy(bias_part[:, 0, :], b3[:, :]))
            step(TT(bias_rest[:, :], b3[:, :], bias_part[:, 0, :], ALU.subtract))
            step(nc.vector.tensor_copy(bias_part[:, 1, :], bias_rest[:, :]))
            step(TT(b3[:, :], bias_rest[:, :], bias_part[:, 1, :], ALU.subtract))
            step(nc.vector.tensor_copy(bias_part[:, 2, :], b3[:, :]))
            step(TS(bias_acc[:, :], bias_part[:, 0, :], ident[0:3, 0:1], None, ALU.mult))
            step(nc.vector.scalar_tensor_tensor(out=bias_acc[:, :], in0=bias_part[:, 1, :], scalar=ident[0:3, 1:2],
                                                in1=bias_acc[:, :], op0=ALU.mult, op1=ALU.add))
            for hlf in range(2):
                ins = nc.vector.scalar_tensor_tensor(out=bias_rows[0:3, 4 * HID * hlf:4 * HID * (hlf + 1)], in0=bias_part[:, 2, :],
                                                     scalar=ident[0:3, 2:3], in1=bias_acc[:, :], op0=ALU.mult, op1=ALU.add)
            dve.wait_ge(S["rows_stored"], 16)
            nc.vector.memset(hidden[HID:HID + 1, :], 1.0).then_inc(S["bias_set"], 1)

            def finish(i, j, par, stage):
                def inputs():
                    dve.wait_ge(S["rows_ready"], i * UNITS + 3 * JT + j + 1)
                    if not is_first(i):
                        dve.wait_ge(y_stored[j], i * 16)
                norm_stage(dve, "", stage, i * JT + j, inputs, x_t[par][j], h_t[j][1], y_t[j], sq,
                           ln_sum[:, 0:NU], var[:, NU * j:NU * j + NU])

            def pre_tanh(i, k):
                kk_, k2 = i * UNITS + k, k % 2
                dve.wait_ge(S["r_ready"], kk_ + 1)
                if not (is_first(i) and k < 2):
                    dve.wait_ge(S["n_ready"], kk_ - 1)
                nc.vector.scalar_tensor_tensor(out=flat(pre[k2]), in0=dense_gate(k2, 2), scalar=bh_col[:, 2:3], in1=flat(RZ[k2])[:, 0:TW],
                                               op0=ALU.add, op1=ALU.mult).then_inc(S["pre_tanh_ready"], 1)

            def diff_unit(i, k):
                kk_, k2, j = i * UNITS + k, k % 2, k % JT
                h = x_turn[j] if k < JT else h_turn[j]
                dve.wait_ge(S["n_ready"], kk_ + 1)
                nc.vector.tensor_tensor(flat(dif[k2]), h, flat(cand[k2]), ALU.subtract).then_inc(S["diff_ready"], 1)

            def gate_diff(i, k):
                kk_, k2 = i * UNITS + k, k % 2
                dve.wait_ge(S["diff_ready"], kk_ + 1)
                dve.wait_ge(S["z_ready"], kk_ + 1)
                nc.vector.tensor_tensor(flat(dif[k2]), flat(dif[k2]), flat(RZ[k2])[:, TW:2 * TW], ALU.mult).then_inc(S["gated_ready"], 1)

            def add_unit(i, k):
                kk_, k2 = i * UNITS + k, k % 2
                dve.wait_ge(S["gated_ready"], kk_ + 1)
                nc.vector.tensor_tensor(h_turn[k % JT], flat(dif[k2]), flat(cand[k2]), ALU.add).then_inc(S["h_ready"], 1)

            def lagged(stage, i, k, lag):
                if k >= lag:
                    stage(i, k - lag)
                elif not is_first(i):
                    stage(i - 1, k - lag + UNITS)

            def dense(i, par, uses):
                for k in range(UNITS):
                    norms = () if is_first(i) else NORM_TICKS.get(k, ())
                    pre_tanh(i, k)
                    lagged(diff_unit, i, k, 1)
                    lagged(add_unit, i, k, 2)
                    for j, stage in norms[0:1]:
                        finish(i - 1, j, 1 - par, stage)
                    lagged(gate_diff, i, k, 1)
                    for j, stage in norms[1:]:
                        finish(i - 1, j, 1 - par, stage)
                    if not is_first(i):
                        if k in NEWTON_TICKS:
                            newton(dve, "", (i - 1) * NEWTON_OPS, i * JT, 16, (NEWTON_TICKS[k],))
                        for j in SCALE_TICKS.get(k, ()):
                            scale_y(i - 1, j)
                    if k == 14:
                        dve.wait_ge(S[f"rows_got{par}"], (uses + 1) * (16 * GT))
                        nc.vector.tensor_copy(src_node[:, bass.ds(i * GT, GT)],
                                              rows_g[par][:, :, ED:ROW].bitcast(I32).rearrange("p u o -> p (u o)")).then_inc(S["src_saved"], 1)

            def scale_y(i, j):
                nc.vector.tensor_tensor(y_t[j], y_t[j], rstd[:, NU * j:NU * j + NU].unsqueeze(2).to_broadcast([P, NU, HID]),
                                        ALU.mult).then_inc(S["y_ready"], 1)

            run_iterations(dve, dense, ITERS)
            diff_unit(ITERS - 1, UNITS - 1)
            add_unit(ITERS - 1, UNITS - 2)
            gate_diff(ITERS - 1, UNITS - 1)
            add_unit(ITERS - 1, UNITS - 1)
            for j in range(JT):
                for stage in range(5):
                    finish(ITERS - 1, j, 0, stage)
            newton(dve, "", (ITERS - 1) * NEWTON_OPS, ITERS * JT, 16)
            for j in range(JT):
                scale_y(ITERS - 1, j)

            for j in range(JT):
                dve.wait_ge(h_stored[j][0], 16 * 2 * ITERS)
                dve.wait_ge(h_stored[j][1], 16 * ITERS)
                dve.wait_ge(y_stored[j], 16 * ITERS)
            dve.wait_ge(S["xj_stored0"], 16 * 25)
            dve.wait_ge(S["xj_stored1"], 16 * 24)
            dve.wait_ge(S["xi_stored0"], 16 * 25)
            dve.wait_ge(S["xi_stored1"], 16 * 24)
            dve.wait_ge(S["base_copied"], 2 * GROUPS)
            for t in range(STEPS):
                def copy_ranks(g, par, t=t):
                    gg = g + t * GROUPS
                    if not (t == 0 and isinstance(g, int) and g < 2):
                        dve.wait_ge(S["bcast_ready"], gg * 2 - 2)
                    nc.vector.tensor_copy(rank_g[par], rank[:, bass.ds(g * GT, GT)]).then_inc(S["rank_copied"], 1)

                def make_same(g, half, t=t):
                    gg = g + t * GROUPS
                    dve.wait_ge(S["bcast_ready"], gg * 2 + half + 1)
                    if not (t == 0 and is_first(g)):
                        dve.wait_ge(S["agg_summed"], gg * GT - GT + 4 * half + 4)
                    rows = bank_b[:, :].rearrange("p (u s) -> p u s", u=4)
                    for o, cols in ((same[half], rank), (same_prev[half], prev_run)):
                        c = cols[:, bass.ds(g * GT + 4 * half, 4)].unsqueeze(2).to_broadcast([P, 4, P])
                        ins = nc.vector.tensor_tensor(o, rows, c, ALU.is_equal)
                    ins.then_inc(S["same_ready"], 1)

                def make_msg(g, par, uses, t=t):
                    gg = g + t * GROUPS
                    if t == 0:
                        dve.wait_ge(S[f"g_loaded{par}"], (uses + 1) * 16)
                    else:
                        dve.wait_ge(S[f"g_got{par}"], (uses + (t - 1) * (25 if par == 0 else 24) + 1) * (16 * GT))
                    if not (t == 0 and isinstance(g, int) and g < 2):
                        dve.wait_ge(S["agg_summed"], gg * GT - GT)
                    nc.vector.tensor_tensor(msg[par].rearrange("p u f -> p (u f)"), g_c[par].rearrange("p u f -> p (u f)"),
                                            msg_base[:, bass.ds(g * (GT * HID), GT * HID)], ALU.mult).then_inc(S["msg_ready"], 1)

                def unit(g, par, uses, b, t=t):
                    n = (g + t * GROUPS) * 2 + b
                    hb = h_c[par][:, 4 * b:4 * b + 4, :]
                    vec_r_hn(dve, "c_", n, b)
                    vec_pre(dve, "c_", n, b)

                def unit_end(g, par, uses, b, t=t):
                    n = (g + t * GROUPS) * 2 + b
                    hb = h_c[par][:, 4 * b:4 * b + 4, :]
                    vec_diff(dve, "c_", n, b, xc[par][:, 4 * b:4 * b + 4, HID:2 * HID])
                    vec_gate(dve, "c_", n, b)
                    if b == 0 and not (t == 0 and isinstance(g, int) and g < 2) and t < STEPS - 1:
                        dve.wait_ge(S[f"hc_stored{par}"], (uses + t * (25 if par == 0 else 24)) * 16)
                    vec_h(dve, "c_", n, b, hb)
                    if t == STEPS - 1:
                        if b == 0:
                            dve.wait_ge(S[f"xi_loaded{par}"], (uses + 1) * 16)
                            if not (isinstance(g, int) and g < 2):
                                dve.wait_ge(S[f"y_put{par}"], uses * (16 * GT))
                        yb = y_c[par][:, 4 * b:4 * b + 4, :]
                        for stage in range(5):
                            norm_stage(dve, "c_", stage, g * 2 + b, lambda: dve.wait_ge(S["c_h_ready"], n + 1),
                                       xi_c[par][:, 4 * b:4 * b + 4, :], hb, yb, sq_c, ln_sum_c[:, 0:NU], var[:, NU * b:NU * b + NU])
                        if b == 1:
                            newton(dve, "c_", g * NEWTON_OPS, g * 2 + 2, 8)
                            for c in range(2):
                                yc = y_c[par][:, 4 * c:4 * c + 4, :]
                                nc.vector.tensor_tensor(yc, yc, rstd[:, NU * c:NU * c + NU].unsqueeze(2).to_broadcast([P, NU, HID]),
                                                        ALU.mult).then_inc(S["c_y_ready"], 1)

                def slots(g, par, uses, t=t):
                    prev = not is_first(g)
                    prev2 = not (isinstance(g, int) and g < 2)
                    pu = uses if par == 1 else uses - 1
                    if prev2:
                        unit(g - 2, par, uses - 1, 1)
                    make_same(g, 1)
                    if not is_end(g, GROUPS):
                        copy_ranks(g + 1, 1 - par)
                    if prev2:
                        unit_end(g - 2, par, uses - 1, 1)
                    if not is_end(g, GROUPS):
                        make_same(g + 1, 0)
                    if prev:
                        unit(g - 1, 1 - par, pu, 0)
                    if not is_end(g, GROUPS):
                        make_msg(g + 1, 1 - par, uses if par == 0 else uses + 1)
                    if prev:
                        unit_end(g - 1, 1 - par, pu, 0)

                copy_ranks(0, 0)
                make_same(0, 0)
                make_msg(0, 0, 0)
                run_groups(dve, slots)
                unit(GROUPS - 2, 1, 23, 1)
                unit_end(GROUPS - 2, 1, 23, 1)
                for b in range(2):
                    unit(GROUPS - 1, 0, 24, b)
                    unit_end(GROUPS - 1, 0, 24, b)


def kernel(**inputs):
    import numpy as np
    import concourse.bacc as bacc
    from concourse.bass_utils import run_bass_kernel_spmd

    nc = bacc.Bacc("TRN2", target_bir_lowering=False, num_devices=1)
    g = {k: np.asarray(v) for k, v in inputs.items()}
    arrays = {
        "x": g["x"], "src": g["src"], "dst": g["dst"], "attr": g["edge_attr_32"],
        "w1t": g["L0_gnn_W1"].T, "b1": g["L0_gnn_b1"], "w2t": g["L0_gnn_W2"].T, "b2": g["L0_gnn_b2"],
        "wit": g["L0_gnn_W_ih"].T, "bih": g["L0_gnn_b_ih"], "wht": g["L0_gnn_W_hh"].T, "bhh": g["L0_gnn_b_hh"],
    }
    arrays = {k + "_dram": np.ascontiguousarray(v) for k, v in arrays.items()}
    args = [nc.dram_tensor(k, v.shape, mybir.dt.from_np(v.dtype), kind="ExternalInput").ap() for k, v in arrays.items()]
    out = nc.dram_tensor("out_0_dram", (N, HID), F32, kind="ExternalOutput").ap()
    gnn_program(nc, *args, out)
    r = run_bass_kernel_spmd(nc, [arrays], core_ids=[0])
    return r.results[0]["out_0_dram"]
```

```python
from contextlib import ExitStack

import concourse.bass as bass
from concourse import mybir

ALU = mybir.AluOpType
ACT = mybir.ActivationFunctionType
F32 = mybir.dt.float32
BF16 = mybir.dt.bfloat16
I32 = mybir.dt.int32
AX_X = mybir.AxisListType.X

P = 128
N = 100000
E = 50000
HID = 64
ED = 32
STEPS = 4
EPS = 1e-5

SORT_COLS = 512
BLOCKS = 4
BLOCK_E = E // BLOCKS
LOAD_P = 125
LOAD_F = BLOCK_E // LOAD_P
LOCAL_BITS = 14
KEY_SHIFT = 512
PAD_KEY = N + 351

GT = 8
GROUPS = (E + GT * P - 1) // (GT * P)
TILES = GROUPS * GT
SLOTS = TILES * P
ROW = ED + 1

NU = 4
NODE_TILE = P * NU
NODE_TILES = (N + NODE_TILE - 1) // NODE_TILE
JT = 4
ITERS = NODE_TILES // JT
UNITS = JT * STEPS
LAST_BASE = N - NODE_TILE
LAST_NEW_P = (NODE_TILES * NODE_TILE - N) // NU
MAP_COLS = (N + P - 1) // P
assert NODE_TILES == ITERS * JT and ITERS == GROUPS and ITERS % 2 == 1
NEWTON = 3
NEWTON_OPS = 4 + 3 * NEWTON


def gnn_program(nc, x, src, dst, attr, w1t, b1, w2t, b2, wit, bih, wht, bhh, out):
    edge_rows = nc.dram_tensor("edge_rows", (E, ROW), F32, kind="Internal").ap()
    row_map = nc.dram_tensor("row_map", (P * MAP_COLS, 1), I32, kind="Internal").ap()
    table = [None] + [nc.dram_tensor(f"table{t}", (N + SLOTS, HID), F32, kind="Internal").ap() for t in range(1, STEPS)]
    slot_x = nc.dram_tensor("slot_x", (SLOTS, HID), F32, kind="Internal").ap()
    slot_src = nc.dram_tensor("slot_src", (SLOTS, HID), F32, kind="Internal").ap()

    def slot_rows(ap, g):
        return ap.rearrange("(g p u) f -> g p (u f)", p=P, u=GT)[bass.ds(g, 1), :, :].rearrange("o p f -> (o p) f")

    slot_table = [slot_x] + [table[t][N:N + SLOTS, :] for t in range(1, STEPS)]

    def node_rows(ap, tile):
        full = ap[0:(NODE_TILES - 1) * NODE_TILE, :].rearrange("(t p u) f -> t p (u f)", p=P, u=NU)
        return full[bass.ds(tile, 1), :, :].rearrange("o p f -> (o p) f")

    with ExitStack() as ctx:
        def sb(name, shape, dt=F32):
            return ctx.enter_context(nc.sbuf_tensor(name, list(shape), dt))

        def ps(name, shape):
            return ctx.enter_context(nc.psum_tensor(name, list(shape), F32))

        def sem(name):
            return ctx.enter_context(nc.semaphore(name))

        ident = sb("ident", [P, P])
        shift_t = sb("shift_t", [P, P])
        wrap_t = sb("wrap_t", [P, P])
        before_t = sb("before_t", [P, P])
        center_pair = sb("center_pair", [P, P])
        ident_bf = sb("ident_bf", [P, P], BF16)
        reverse_t = sb("reverse_t", [P, P])
        is_end_p = sb("is_end_p", [P, 2])
        p_col = sb("p_col", [P, 8], I32)
        p_bit = sb("p_bit", [P, 8], I32)
        sign = sb("sign", [P, 8])
        slot_row_id = sb("slot_row_id", [P, TILES], I32)
        ones_bf = sb("ones_bf", [P, P], BF16)
        gate_w = sb("gate_w", [P, 4 * HID])
        gate_pair = sb("gate_pair", [P, 3 * P])
        bi_col = sb("bi_col", [P, 3])
        bh_col = sb("bh_col", [P, 3])
        b_rz = sb("b_rz", [P, 2])
        w1_t = sb("w1_t", [ED, HID])
        w2_b = sb("w2_b", [HID + 1, HID])
        b1_col = sb("b1_col", [HID, 1])
        bi3 = sb("bi3", [3, 3 * HID])
        bh3 = sb("bh3", [3, 3 * HID])
        b3 = sb("b3", [3, 4 * HID])
        bias_rest = sb("bias_rest", [3, 4 * HID])
        bias_part = sb("bias_part", [3, 3, 4 * HID], BF16)
        bias_acc = sb("bias_acc", [3, 4 * HID])
        bias_rows = sb("bias_rows", [P, 8 * HID], BF16)

        target = sb("target", [P, TILES + 1])
        rank = sb("rank", [P, TILES])
        carry_mask = sb("carry_mask", [P, TILES])
        target_idx = sb("target_idx", [P, TILES], I32)
        edge_idx = sb("edge_idx", [P, TILES], I32)
        rep_idx = sb("rep_idx", [P, TILES], I32)
        src_node = sb("src_node", [P, TILES], I32)
        src_row = sb("src_row", [P, TILES], I32)

        msg_base = sb("msg_base", [P, TILES * HID])
        idx_g = {name: [sb(f"{name}_idx{b}", [P, GT], I32) for b in range(2)] for name in ("rows", "xj", "xi", "map", "node", "src", "y")}
        map_row_g = [sb(f"map_row_g{b}", [P, GT], I32) for b in range(2)]
        src_row_g = [sb(f"src_row_g{b}", [P, GT], I32) for b in range(2)]
        run_on = sb("run_on", [P, TILES])
        edge_f = sb("edge_f", [P, TILES])
        rep_f = sb("rep_f", [P, TILES])
        run_end = sb("run_end", [P, TILES])
        dst_stage = sb("dst_stage", [LOAD_P, E // LOAD_P], I32)[:, :]
        attr_stage = msg_base[0:LOAD_P, 0:E // LOAD_P * ED]
        scratch = [E // LOAD_P * ED]

        def square(cols=SORT_COLS, dt=F32):
            a = msg_base[:, scratch[0]:scratch[0] + cols]
            scratch[0] += cols
            assert scratch[0] <= TILES * HID
            return a.bitcast(dt) if dt != F32 else a

        key_i = square(dt=I32)
        local_e = square(dt=I32)
        block_e = square()
        kk = [square(), square()]
        pp = [square(), square()]
        swap = square(SORT_COLS // 2)
        delta = square(SORT_COLS // 2)
        node_id = square(MAP_COLS, I32)

        RZ = [sb(f"rz{b}", [P, NU, 2 * HID]) for b in range(2)]
        pre = [sb(f"pre{b}", [P, NU, HID]) for b in range(2)]
        cand = [sb(f"cand{b}", [P, NU, HID]) for b in range(2)]
        dif = [sb(f"dif{b}", [P, NU, HID]) for b in range(2)]
        xt = [sb(f"xt{b}", [P, 4 * P]) for b in range(2)]
        var = sb("var", [P, 16])
        vhalf = sb("vhalf", [P, 16])
        rstd = sb("rstd", [P, 16])
        nt1 = sb("nt1", [P, 16])
        nt2 = sb("nt2", [P, 16])

        ARENA = E // LOAD_P * ROW
        arena = sb("arena", [P, ARENA])
        at = [0]

        def carve(cols):
            a = arena[:, at[0]:at[0] + cols]
            at[0] += cols
            assert at[0] <= ARENA, at[0]
            return a

        def v3(a, u):
            return a.rearrange("p (u f) -> p u f", u=u)

        edge_stage = arena[0:LOAD_P, :].rearrange("p (r d) -> p r d", d=ROW)
        TW = NU * HID
        x_t = [[v3(carve(TW), NU) for j in range(JT)] for b in range(2)]
        h_t = [[v3(carve(TW), NU) for b in range(2)] for j in range(JT)]
        x_turn = [[carve(TW) for j in range(JT)] for b in range(2)]
        h_turn = [carve(TW) for j in range(JT)]
        y_t = [v3(carve(TW), NU) for j in range(JT)]
        sq = [v3(carve(TW), NU) for b in range(2)]
        rows_g = [v3(carve(GT * ROW), GT) for b in range(2)]
        xj_g = [v3(carve(GT * HID), GT) for b in range(2)]
        xi_g = [v3(carve(GT * HID), GT) for b in range(2)]
        attr_t = carve(4 * P)
        hidden = carve(4 * P)
        ln_sum = carve(8)
        at[0] = 0
        xc = [v3(carve(GT * 2 * HID), GT) for b in range(2)]
        g_c = [v3(carve(GT * HID), GT) for b in range(2)]
        msg = [v3(carve(GT * HID), GT) for b in range(2)]
        same = [v3(carve(4 * P), 4) for h in range(2)]
        h_c = [v3(carve(GT * HID), GT) for b in range(2)]
        xi_c = [v3(carve(GT * HID), GT) for b in range(2)]
        y_c = [v3(carve(GT * HID), GT) for b in range(2)]
        sq_c = v3(carve(TW), NU)
        rank_g = [carve(GT // 2).bitcast(BF16) for b in range(2)]
        mask_g = [carve(GT) for b in range(2)]
        ln_sum_c = carve(8)

        gates = [ps(f"gates{b}", [P, NU, 4 * HID]) for b in range(2)]
        xt_ps = [ps(f"xt_ps{b}", [P, 4 * P]) for b in range(2)]
        bank_a = ps("bank_a", [P, 4 * P])
        bank_b = ps("bank_b", [P, 4 * P])

        sum_bank = [bank_a, xt_ps[1]]

        def slot_sum(u):
            return sum_bank[u // 4][:, u % 4 * HID:(u % 4 + 1) * HID]

        def dense_gate(k2, g):
            return gates[k2][:, :, :].rearrange("p u f -> p (u f)")[:, g * TW:(g + 1) * TW]

        def flat(tile):
            return tile[:, :, :].rearrange("p u f -> p (u f)")

        S = {}
        for name in (
            "pad_set", "keys_loaded", "weights_loaded", "attr_loaded", "dst_loaded", "zero_set", "consts_set", "masks_set",
            "rows_made", "rows_stored", "map_stored", "sort_step", "flipped", "unflipped", "sorted_", "shifted", "columns_set", "before_set", "mean_set", "ends_set", "ranked", "ranks_set", "reverse_asked", "reversed_", "carried",
            "setup_step", "bias_set",
            "x_loaded0", "x_loaded1", "x_turned", "x_turn_copied", "back_turned", "rows_ready", "gates_ready", "r_ready", "z_ready", "pre_tanh_ready",
            "n_ready", "diff_ready", "gated_ready", "h_ready", "square_ready",
            "var_ready", "newton_step", "y_ready",
            "rows_got0", "rows_got1", "xj_got0", "xj_got1", "xi_got0", "xi_got1", "map_put0", "map_put1", "xj_stored0", "xj_stored1",
            "xi_stored0", "xi_stored1", "src_saved", "attr_turned", "attr_t_copied", "hidden_summed", "hidden_ready", "base_summed", "base_copied",
            "src_row_got0", "src_row_got1", "rows_idx_set", "xj_idx_set", "xi_idx_set", "map_idx_set", "node_idx_set", "src_idx_set", "y_idx_set", "pool_passed", "map_rows_set", "src_rows_saved",
            "rank_copied", "bcast_ready", "same_ready", "msg_ready", "agg_summed", "agg_copied", "g_got0", "g_got1",
            "g_loaded0", "g_loaded1", "xc_loaded0", "xc_loaded1", "xi_loaded0", "xi_loaded1", "hc_stored0", "hc_stored1",
            "c_xt_ready", "c_xt_copied", "c_gates_ready", "c_rz_ready", "c_r_hn_ready", "c_pre_tanh_ready",
            "c_n_ready", "c_diff_ready", "c_gated_ready", "c_h_ready", "c_resid_ready", "c_sum_ready", "c_center_ready",
            "c_square_ready", "c_var_ready", "c_newton_step", "c_y_ready", "y_put0", "y_put1",
        ):
            S[name] = sem(name)
        h_stored = [[sem(f"h_stored_{j}_{b}") for b in range(2)] for j in range(JT)]
        y_stored = [sem(f"y_stored_{j}") for j in range(JT)]

        turn_asked = sem("turn_asked")
        turned = sem("turned")

        block = ctx.enter_context(nc.Block())

        WEIGHT_DMAS = 23
        BACK_LAG = 3
        X_TICKS = {10: 0, 11: 1, 12: 2, 13: 3}
        NORM_TICKS = {1: ((0, 0),), 2: ((0, 1), (1, 0)), 3: ((1, 1), (2, 0)), 4: ((2, 1), (3, 0)), 5: ((3, 1),)}
        NEWTON_TICKS = (6, 7, 8, 9)
        SCALE_TICKS = {10: (0, 1), 11: (2, 3)}
        MLP_TICKS = {3: (0, 0), 4: (0, 1), 6: (0, 2), 7: (1, 0), 8: (1, 1), 9: (1, 2)}

        def run_groups(eng, body, peel=3):
            for g in range(peel):
                body(g, g % 2, g // 2)
            with eng.Fori((peel - 1) // 2, (GROUPS - 3) // 2) as m:
                body(m * 2 + 1, 1, m)
                body(m * 2 + 2, 0, m + 1)
            body(GROUPS - 2, 1, (GROUPS - 3) // 2)
            body(GROUPS - 1, 0, (GROUPS - 1) // 2)

        def is_first(i):
            return isinstance(i, int) and i == 0

        def is_end(i, count):
            return isinstance(i, int) and i == count - 1

        def phases():
            res = []
            for m in range(1, 17):
                high = [l for l in range(m - 1, -1, -1) if l >= 14 or 7 <= l]
                low = [l for l in range(m - 1, -1, -1) if l < 7]
                if high:
                    res.append(("N", m, high))
                res.append(("T", m, low))
            return res

        def turn_list():
            res, lay, k, p = [], "T", 0, 0
            for L, m, ls in phases():
                if L != lay:
                    res.append(kk[k])
                    k ^= 1
                    if m >= 15:
                        res.append(pp[p])
                        p ^= 1
                    lay = L
                k ^= len(ls) & 1
                if m >= 15:
                    p ^= len(ls) & 1
                if L == "T" and m == 14:
                    k ^= 1
            return res + [kk[k], pp[p]]

        TURNS = turn_list()

        def reversals():
            bank_c = gates[0][:, 0:2, :].rearrange("p u f -> p (u f)")
            return ((edge_f, bank_a), (target, bank_b), (rank, xt_ps[0]), (run_on, xt_ps[1]), (rep_f, bank_c))

        @block.sync
        def _(sp):
            sp.wait_ge(S["pad_set"], 1)
            with nc.allow_non_contiguous_dma(reason="small loads"):
                sp.dma_start(key_i[0:LOAD_P, :].rearrange("p (q f) -> p q f", q=BLOCKS)[:, :, 0:LOAD_F],
                             src.rearrange("(q p f) -> p q f", q=BLOCKS, p=LOAD_P)).then_inc(S["keys_loaded"], 16)
                sp.dma_start(attr_stage, attr.rearrange("(p r) d -> p (r d)", p=LOAD_P)).then_inc(S["attr_loaded"], 16)
                sp.dma_start(dst_stage, dst.rearrange("(p r) -> p r", p=LOAD_P)).then_inc(S["dst_loaded"], 16)
                sp.wait_ge(S["zero_set"], 5)
                w = S["weights_loaded"]
                sp.dma_start(gate_w[0:HID, 0:2 * HID], wit[:, 0:2 * HID]).then_inc(w, 16)
                sp.dma_start(gate_w[0:HID, 3 * HID:4 * HID], wit[:, 2 * HID:3 * HID]).then_inc(w, 16)
                sp.dma_start(gate_w[HID:P, 0:3 * HID], wht).then_inc(w, 16)
                for hf in range(2):
                    rows = slice(hf * HID, (hf + 1) * HID)
                    for g in range(3):
                        sp.dma_start(gate_pair[rows, g * P + hf * HID:g * P + (hf + 1) * HID], wht[:, g * HID:(g + 1) * HID]).then_inc(w, 16)
                    sp.dma_start(bi_col[rows, :], bih.rearrange("(g f) -> f g", g=3)).then_inc(w, 16)
                    sp.dma_start(bh_col[rows, :], bhh.rearrange("(g f) -> f g", g=3)).then_inc(w, 16)
                sp.dma_start(w1_t[:, :], w1t).then_inc(w, 16)
                sp.dma_start(w2_b[0:HID, :], w2t).then_inc(w, 16)
                sp.dma_start(w2_b[HID:HID + 1, :], b2.rearrange("(o f) -> o f", o=1)).then_inc(w, 16)
                sp.dma_start(b1_col[:, :], b1.rearrange("(f o) -> f o", o=1)).then_inc(w, 16)
                for k in range(3):
                    sp.dma_start(bi3[k:k + 1, :], bih.rearrange("(o f) -> o f", o=1)).then_inc(w, 16)
                    sp.dma_start(bh3[k:k + 1, :], bhh.rearrange("(o f) -> o f", o=1)).then_inc(w, 16)
            sp.wait_ge(S["consts_set"], 1)
            sp.dma_start(row_map.rearrange("(p c) o -> p (c o)", p=P), node_id[:, :]).then_inc(S["map_stored"], 16)
            sp.wait_ge(S["rows_made"], 2)
            sp.dma_start(edge_rows.rearrange("(p r) d -> p (r d)", p=LOAD_P),
                         edge_stage[:, :, :].rearrange("p r d -> p (r d)")).then_inc(S["rows_stored"], 16)

            def load_x(i, par):
                for j in range(JT):
                    if is_end(i, ITERS) and j == JT - 1:
                        rows = x[LAST_BASE:N, :].rearrange("(p u) f -> p (u f)", p=P)
                    else:
                        rows = node_rows(x, i * JT + j)
                    sp.dma_start(x_t[par][j].rearrange("p u f -> p (u f)"), rows).then_inc(S[f"x_loaded{par}"], 16)

            def store_tile(dram, i, j, tile):
                if is_end(i, ITERS) and j == JT - 1:
                    return (dram[LAST_BASE + NU * LAST_NEW_P:N, :].rearrange("(p u) f -> p (u f)", u=NU),
                            tile[LAST_NEW_P:P].rearrange("p u f -> p (u f)"))
                return node_rows(dram, i * JT + j), tile.rearrange("p u f -> p (u f)")

            def store_y(i, j):
                sp.wait_ge(S["y_ready"], i * JT + j + 1)
                d, s = store_tile(out, i, j, y_t[j])
                sp.dma_start(d, s).then_inc(y_stored[j], 16)

            def store_gathers(i, par, uses):
                sp.wait_ge(S[f"xj_got{par}"], (uses + 1) * (16 * GT))
                sp.dma_start(slot_rows(slot_src, i), xj_g[par].rearrange("p u f -> p (u f)")).then_inc(S[f"xj_stored{par}"], 16)
                sp.wait_ge(S[f"xi_got{par}"], (uses + 1) * (16 * GT))
                sp.dma_start(slot_rows(slot_x, i), xi_g[par].rearrange("p u f -> p (u f)")).then_inc(S[f"xi_stored{par}"], 16)

            def dense(i, par, uses):
                for k in range(3 * JT):
                    j, t = k % JT, k // JT
                    if k == 2 and not is_end(i, ITERS):
                        if not is_first(i):
                            sp.wait_ge(S["x_turned"], i * JT)
                        load_x(i + 1, 1 - par)
                    if k == 6 and not is_first(i):
                        store_gathers(i - 1, 1 - par, uses - par_uses(par))
                    if k in (9, 10) and not is_first(i):
                        store_y(i - 1, 2 * (k - 9))
                        store_y(i - 1, 2 * (k - 9) + 1)
                    sp.wait_ge(S["rows_ready"], i * UNITS + k + 1)
                    d, s = store_tile(table[t + 1], i, j, h_t[j][t % 2])
                    sp.dma_start(d, s).then_inc(h_stored[j][t % 2], 16)

            def par_uses(par):
                return 0 if par == 1 else 1

            sp.wait_ge(S["rows_stored"], 16)
            load_x(0, 0)
            run_groups(sp, dense)
            for j in range(JT):
                store_y(ITERS - 1, j)
            store_gathers(ITERS - 1, 0, (ITERS - 1) // 2)

            def load_g(g, par):
                if not (isinstance(g, int) and g < 2):
                    sp.wait_ge(S["msg_ready"], g - 1)
                sp.dma_start(g_c[par].rearrange("p u f -> p (u f)"), slot_rows(slot_src, g)).then_inc(S[f"g_loaded{par}"], 16)

            def load_states(t, g, par):
                early = isinstance(g, int) and g < 2
                if t == STEPS - 1 and not early:
                    sp.wait_ge(S["c_resid_ready"], (g - 1) * 2)
                elif not (early and t == 0):
                    sp.wait_ge(S["c_diff_ready"], t * GROUPS * 2 if early else (g + t * GROUPS - 1) * 2)
                sp.dma_start(xc[par][:, :, HID:2 * HID],
                             slot_rows(slot_table[t], g).rearrange("p (u f) -> p u f", u=GT)).then_inc(S[f"xc_loaded{par}"], 16)
                if t == STEPS - 1:
                    sp.dma_start(xi_c[par].rearrange("p u f -> p (u f)"), slot_rows(slot_x, g)).then_inc(S[f"xi_loaded{par}"], 16)

            def slot_store(t, g, par):
                sp.wait_ge(S["c_h_ready"], (g + t * GROUPS) * 2 + 2)
                sp.dma_start(slot_rows(slot_table[t + 1], g), h_c[par].rearrange("p u f -> p (u f)")).then_inc(S[f"hc_stored{par}"], 16)

            for j in range(JT):
                sp.wait_ge(h_stored[j][0], 16 * 2 * ITERS)
                sp.wait_ge(h_stored[j][1], 16 * ITERS)
                sp.wait_ge(y_stored[j], 16 * ITERS)
            sp.wait_ge(S["xj_stored0"], 16 * 25)
            sp.wait_ge(S["xj_stored1"], 16 * 24)
            sp.wait_ge(S["xi_stored0"], 16 * 25)
            sp.wait_ge(S["xi_stored1"], 16 * 24)
            sp.wait_ge(S["base_copied"], 2 * GROUPS)
            sp.wait_ge(S["src_saved"], GROUPS)
            for t in range(STEPS):
                def both(g, par, uses, t=t):
                    if t == 0 and not (isinstance(g, int) and g >= GROUPS - 2):
                        load_g(g + 2, par)
                    if not is_end(g, GROUPS):
                        load_states(t, g + 1, 1 - par)
                    if not is_first(g) and t < STEPS - 1:
                        slot_store(t, g - 1, 1 - par)

                if t == 0:
                    load_g(0, 0)
                    load_g(1, 1)
                load_states(t, 0, 0)
                run_groups(sp, both)
                if t < STEPS - 1:
                    slot_store(t, GROUPS - 1, 0)
                    sp.wait_ge(S["hc_stored0"], 16 * 25 * (t + 1))
                    sp.wait_ge(S["hc_stored1"], 16 * 24 * (t + 1))

        @block.gpsimd
        def _(pool):
            pool.memset(key_i[:, :], PAD_KEY).then_inc(S["pad_set"], 1)
            pool.memset(gate_w[:, :], 0.0).then_inc(S["zero_set"], 1)
            pool.memset(gate_pair[:, :], 0.0).then_inc(S["zero_set"], 1)
            pool.memset(bias_rows[:, :], 0.0).then_inc(S["zero_set"], 1)
            pool.memset(ones_bf[:, :], 1.0).then_inc(S["zero_set"], 1)
            pool.memset(w2_b[:, :], 0.0).then_inc(S["zero_set"], 1)
            pool.memset(center_pair[:, :], 0.0).then_inc(S["mean_set"], 1)
            pool.wait_ge(S["mean_set"], 1)
            for hf in range(2):
                span = slice(hf * HID, (hf + 1) * HID)
                pool.memset(center_pair[span, span], 1.0 / HID).then_inc(S["mean_set"], 1)
            pool.wait_ge(S["mean_set"], 3)
            pool.memset(before_t[:, :], 1.0).then_inc(S["before_set"], 1)
            pool.wait_ge(S["before_set"], 1)
            pool.affine_select(out=before_t[:, :], in_=before_t[:, :], pattern=[[1, P]], compare_op=ALU.is_gt,
                               fill=0.0, base=0, channel_multiplier=-1).then_inc(S["before_set"], 1)
            for n, (tile, base, cm) in enumerate(((ident, 0, 1), (shift_t, -1, 1), (wrap_t, P - 1, P))):
                pool.memset(tile[:, :], 0.0).then_inc(S["masks_set"], 1)
                pool.wait_ge(S["masks_set"], 2 * n + 1)
                pool.affine_select(out=tile[:, :], in_=tile[:, :], pattern=[[-1, P]], compare_op=ALU.not_equal,
                                   fill=1.0, base=base, channel_multiplier=cm).then_inc(S["masks_set"], 1)
            pool.memset(is_end_p[:, :], 0.0).then_inc(S["masks_set"], 1)
            pool.memset(reverse_t[:, :], 0.0).then_inc(S["masks_set"], 1)
            pool.wait_ge(S["masks_set"], 8)
            for end, base in ((0, 0), (1, -(P - 1))):
                pool.affine_select(out=is_end_p[:, end:end + 1], in_=is_end_p[:, end:end + 1], pattern=[[0, 1]],
                                   compare_op=ALU.not_equal, fill=1.0, base=base, channel_multiplier=1).then_inc(S["masks_set"], 1)
            pool.affine_select(out=reverse_t[:, :], in_=reverse_t[:, :], pattern=[[1, P]], compare_op=ALU.not_equal,
                               fill=1.0, base=-(P - 1), channel_multiplier=1).then_inc(S["masks_set"], 1)
            pool.iota(local_e[:, :], [[0, BLOCKS], [1, P]], base=0, channel_multiplier=LOAD_F).then_inc(S["masks_set"], 1)
            pool.iota(p_col[:, :], [[0, 8]], base=0, channel_multiplier=1).then_inc(S["masks_set"], 1)
            pool.iota(block_e[:, :], [[BLOCK_E, BLOCKS], [0, P]], base=0, channel_multiplier=0,
                      allow_small_or_imprecise_dtypes=True).then_inc(S["masks_set"], 1)
            pool.iota(node_id[:, :], [[1, MAP_COLS]], base=0, channel_multiplier=MAP_COLS).then_inc(S["consts_set"], 1)
            pool.iota(slot_row_id[:, :], [[GT * P, GROUPS], [1, GT]], base=N, channel_multiplier=GT).then_inc(S["consts_set"], 1)
            pool.wait_ge(S["dst_loaded"], 16)
            pool.tensor_copy(edge_stage[:, :, ED:ROW].bitcast(I32).rearrange("p r o -> p (r o)"), dst_stage).then_inc(S["rows_made"], 1)

            def gather(o, table_ap, idx, bound, s):
                pool.indirect_dma_start(out=o, out_offset=None, in_=table_ap,
                                        in_offset=bass.IndirectOffsetOnAxis(ap=idx, axis=0),
                                        bounds_check=bound).then_inc(s, 16)

            def column(tile, g, u):
                return tile[:, bass.ds(g * GT + u, 1)]

            def copy_indices(name, tile, g, par):
                pool.tensor_copy(idx_g[name][par][:, :], tile[:, bass.ds(g * GT, GT)]).then_inc(S[name + "_idx_set"], 1)

            def passed(semaphore, count):
                pool.wait_ge(S[semaphore], count)
                pool.sem_inc(S["pool_passed"], 1)

            def get_rows(par):
                for u in range(GT):
                    gather(rows_g[par][:, u, :], edge_rows, idx_g["rows"][par][:, u:u + 1], E - 1, S[f"rows_got{par}"])

            def setup(i, par, uses):
                if not is_end(i, ITERS):
                    copy_indices("rows", edge_idx, i + 1, 1 - par)
                if not (isinstance(i, int) and i < 2):
                    passed(f"xj_stored{par}", uses * 16)
                    passed(f"xi_stored{par}", uses * 16)
                    passed(f"map_put{par}", uses * (16 * GT))
                copy_indices("xi", target_idx, i, par)
                copy_indices("map", rep_idx, i, par)
                pool.tensor_copy(map_row_g[par][:, :], slot_row_id[:, bass.ds(i * GT, GT)]).then_inc(S["map_rows_set"], 1)
                passed(f"rows_got{par}", (uses + 1) * (16 * GT))
                pool.tensor_copy(idx_g["xj"][par][:, :], rows_g[par][:, :, ED:ROW].bitcast(I32).rearrange("p u o -> p (u o)")).then_inc(S["xj_idx_set"], 1)
                passed("xi_idx_set", i + 1)
                for u in range(GT):
                    gather(xi_g[par][:, u, :], x, idx_g["xi"][par][:, u:u + 1], N - 1, S[f"xi_got{par}"])
                if not is_end(i, ITERS):
                    if not is_first(i):
                        passed("attr_turned", i * 2)
                        passed("src_saved", i)
                    passed("rows_idx_set", i + 2)
                    get_rows(1 - par)
                passed("xj_idx_set", i + 1)
                for u in range(GT):
                    gather(xj_g[par][:, u, :], x, idx_g["xj"][par][:, u:u + 1], N - 1, S[f"xj_got{par}"])
                passed("map_idx_set", i + 1)
                passed("map_rows_set", i + 1)
                for u in range(GT):
                    pool.indirect_dma_start(out=row_map, out_offset=bass.IndirectOffsetOnAxis(ap=idx_g["map"][par][:, u:u + 1], axis=0),
                                            in_=map_row_g[par][:, u:u + 1], in_offset=None,
                                            bounds_check=N - 1, oob_is_err=False).then_inc(S[f"map_put{par}"], 16)

            pool.wait_ge(S["rows_stored"], 16)
            pool.wait_ge(S["map_stored"], 16)
            pool.wait_ge(S["columns_set"], 3)
            copy_indices("rows", edge_idx, 0, 0)
            pool.wait_ge(S["rows_idx_set"], 1)
            get_rows(0)
            run_groups(pool, setup)

            pool.wait_ge(S["map_put0"], 16 * GT * 25)
            pool.wait_ge(S["map_put1"], 16 * GT * 24)
            pool.wait_ge(S["src_saved"], GROUPS)

            def get_src_rows(g, par, uses):
                early = isinstance(g, int) and g < 2
                if not early:
                    passed(f"src_row_got{par}", uses * (16 * GT))
                    pool.tensor_copy(src_row[:, bass.ds((g - 2) * GT, GT)], src_row_g[par][:, :]).then_inc(S["src_rows_saved"], 1)
                copy_indices("node", src_node, g, par)
                if not early:
                    passed("src_rows_saved", g - 1)
                passed("node_idx_set", g + 1)
                for u in range(GT):
                    gather(src_row_g[par][:, u:u + 1], row_map, idx_g["node"][par][:, u:u + 1], N - 1, S[f"src_row_got{par}"])

            run_groups(pool, get_src_rows)
            pool.wait_ge(S["src_row_got0"], 16 * GT * 25)
            pool.wait_ge(S["src_row_got1"], 16 * GT * 24)
            for g in (GROUPS - 2, GROUPS - 1):
                pool.tensor_copy(src_row[:, g * GT:(g + 1) * GT], src_row_g[g % 2][:, :]).then_inc(S["src_rows_saved"], 1)
            pool.wait_ge(S["src_rows_saved"], GROUPS)

            def put_y(g, par, uses):
                if not (isinstance(g, int) and g < 2):
                    passed(f"y_put{par}", uses * (16 * GT))
                copy_indices("y", rep_idx, g, par)
                passed("y_idx_set", g + 1)
                passed("c_y_ready", g * 2 + 2)
                for u in range(GT):
                    pool.indirect_dma_start(out=out, out_offset=bass.IndirectOffsetOnAxis(ap=idx_g["y"][par][:, u:u + 1], axis=0),
                                            in_=y_c[par][:, u, :], in_offset=None,
                                            bounds_check=N - 1, oob_is_err=False).then_inc(S[f"y_put{par}"], 16)

            for j in range(JT):
                pool.wait_ge(h_stored[j][0], 16 * 2 * ITERS)
                pool.wait_ge(h_stored[j][1], 16 * ITERS)
                pool.wait_ge(y_stored[j], 16 * ITERS)
            for t in range(1, STEPS):
                def get(g, par, uses, t=t):
                    gg = g + t * GROUPS
                    if is_first(g):
                        pool.wait_ge(S["hc_stored0"], 16 * 25 * t)
                        pool.wait_ge(S["hc_stored1"], 16 * 24 * t)
                    early = isinstance(g, int) and g < 2
                    if not (early and t == 1):
                        passed(f"g_got{par}", (uses + (t - 1) * (25 if par == 0 else 24)) * (16 * GT))
                    copy_indices("src", src_row, g, par)
                    passed("src_idx_set", gg - GROUPS + 1)
                    passed("msg_ready", t * GROUPS if early else gg - 1)
                    for u in range(GT):
                        gather(g_c[par][:, u, :], table[t], idx_g["src"][par][:, u:u + 1], N + SLOTS - 1, S[f"g_got{par}"])
                    if t == STEPS - 1 and not (isinstance(g, int) and g < 3):
                        put_y(g - 3, 1 - par, uses - 1 if par == 1 else uses - 2)

                run_groups(pool, get, 5 if t == STEPS - 1 else 3)
            put_y(GROUPS - 3, 0, 23)
            put_y(GROUPS - 2, 1, 23)
            put_y(GROUPS - 1, 0, 24)
            pool.wait_ge(S["y_put0"], 16 * GT * 25)
            pool.wait_ge(S["y_put1"], 16 * GT * 24)

        def gate_matmuls_bias(k2):
            for b in range(2):
                nc.tensor.matmul(gates[k2][:, 2 * b:2 * b + 2, :].rearrange("p u f -> p (u f)"), ones_bf[:, :], bias_rows[:, :],
                                 start=True, stop=False, skip_group_check=True)

        def sigmoid_unit(act, c, k, k2):
            act.wait_ge(S[c + "gates_ready"], k + 1)
            if not (isinstance(k, int) and k < 2):
                act.wait_ge(S[c + "gated_ready"], k - 1)
            nc.scalar.activation(RZ[k2][:, :, :], gates[k2][:, :, 0:2 * HID], ACT.Sigmoid).then_inc(S[c + "rz_ready"], 1)

        def tanh_unit(act, c, k, k2):
            act.wait_ge(S[c + "pre_tanh_ready"], k + 1)
            if not (isinstance(k, int) and k < 2):
                act.wait_ge(S[c + "h_ready"], k - 1)
            nc.scalar.activation(cand[k2][:, :, :], pre[k2][:, :, :], ACT.Tanh).then_inc(S[c + "n_ready"], 1)

        def vec_r_hn(dve, c, k, k2):
            dve.wait_ge(S[c + "rz_ready"], k + 1)
            if not (isinstance(k, int) and k < 2):
                dve.wait_ge(S[c + "n_ready"], k - 1)
            nc.vector.tensor_tensor(pre[k2][:, :, :], gates[k2][:, :, 2 * HID:3 * HID], RZ[k2][:, :, 0:HID],
                                    ALU.mult).then_inc(S[c + "r_hn_ready"], 1)

        def vec_pre(dve, c, k, k2):
            dve.wait_ge(S[c + "r_hn_ready"], k + 1)
            nc.vector.tensor_tensor(pre[k2][:, :, :], pre[k2][:, :, :], gates[k2][:, :, 3 * HID:4 * HID],
                                    ALU.add).then_inc(S[c + "pre_tanh_ready"], 1)

        def vec_diff(dve, c, k, k2, h):
            dve.wait_ge(S[c + "n_ready"], k + 1)
            nc.vector.tensor_tensor(dif[k2][:, :, :], h, cand[k2][:, :, :],
                                    ALU.subtract).then_inc(S[c + "diff_ready"], 1)

        def vec_gate(dve, c, k, k2):
            dve.wait_ge(S[c + "diff_ready"], k + 1)
            nc.vector.tensor_tensor(dif[k2][:, :, :], dif[k2][:, :, :], RZ[k2][:, :, HID:2 * HID],
                                    ALU.mult).then_inc(S[c + "gated_ready"], 1)

        def vec_h(dve, c, k, k2, h_new):
            dve.wait_ge(S[c + "gated_ready"], k + 1)
            nc.vector.tensor_tensor(h_new, dif[k2][:, :, :], cand[k2][:, :, :],
                                    ALU.add).then_inc(S[c + "h_ready"], 1)

        def norm_stage(dve, c, stage, n, inputs, xx, hh, y, sqt, sums, v4):
            if stage == 0:
                inputs()
                nc.vector.tensor_tensor(y, xx, hh, ALU.add).then_inc(S[c + "resid_ready"], 1)
            elif stage == 1:
                dve.wait_ge(S[c + "resid_ready"], n + 1)
                nc.vector.tensor_reduce(sums, y, AX_X, ALU.add).then_inc(S[c + "sum_ready"], 1)
            elif stage == 2:
                dve.wait_ge(S[c + "sum_ready"], n + 1)
                nc.vector.scalar_tensor_tensor(out=y, in0=sums.unsqueeze(2).to_broadcast([P, NU, HID]), scalar=-1.0 / HID, in1=y,
                                               op0=ALU.mult, op1=ALU.add).then_inc(S[c + "center_ready"], 1)
            elif stage == 3:
                dve.wait_ge(S[c + "center_ready"], n + 1)
                nc.vector.tensor_tensor(sqt, y, y, ALU.mult).then_inc(S[c + "square_ready"], 1)
            else:
                dve.wait_ge(S[c + "square_ready"], n + 1)
                nc.vector.tensor_reduce(v4, sqt, AX_X, ALU.add).then_inc(S[c + "var_ready"], 1)

        def newton_op(dve, c, done, stats, w, n):
            v, hf, r, a, b = (q[:, 0:w] for q in (var, vhalf, rstd, nt1, nt2))
            if n == 0:
                dve.wait_ge(S[c + "var_ready"], stats)
                ins = nc.vector.tensor_scalar(v, v, 1.0 / HID, EPS, ALU.mult, ALU.add)
            else:
                dve.wait_ge(S[c + "newton_step"], done + n)
            if n == 1:
                ins = nc.vector.tensor_scalar(hf, v, -0.5, None, ALU.mult)
            elif n == 2:
                ins = nc.vector.tensor_scalar(a.bitcast(I32), v.bitcast(I32), 1, None, ALU.logical_shift_right)
            elif n == 3:
                ins = nc.vector.tensor_scalar(r.bitcast(I32), a.bitcast(I32), -1.0, float(0x5F3759DF), ALU.mult, ALU.add)
            elif n > 3 and n % 3 == 1:
                ins = nc.vector.tensor_tensor(a, r, r, ALU.mult)
            elif n > 3 and n % 3 == 2:
                ins = nc.vector.tensor_tensor(b, a, hf, ALU.mult)
            elif n > 3:
                ins = nc.vector.scalar_tensor_tensor(out=r, in0=b, scalar=1.5, in1=r, op0=ALU.add, op1=ALU.mult)
            ins.then_inc(S[c + "newton_step"], 1)

        @block.tensor
        def _(pe):
            pe.wait_ge(S["masks_set"], 2)
            for n, square_in in enumerate(TURNS):
                pe.wait_ge(turn_asked, n + 1)
                for q in range(BLOCKS):
                    mm = nc.tensor.transpose(xt_ps[q // 2][:, q % 2 * P:(q % 2 + 1) * P], square_in[:, q * P:(q + 1) * P], ident[:, :])
                    if q % 2:
                        mm.then_inc(turned, 1)
            pe.wait_ge(S["sorted_"], 1)
            pe.wait_ge(S["masks_set"], 6)
            nc.tensor.matmul(bank_a[:, 0:TILES], shift_t[:, :], target[:, 0:TILES], start=True, stop=False)
            nc.tensor.matmul(bank_a[:, 0:TILES], wrap_t[:, :], target[:, 1:TILES + 1], start=False, stop=True).then_inc(S["shifted"], 1)
            pe.wait_ge(S["ends_set"], 1)
            pe.wait_ge(S["before_set"], 2)
            nc.tensor.matmul(bank_b[:, 0:TILES], before_t[:, :], run_end[:, :], start=True, stop=True).then_inc(S["ranked"], 1)
            pe.wait_ge(S["masks_set"], 11)
            pe.wait_ge(S["reverse_asked"], 1)
            for column, bank in reversals():
                nc.tensor.matmul(bank[:, 0:TILES], reverse_t[:, :], column[:, 0:TILES], start=True, stop=True).then_inc(S["reversed_"], 1)

            pe.wait_ge(S["weights_loaded"], 16 * WEIGHT_DMAS)
            pe.wait_ge(S["zero_set"], 5)
            pe.wait_ge(S["bias_set"], 1)

            def turn_x(i, j, par, uses):
                if j == 0:
                    pe.wait_ge(S[f"x_loaded{par}"], (uses + 1) * (16 * JT))
                if not (is_first(i) and j == 0):
                    pe.wait_ge(S["x_turn_copied"], i * JT + j)
                for a in range(2):
                    mm = nc.tensor.transpose(xt_ps[1][:, a * P:(a + 1) * P],
                                             x_t[par][j][:, 2 * a:2 * a + 2, :].rearrange("p u f -> p (u f)"), ident[:, :])
                mm.then_inc(S["x_turned"], 1)

            def turn_back(i, k, par):
                kk_, j = i * UNITS + k, k % JT
                pe.wait_ge(S["h_ready"], kk_ + 1)
                if not (is_first(i) and k == 0):
                    pe.wait_ge(S["rows_ready"], kk_)
                for a in range(2):
                    cols = slice(a * P, (a + 1) * P)
                    if k < 3 * JT:
                        mm = nc.tensor.transpose(xt_ps[0][:, cols], h_turn[j][:, cols], ident[:, :])
                    else:
                        nc.tensor.matmul(xt_ps[0][:, cols], h_turn[j][:, cols], center_pair[:, :], start=True, stop=False)
                        mm = nc.tensor.matmul(xt_ps[0][:, cols], x_turn[par][j][:, cols], center_pair[:, :], start=False, stop=True)
                mm.then_inc(S["back_turned"], 1)

            def gate_unit(i, k, par):
                kk_ = i * UNITS + k
                k2, j = k % 2, k % JT
                if not (is_first(i) and k < 2):
                    pe.wait_ge(S["pre_tanh_ready"], kk_ - 1)
                    pe.wait_ge(S["z_ready"], kk_ - 1)
                if k < JT:
                    pe.wait_ge(S["x_turn_copied"], i * JT + j + 1)
                else:
                    pe.wait_ge(S["h_ready"], kk_ - JT + 1)
                h = x_turn[par][j] if k < JT else h_turn[j]
                for g in range(3):
                    mm = nc.tensor.matmul(dense_gate(k2, g), gate_pair[:, g * P:(g + 1) * P], h, start=True, stop=True)
                mm.then_inc(S["gates_ready"], 1)

            def mlp(i, par, uses, half, stage):
                n = i * 2 + half
                if stage == 0:
                    if half == 0:
                        pe.wait_ge(S[f"rows_got{par}"], (uses + 1) * (16 * GT))
                    if not (is_first(i) and half == 0):
                        pe.wait_ge(S["base_copied"], n)
                    for u in range(4):
                        mm = nc.tensor.transpose(bank_a[0:ED, u * P:(u + 1) * P], rows_g[par][:, 4 * half + u, 0:ED], ident[:, :])
                    mm.then_inc(S["attr_turned"], 1)
                elif stage == 1:
                    pe.wait_ge(S["attr_t_copied"], n + 1)
                    nc.tensor.matmul(bank_b[0:HID, :], w1_t[:, :], attr_t[0:ED, :], start=True, stop=True).then_inc(S["hidden_summed"], 1)
                else:
                    pe.wait_ge(S["hidden_ready"], n + 1)
                    for u in range(4):
                        mm = nc.tensor.matmul(bank_a[:, u * HID:(u + 1) * HID], hidden[0:HID + 1, u * P:(u + 1) * P], w2_b[:, :],
                                              start=True, stop=True)
                    mm.then_inc(S["base_summed"], 1)

            def dense(i, par, uses):
                for k in range(UNITS):
                    gate_unit(i, k, par)
                    if k >= BACK_LAG:
                        turn_back(i, k - BACK_LAG, par)
                    elif not is_first(i):
                        turn_back(i - 1, k - BACK_LAG + UNITS, 1 - par)
                    if k in X_TICKS and not is_end(i, ITERS):
                        turn_x(i + 1, X_TICKS[k], 1 - par, uses if par == 0 else uses + 1)
                    if k in MLP_TICKS:
                        half, stage = MLP_TICKS[k]
                        mlp(i, par, uses, half, stage)

            for j in range(JT):
                turn_x(0, j, 0, 0)
            run_groups(pe, dense)
            for k in range(UNITS - BACK_LAG, UNITS):
                turn_back(ITERS - 1, k, 0)

            pe.wait_ge(S["base_copied"], 2 * GROUPS)
            pe.wait_ge(S["rows_ready"], ITERS * UNITS)

            for t in range(STEPS):
                def bcast(g, par, half, t=t):
                    gg = g + t * GROUPS
                    if half == 0:
                        pe.wait_ge(S["rank_copied"], gg + 1)
                    if not (t == 0 and is_first(g) and half == 0):
                        pe.wait_ge(S["same_ready"], gg * 2 + half)
                    for u in range(4):
                        col = rank_g[par][:, 4 * half + u:4 * half + u + 1].to_broadcast([P, P])
                        mm = nc.tensor.matmul(bank_b[:, u * P:(u + 1) * P], col, ident_bf[:, :], start=True, stop=True)
                    mm.then_inc(S["bcast_ready"], 1)

                def turn_slots(g, par, uses, b, t=t):
                    gg = g + t * GROUPS
                    n = gg * 2 + b
                    if b == 0:
                        pe.wait_ge(S[f"xc_loaded{par}"], (uses + t * (25 if par == 0 else 24) + 1) * 16)
                    pe.wait_ge(S["agg_copied"], gg * 2 + b + 1)
                    if not (t == 0 and is_first(g) and b == 0):
                        pe.wait_ge(S["c_xt_copied"], n)
                    for u in range(4):
                        mm = nc.tensor.transpose(xt_ps[0][:, u * P:(u + 1) * P], xc[par][:, 4 * b + u, :], ident[:, :])
                    mm.then_inc(S["c_xt_ready"], 1)

                def gate_bias(g, b, t=t):
                    n = (g + t * GROUPS) * 2 + b
                    if not (t == 0 and is_first(g)):
                        pe.wait_ge(S["c_pre_tanh_ready"], n - 1)
                    gate_matmuls_bias(b)

                def gate_part(g, b, u, t=t):
                    if u == 0:
                        pe.wait_ge(S["c_xt_copied"], (g + t * GROUPS) * 2 + b + 1)
                    mm = nc.tensor.matmul(gates[b][:, u, :], xt[b][:, u * P:(u + 1) * P], gate_w[:, :],
                                          start=False, stop=(u == 3), skip_group_check=True)
                    if u == 3:
                        mm.then_inc(S["c_gates_ready"], 1)

                def slots(g, par, uses, t=t):
                    gg = g + t * GROUPS
                    prev = not is_first(g)
                    pu = uses if par == 1 else uses - 1
                    for u in range(GT):
                        if u % 4 == 0:
                            pe.wait_ge(S["same_ready"], gg * 2 + u // 4 + 1)
                        if u == 0:
                            pe.wait_ge(S["msg_ready"], gg + 1)
                        if u % 4 == 0 and not (t == 0 and is_first(g)):
                            pe.wait_ge(S["agg_copied"], gg * 2 + u // 4 - 1)
                        if not (t == 0 and is_first(g) and u == 0):
                            pe.wait_ge(S["carried"], gg * GT + u)
                        nc.tensor.matmul(slot_sum(u), same[u // 4][:, u % 4, :], msg[par][:, u, :],
                                         start=True, stop=True).then_inc(S["agg_summed"], 1)
                        if prev and u > 0:
                            gate_part(g - 1, (u - 1) // 4, (u - 1) % 4)
                        if prev and u == 0:
                            turn_slots(g - 1, 1 - par, pu, 0)
                        if prev and u % 4 == 0:
                            gate_bias(g - 1, u // 4)
                        if prev and u == 2:
                            turn_slots(g - 1, 1 - par, pu, 1)
                        if u == 0:
                            bcast(g, par, 1)
                        if u == 4 and not is_end(g, GROUPS):
                            bcast(g + 1, 1 - par, 0)
                    if prev:
                        gate_part(g - 1, 1, 3)

                bcast(0, 0, 0)
                run_groups(pe, slots)
                for b in range(2):
                    turn_slots(GROUPS - 1, 0, 24, b)
                for b in range(2):
                    gate_bias(GROUPS - 1, b)
                    for u in range(4):
                        gate_part(GROUPS - 1, b, u)

        @block.scalar
        def _(act):
            act.wait_ge(S["attr_loaded"], 16)
            nc.scalar.copy(edge_stage[:, :, 0:ED], attr_stage.rearrange("p (r d) -> p r d", d=ED)).then_inc(S["rows_made"], 1)
            act.wait_ge(S["weights_loaded"], 16 * WEIGHT_DMAS)
            act.wait_ge(S["columns_set"], 3)

            def copy_x(i, j, par):
                act.wait_ge(S["x_turned"], i * JT + j + 1)
                if not (isinstance(i, int) and i < 2):
                    act.wait_ge(S["back_turned"], (i - 1) * UNITS - JT + j + 1)
                nc.scalar.copy(x_turn[par][j], xt_ps[1][:, 0:TW]).then_inc(S["x_turn_copied"], 1)

            def copy_back(i, k):
                j, t = k % JT, k // JT
                act.wait_ge(S["back_turned"], i * UNITS + k + 1)
                if t == 0 and not is_first(i):
                    act.wait_ge(h_stored[j][0], i * 32)
                if t == 1 and not is_first(i):
                    act.wait_ge(h_stored[j][1], i * 16)
                if t == 2:
                    act.wait_ge(h_stored[j][0], i * 32 + 16)
                if t == 3 and not is_first(i):
                    act.wait_ge(y_stored[j], i * 16)
                rows = y_t[j] if t == 3 else h_t[j][t % 2]
                nc.scalar.copy(rows.rearrange("p u f -> p (u f)"), xt_ps[0][:, 0:TW]).then_inc(S["rows_ready"], 1)

            def dense_sigmoid(i, k, g):
                kk_, k2 = i * UNITS + k, k % 2
                if g == 0:
                    act.wait_ge(S["gates_ready"], kk_ + 1)
                    if not (is_first(i) and k < 2):
                        act.wait_ge(S["pre_tanh_ready"], kk_ - 1)
                elif not (is_first(i) and k < 2):
                    act.wait_ge(S["gated_ready"], kk_ - 1)
                nc.scalar.activation(flat(RZ[k2])[:, g * TW:(g + 1) * TW], dense_gate(k2, g), ACT.Sigmoid,
                                     bias=b_rz[:, g:g + 1]).then_inc(S["r_ready" if g == 0 else "z_ready"], 1)

            def dense_tanh(kk_, k2, first):
                act.wait_ge(S["pre_tanh_ready"], kk_ + 1)
                if not first:
                    act.wait_ge(S["h_ready"], kk_ - 1)
                nc.scalar.activation(flat(cand[k2]), flat(pre[k2]), ACT.Tanh, bias=bi_col[:, 2:3]).then_inc(S["n_ready"], 1)

            def mlp(i, half, stage):
                n = i * 2 + half
                if stage == 0:
                    act.wait_ge(S["attr_turned"], n + 1)
                    if not (is_first(i) and half == 0):
                        act.wait_ge(S["hidden_summed"], n)
                    nc.scalar.copy(attr_t[0:ED, :], bank_a[0:ED, :]).then_inc(S["attr_t_copied"], 1)
                elif stage == 1:
                    act.wait_ge(S["hidden_summed"], n + 1)
                    if not (is_first(i) and half == 0):
                        act.wait_ge(S["base_summed"], n)
                    nc.scalar.activation(hidden[0:HID, :], bank_b[0:HID, :], ACT.Relu, bias=b1_col[:, :]).then_inc(S["hidden_ready"], 1)
                else:
                    act.wait_ge(S["base_summed"], n + 1)
                    nc.scalar.copy(msg_base[:, bass.ds(i * (GT * HID) + half * 4 * HID, 4 * HID)],
                                   bank_a[:, 0:4 * HID]).then_inc(S["base_copied"], 1)

            def dense(i, par, uses):
                for k in range(UNITS):
                    dense_sigmoid(i, k, 0)
                    if not (is_first(i) and k == 0):
                        dense_tanh(i * UNITS + k - 1, (k - 1) % 2, is_first(i) and k < 3)
                    dense_sigmoid(i, k, 1)
                    if k >= BACK_LAG:
                        copy_back(i, k - BACK_LAG)
                    elif not is_first(i):
                        copy_back(i - 1, k - BACK_LAG + UNITS)
                    if k in X_TICKS and not is_end(i, ITERS):
                        copy_x(i + 1, X_TICKS[k], 1 - par)
                    if k in MLP_TICKS:
                        half, stage = MLP_TICKS[k]
                        mlp(i, half, stage)

            act.wait_ge(S["rows_stored"], 16)
            act.wait_ge(S["bias_set"], 1)
            for j in range(JT):
                copy_x(0, j, 0)
            run_groups(act, dense)
            dense_tanh(ITERS * UNITS - 1, 1, False)
            for k in range(UNITS - BACK_LAG, UNITS):
                copy_back(ITERS - 1, k)
            for q in ("xj_stored", "xi_stored"):
                act.wait_ge(S[q + "0"], 16 * 25)
                act.wait_ge(S[q + "1"], 16 * 24)
            act.wait_ge(S["src_saved"], GROUPS)
            for j in range(JT):
                act.wait_ge(h_stored[j][0], 16 * 2 * ITERS)
                act.wait_ge(h_stored[j][1], 16 * ITERS)
                act.wait_ge(y_stored[j], 16 * ITERS)
            act.wait_ge(S["base_summed"], 2 * GROUPS)

            for t in range(STEPS):
                def copy_agg(g, par, half, t=t):
                    gg = g + t * GROUPS
                    act.wait_ge(S["carried"], gg * GT + 4 * half + 4)
                    if half == 0 and not (t == 0 and isinstance(g, int) and g < 2):
                        act.wait_ge(S["c_xt_ready"], gg * 2 - 2)
                    nc.scalar.copy(xc[par][:, 4 * half:4 * half + 4, 0:HID],
                                   sum_bank[half][:, 0:TW].rearrange("p (u f) -> p u f", u=4)).then_inc(S["agg_copied"], 1)

                def copy_xt_c(g, b, t=t):
                    n = (g + t * GROUPS) * 2 + b
                    act.wait_ge(S["c_xt_ready"], n + 1)
                    if not (t == 0 and is_first(g)):
                        act.wait_ge(S["c_gates_ready"], n - 1)
                    nc.scalar.copy(xt[b][:, :], xt_ps[0][:, :]).then_inc(S["c_xt_copied"], 1)

                def slots(g, par, uses, t=t):
                    prev = not is_first(g)
                    prev2 = not (isinstance(g, int) and g < 2)
                    k = (g + (t * GROUPS - 1)) * 2
                    if prev2:
                        tanh_unit(act, "c_", k - 2, 0)
                        sigmoid_unit(act, "c_", k - 1, 1)
                    if prev:
                        copy_xt_c(g - 1, 0)
                        copy_xt_c(g - 1, 1)
                    if prev2:
                        tanh_unit(act, "c_", k - 1, 1)
                    copy_agg(g, par, 0)
                    if prev:
                        sigmoid_unit(act, "c_", k, 0)
                    copy_agg(g, par, 1)

                run_groups(act, slots)
                k = (t * GROUPS + GROUPS - 1) * 2
                tanh_unit(act, "c_", k - 2, 0)
                sigmoid_unit(act, "c_", k - 1, 1)
                copy_xt_c(GROUPS - 1, 0)
                copy_xt_c(GROUPS - 1, 1)
                tanh_unit(act, "c_", k - 1, 1)
                for b in range(2):
                    sigmoid_unit(act, "c_", k + b, b)
                    tanh_unit(act, "c_", k + b, b)

        @block.vector
        def _(dve):
            sstep = [0]

            def step(ins):
                ins.then_inc(S["sort_step"], 1)
                sstep[0] += 1
                dve.wait_ge(S["sort_step"], sstep[0])

            TT = nc.vector.tensor_tensor
            TS = nc.vector.tensor_scalar
            dve.wait_ge(S["keys_loaded"], 16)
            dve.wait_ge(S["masks_set"], 14)
            cur, oth = kk[0], kk[1]
            step(TS(key_i[:, :], key_i[:, :], float(KEY_SHIFT), None, ALU.add))
            step(TS(key_i[:, :], key_i[:, :], LOCAL_BITS, None, ALU.logical_shift_left))
            step(TT(cur[:, :].bitcast(I32), key_i[:, :], local_e[:, :], ALU.bitwise_or))
            for b in range(7):
                step(TS(p_bit[:, b:b + 1], p_col[:, b:b + 1], b, 1, ALU.logical_shift_right, ALU.bitwise_and))
            step(TS(sign[:, 0:7], p_bit[:, 0:7], -2.0, 1.0, ALU.mult, ALU.add))

            def free_bit(lay, b):
                if lay == "N":
                    return b - 7
                return b if b < 7 else (b - 7 if b >= 14 else None)

            def halves(tile, lay, m, l):
                fl = free_bit(lay, l)
                fm = free_bit(lay, m) if m < 16 else None
                w = tile.shape[1]
                if fm is None:
                    v = tile[:, :].rearrange("p (h t l) -> p t h l", t=2, l=1 << fl)
                    return [(v[:, 0], v[:, 1], False)]
                v = tile[:, :].rearrange("p (h d m t l) -> p d t h m l", d=2, t=2, l=1 << fl, m=1 << (fm - fl - 1))
                return [(v[:, d, 0], v[:, d, 1], d == 1) for d in range(2)]

            def pair_view(tile, lay, m, l):
                fl = free_bit(lay, l)
                fm = free_bit(lay, m) if m < 16 else None
                if fm is None:
                    return [tile[:, :].rearrange("p (h l) -> p h l", l=1 << fl)]
                v = tile[:, :].rearrange("p (h d m l) -> p d h m l", d=2, l=1 << fl, m=1 << (fm - fl - 1))
                return [v[:, 0], v[:, 1]]

            lay = "T"
            cp, op = pp[0], pp[1]
            nturn = [0]

            def turn(tile, dest):
                assert tile is TURNS[nturn[0]]
                dve.sem_inc(turn_asked, 1)
                nturn[0] += 1
                for hf in range(2):
                    dve.wait_ge(turned, 2 * nturn[0] - 1 + hf)
                    ins = nc.vector.tensor_copy(dest[:, 2 * P * hf:2 * P * (hf + 1)], xt_ps[hf][:, 0:2 * P])
                step(ins)

            todo = phases()
            for n, (L, m, ls) in enumerate(todo):
                payload = m >= 15
                if L != lay:
                    turn(cur, oth)
                    cur, oth = oth, cur
                    if payload:
                        turn(cp, op)
                        cp, op = op, cp
                    lay = L
                flip = L == "T" and 7 <= m <= 13
                if flip:
                    step(TS(oth[:, :], cur[:, :], sign[:, m - 7:m - 6], None, ALU.mult))
                    cur, oth = oth, cur
                for l in ls:
                    c2, o2 = halves(cur, L, m, l), halves(oth, L, m, l)
                    if payload:
                        sw = pair_view(swap, L, m, l)
                        for (a, b, desc), s_ in zip(c2, sw):
                            TT(s_, a, b, ALU.is_lt if desc else ALU.is_gt)
                        pa, pb = halves(cp, L, 16, l)[0][0:2]
                        qa, qb = halves(op, L, 16, l)[0][0:2]
                        dl = pair_view(delta, L, 16, l)[0]
                        sf = pair_view(swap, L, 16, l)[0]
                        step(TT(dl, pb, pa, ALU.subtract))
                        ins = TT(dl, dl, sf, ALU.mult)
                        ins.then_inc(S["sort_step"], 1)
                        sstep[0] += 1
                    for n2, ((a, b, desc), (oa, ob, _)) in enumerate(zip(c2, o2)):
                        TT(oa, a, b, ALU.max if desc else ALU.min)
                        ins = TT(ob, a, b, ALU.min if desc else ALU.max)
                    step(ins)
                    cur, oth = oth, cur
                    if payload:
                        TT(qa, pa, dl, ALU.add)
                        step(TT(qb, pb, dl, ALU.subtract))
                        cp, op = op, cp
                if flip:
                    step(TS(oth[:, :], cur[:, :], sign[:, m - 7:m - 6], None, ALU.mult))
                    cur, oth = oth, cur
                if L == "T" and m == 14:
                    step(TS(key_i[:, :], cur[:, :].bitcast(I32), (1 << LOCAL_BITS) - 1, None, ALU.bitwise_and))
                    step(TT(cp[:, :], key_i[:, :], block_e[:, :], ALU.add))
                    step(TS(key_i[:, :], cur[:, :].bitcast(I32), LOCAL_BITS, None, ALU.logical_shift_right))
                    step(TS(oth[:, :], key_i[:, :], -float(KEY_SHIFT), None, ALU.add))
                    cur, oth = oth, cur
            turn(cur, oth)
            cur, oth = oth, cur
            turn(cp, op)
            cp, op = op, cp
            nc.vector.tensor_copy(target[:, :], cur[:, 0:TILES + 1]).then_inc(S["sorted_"], 1)
            dve.wait_ge(S["shifted"], 1)
            step(TT(run_on[:, :], target[:, 0:TILES], bank_a[:, 0:TILES], ALU.is_equal))
            TS(run_end[:, :], run_on[:, :], -1.0, 1.0, ALU.mult, ALU.add).then_inc(S["ends_set"], 1)
            nc.vector.scalar_tensor_tensor(out=rep_f[:, :], in0=run_on[:, :], scalar=float(1 << 20), in1=target[:, 0:TILES],
                                           op0=ALU.mult, op1=ALU.add)
            step(TS(edge_f[:, :], cp[:, 0:TILES], float(E - 1), None, ALU.min))
            dve.wait_ge(S["ranked"], 1)
            step(nc.vector.tensor_copy(rank[:, :], bank_b[:, 0:TILES]))
            dve.sem_inc(S["reverse_asked"], 1)
            for n, (column, bank) in enumerate(reversals()):
                dve.wait_ge(S["reversed_"], n + 1)
                ins = nc.vector.tensor_copy(column[:, 1:TILES:2], bank[:, 1:TILES:2])
            step(ins)
            nc.vector.tensor_copy(edge_idx[:, :], edge_f[:, :]).then_inc(S["columns_set"], 1)
            TS(target_idx[:, :], target[:, 0:TILES], float(N - 1), None, ALU.min).then_inc(S["columns_set"], 1)
            nc.vector.tensor_copy(rep_idx[:, :], rep_f[:, :]).then_inc(S["columns_set"], 1)
            nc.vector.memset(carry_mask[:, 0:1], 0.0).then_inc(S["ranks_set"], 1)
            TS(carry_mask[:, 1:TILES:2], run_on[:, 0:TILES - 1:2], is_end_p[:, 1:2], None, ALU.mult).then_inc(S["ranks_set"], 1)
            TS(carry_mask[:, 2:TILES:2], run_on[:, 1:TILES - 1:2], is_end_p[:, 0:1], None, ALU.mult).then_inc(S["ranks_set"], 1)
            nc.vector.tensor_copy(ident_bf[:, :], ident[:, :]).then_inc(S["ranks_set"], 1)
            dve.wait_ge(S["ranks_set"], 4)
            dve.wait_ge(S["weights_loaded"], 16 * WEIGHT_DMAS)
            dve.wait_ge(S["zero_set"], 5)
            dve.wait_ge(S["mean_set"], 3)
            step(TT(center_pair[:, :], ident[:, :], center_pair[:, :], ALU.subtract))
            TT(b_rz[:, :], bi_col[:, 0:2], bh_col[:, 0:2], ALU.add)
            TT(b3[:, 0:2 * HID], bi3[:, 0:2 * HID], bh3[:, 0:2 * HID], ALU.add)
            nc.vector.tensor_copy(b3[:, 2 * HID:3 * HID], bh3[:, 2 * HID:3 * HID])
            step(nc.vector.tensor_copy(b3[:, 3 * HID:4 * HID], bi3[:, 2 * HID:3 * HID]))
            step(nc.vector.tensor_copy(bias_part[:, 0, :], b3[:, :]))
            step(TT(bias_rest[:, :], b3[:, :], bias_part[:, 0, :], ALU.subtract))
            step(nc.vector.tensor_copy(bias_part[:, 1, :], bias_rest[:, :]))
            step(TT(b3[:, :], bias_rest[:, :], bias_part[:, 1, :], ALU.subtract))
            step(nc.vector.tensor_copy(bias_part[:, 2, :], b3[:, :]))
            step(TS(bias_acc[:, :], bias_part[:, 0, :], ident[0:3, 0:1], None, ALU.mult))
            step(nc.vector.scalar_tensor_tensor(out=bias_acc[:, :], in0=bias_part[:, 1, :], scalar=ident[0:3, 1:2],
                                                in1=bias_acc[:, :], op0=ALU.mult, op1=ALU.add))
            for hlf in range(2):
                ins = nc.vector.scalar_tensor_tensor(out=bias_rows[0:3, 4 * HID * hlf:4 * HID * (hlf + 1)], in0=bias_part[:, 2, :],
                                                     scalar=ident[0:3, 2:3], in1=bias_acc[:, :], op0=ALU.mult, op1=ALU.add)
            dve.wait_ge(S["rows_stored"], 16)
            nc.vector.memset(hidden[HID:HID + 1, :], 1.0).then_inc(S["bias_set"], 1)

            def finish(i, j, stage):
                if stage == 0:
                    dve.wait_ge(S["rows_ready"], i * UNITS + 3 * JT + j + 1)
                    if not (is_first(i) and j < 2):
                        dve.wait_ge(S["var_ready"], i * JT + j - 1)
                    nc.vector.tensor_tensor(sq[j % 2], y_t[j], y_t[j], ALU.mult).then_inc(S["square_ready"], 1)
                else:
                    dve.wait_ge(S["square_ready"], i * JT + j + 1)
                    nc.vector.tensor_reduce(var[:, NU * j:NU * j + NU], sq[j % 2], AX_X, ALU.add).then_inc(S["var_ready"], 1)

            def pre_tanh(i, k):
                kk_, k2 = i * UNITS + k, k % 2
                dve.wait_ge(S["r_ready"], kk_ + 1)
                if not (is_first(i) and k < 2):
                    dve.wait_ge(S["n_ready"], kk_ - 1)
                nc.vector.scalar_tensor_tensor(out=flat(pre[k2]), in0=dense_gate(k2, 2), scalar=bh_col[:, 2:3], in1=flat(RZ[k2])[:, 0:TW],
                                               op0=ALU.add, op1=ALU.mult).then_inc(S["pre_tanh_ready"], 1)

            def diff_unit(i, k, par):
                kk_, k2, j = i * UNITS + k, k % 2, k % JT
                h = x_turn[par][j] if k < JT else h_turn[j]
                dve.wait_ge(S["n_ready"], kk_ + 1)
                nc.vector.tensor_tensor(flat(dif[k2]), h, flat(cand[k2]), ALU.subtract).then_inc(S["diff_ready"], 1)

            def gate_diff(i, k, par):
                kk_, k2 = i * UNITS + k, k % 2
                dve.wait_ge(S["diff_ready"], kk_ + 1)
                dve.wait_ge(S["z_ready"], kk_ + 1)
                nc.vector.tensor_tensor(flat(dif[k2]), flat(dif[k2]), flat(RZ[k2])[:, TW:2 * TW], ALU.mult).then_inc(S["gated_ready"], 1)

            def add_unit(i, k, par):
                kk_, k2 = i * UNITS + k, k % 2
                dve.wait_ge(S["gated_ready"], kk_ + 1)
                nc.vector.tensor_tensor(h_turn[k % JT], flat(dif[k2]), flat(cand[k2]), ALU.add).then_inc(S["h_ready"], 1)

            def lagged(stage, i, k, par, lag):
                if k >= lag:
                    stage(i, k - lag, par)
                elif not is_first(i):
                    stage(i - 1, k - lag + UNITS, 1 - par)

            def dense(i, par, uses):
                for k in range(UNITS):
                    norms = () if is_first(i) else NORM_TICKS.get(k, ())

                    def root(n):
                        if k in NEWTON_TICKS and not is_first(i) and 4 * NEWTON_TICKS.index(k) + n < NEWTON_OPS:
                            newton_op(dve, "", (i - 1) * NEWTON_OPS, i * JT, 16, 4 * NEWTON_TICKS.index(k) + n)

                    pre_tanh(i, k)
                    root(0)
                    lagged(diff_unit, i, k, par, 1)
                    root(1)
                    lagged(add_unit, i, k, par, 2)
                    root(2)
                    for j, stage in norms[0:1]:
                        finish(i - 1, j, stage)
                    lagged(gate_diff, i, k, par, 1)
                    root(3)
                    for j, stage in norms[1:]:
                        finish(i - 1, j, stage)
                    if not is_first(i):
                        for j in SCALE_TICKS.get(k, ()):
                            scale_y(i - 1, j)
                    if k == 5:
                        dve.wait_ge(S[f"rows_got{par}"], (uses + 1) * (16 * GT))
                        nc.vector.tensor_copy(src_node[:, bass.ds(i * GT, GT)],
                                              rows_g[par][:, :, ED:ROW].bitcast(I32).rearrange("p u o -> p (u o)")).then_inc(S["src_saved"], 1)

            def scale_y(i, j):
                dve.wait_ge(S["newton_step"], (i + 1) * NEWTON_OPS)
                nc.vector.tensor_tensor(y_t[j], y_t[j], rstd[:, NU * j:NU * j + NU].unsqueeze(2).to_broadcast([P, NU, HID]),
                                        ALU.mult).then_inc(S["y_ready"], 1)

            run_groups(dve, dense)
            diff_unit(ITERS - 1, UNITS - 1, 0)
            add_unit(ITERS - 1, UNITS - 2, 0)
            gate_diff(ITERS - 1, UNITS - 1, 0)
            add_unit(ITERS - 1, UNITS - 1, 0)
            for j in range(JT):
                for stage in range(2):
                    finish(ITERS - 1, j, stage)
            for n in range(NEWTON_OPS):
                newton_op(dve, "", (ITERS - 1) * NEWTON_OPS, ITERS * JT, 16, n)
            for j in range(JT):
                scale_y(ITERS - 1, j)

            for j in range(JT):
                dve.wait_ge(h_stored[j][0], 16 * 2 * ITERS)
                dve.wait_ge(h_stored[j][1], 16 * ITERS)
                dve.wait_ge(y_stored[j], 16 * ITERS)
            dve.wait_ge(S["xj_stored0"], 16 * 25)
            dve.wait_ge(S["xj_stored1"], 16 * 24)
            dve.wait_ge(S["xi_stored0"], 16 * 25)
            dve.wait_ge(S["xi_stored1"], 16 * 24)
            dve.wait_ge(S["base_copied"], 2 * GROUPS)
            for t in range(STEPS):
                def copy_ranks(g, par, t=t):
                    gg = g + t * GROUPS
                    if not (t == 0 and isinstance(g, int) and g < 2):
                        dve.wait_ge(S["bcast_ready"], gg * 2 - 2)
                    nc.vector.tensor_copy(rank_g[par], rank[:, bass.ds(g * GT, GT)])
                    if not (t == 0 and isinstance(g, int) and g < 2):
                        dve.wait_ge(S["carried"], (gg - 1) * GT)
                    nc.vector.tensor_copy(mask_g[par], carry_mask[:, bass.ds(g * GT, GT)]).then_inc(S["rank_copied"], 1)

                def make_same(g, half, t=t):
                    gg = g + t * GROUPS
                    dve.wait_ge(S["bcast_ready"], gg * 2 + half + 1)
                    if not (t == 0 and is_first(g)):
                        dve.wait_ge(S["agg_summed"], gg * GT - GT + 4 * half + 4)
                    rows = bank_b[:, :].rearrange("p (u s) -> p u s", u=4)
                    c = rank[:, bass.ds(g * GT + 4 * half, 4)].unsqueeze(2).to_broadcast([P, 4, P])
                    nc.vector.tensor_tensor(same[half], rows, c, ALU.is_equal).then_inc(S["same_ready"], 1)

                def carry(g, par, u, t=t):
                    gg = g + t * GROUPS
                    dve.wait_ge(S["agg_summed"], gg * GT + u + 1)
                    if is_end(g, GROUPS) and u == GT - 1:
                        dve.sem_inc(S["carried"], 1)
                        return
                    if u == GT - 1:
                        dve.wait_ge(S["msg_ready"], gg + 2)
                        dve.wait_ge(S["rank_copied"], gg + 2)
                    elif u == 0:
                        dve.wait_ge(S["rank_copied"], gg + 1)
                    to_par, to_u = (par, u + 1) if u < GT - 1 else (1 - par, 0)
                    nc.vector.scalar_tensor_tensor(out=msg[to_par][:, to_u, :], in0=slot_sum(u), scalar=mask_g[to_par][:, to_u:to_u + 1],
                                                   in1=msg[to_par][:, to_u, :], op0=ALU.mult, op1=ALU.add).then_inc(S["carried"], 1)

                def make_msg(g, par, uses, t=t):
                    gg = g + t * GROUPS
                    if t == 0:
                        dve.wait_ge(S[f"g_loaded{par}"], (uses + 1) * 16)
                    else:
                        dve.wait_ge(S[f"g_got{par}"], (uses + (t - 1) * (25 if par == 0 else 24) + 1) * (16 * GT))
                    if not (t == 0 and isinstance(g, int) and g < 2):
                        dve.wait_ge(S["agg_summed"], gg * GT - GT)
                    nc.vector.tensor_tensor(msg[par].rearrange("p u f -> p (u f)"), g_c[par].rearrange("p u f -> p (u f)"),
                                            msg_base[:, bass.ds(g * (GT * HID), GT * HID)], ALU.mult).then_inc(S["msg_ready"], 1)

                def diff(g, par, b, t=t):
                    vec_diff(dve, "c_", (g + t * GROUPS) * 2 + b, b, xc[par][:, 4 * b:4 * b + 4, HID:2 * HID])

                def unit_end(g, par, uses, b, t=t):
                    k = (g + t * GROUPS) * 2 + b
                    hb = h_c[par][:, 4 * b:4 * b + 4, :]
                    if b == 0 and not (t == 0 and isinstance(g, int) and g < 2) and t < STEPS - 1:
                        dve.wait_ge(S[f"hc_stored{par}"], (uses + t * (25 if par == 0 else 24)) * 16)
                    vec_h(dve, "c_", k, b, hb)

                def result(g, par, uses, b, stages, t=t):
                    if t < STEPS - 1:
                        return
                    for stage in stages:
                        if b == 0 and stage == 0:
                            dve.wait_ge(S[f"xi_loaded{par}"], (uses + 1) * 16)
                            if not (isinstance(g, int) and g < 2):
                                dve.wait_ge(S[f"y_put{par}"], uses * (16 * GT))
                        half = slice(4 * b, 4 * b + 4)
                        norm_stage(dve, "c_", stage, g * 2 + b, lambda: dve.wait_ge(S["c_h_ready"], (g + t * GROUPS) * 2 + b + 1),
                                   xi_c[par][:, half, :], h_c[par][:, half, :], y_c[par][:, half, :], sq_c,
                                   ln_sum_c[:, 0:NU], var[:, NU * b:NU * b + NU])
                    if b == 1 and 4 in stages:
                        for n in range(NEWTON_OPS):
                            newton_op(dve, "c_", g * NEWTON_OPS, g * 2 + 2, 8, n)
                        dve.wait_ge(S["c_newton_step"], (g + 1) * NEWTON_OPS)
                        for c in range(2):
                            yc = y_c[par][:, 4 * c:4 * c + 4, :]
                            nc.vector.tensor_tensor(yc, yc, rstd[:, NU * c:NU * c + NU].unsqueeze(2).to_broadcast([P, NU, HID]),
                                                    ALU.mult).then_inc(S["c_y_ready"], 1)

                def slots(g, par, uses, t=t):
                    prev = not is_first(g)
                    prev2 = not (isinstance(g, int) and g < 2)
                    more = not is_end(g, GROUPS)
                    k = (g + t * GROUPS) * 2
                    carry(g, par, 0)
                    if prev2:
                        diff(g - 2, par, 0)
                        vec_r_hn(dve, "c_", k - 3, 1)
                    carry(g, par, 1)
                    if prev2:
                        vec_gate(dve, "c_", k - 4, 0)
                        vec_pre(dve, "c_", k - 3, 1)
                    carry(g, par, 2)
                    make_same(g, 1)
                    if prev2:
                        unit_end(g - 2, par, uses - 1, 0)
                        result(g - 2, par, uses - 1, 0, (0,))
                    carry(g, par, 3)
                    if more:
                        copy_ranks(g + 1, 1 - par)
                    if prev2:
                        diff(g - 2, par, 1)
                        result(g - 2, par, uses - 1, 0, (1,))
                    carry(g, par, 4)
                    if prev2:
                        vec_gate(dve, "c_", k - 3, 1)
                        result(g - 2, par, uses - 1, 0, (2,))
                    carry(g, par, 5)
                    if more:
                        make_same(g + 1, 0)
                    if prev2:
                        unit_end(g - 2, par, uses - 1, 1)
                        result(g - 2, par, uses - 1, 0, (3,))
                        result(g - 2, par, uses - 1, 1, (0,))
                        result(g - 2, par, uses - 1, 0, (4,))
                        result(g - 2, par, uses - 1, 1, (1,))
                    carry(g, par, 6)
                    if prev2:
                        result(g - 2, par, uses - 1, 1, (2, 3, 4))
                    if more:
                        make_msg(g + 1, 1 - par, uses if par == 0 else uses + 1)
                    if prev:
                        vec_r_hn(dve, "c_", k - 2, 0)
                    carry(g, par, 7)
                    if prev:
                        vec_pre(dve, "c_", k - 2, 0)

                copy_ranks(0, 0)
                make_same(0, 0)
                make_msg(0, 0, 0)
                run_groups(dve, slots)
                diff(GROUPS - 2, 1, 0)
                vec_gate(dve, "c_", (t * GROUPS + GROUPS - 2) * 2, 0)
                unit_end(GROUPS - 2, 1, 23, 0)
                result(GROUPS - 2, 1, 23, 0, range(5))
                for g, par, uses, b in ((GROUPS - 2, 1, 23, 1), (GROUPS - 1, 0, 24, 0), (GROUPS - 1, 0, 24, 1)):
                    k = (g + t * GROUPS) * 2 + b
                    vec_r_hn(dve, "c_", k, b)
                    vec_pre(dve, "c_", k, b)
                    diff(g, par, b)
                    vec_gate(dve, "c_", k, b)
                    unit_end(g, par, uses, b)
                    result(g, par, uses, b, range(5))


def kernel(**inputs):
    import numpy as np
    import concourse.bacc as bacc
    from concourse.bass_utils import run_bass_kernel_spmd

    nc = bacc.Bacc("TRN2", target_bir_lowering=False, num_devices=1)
    g = {k: np.asarray(v) for k, v in inputs.items()}
    arrays = {
        "x": g["x"], "src": g["src"], "dst": g["dst"], "attr": g["edge_attr_32"],
        "w1t": g["L0_gnn_W1"].T, "b1": g["L0_gnn_b1"], "w2t": g["L0_gnn_W2"].T, "b2": g["L0_gnn_b2"],
        "wit": g["L0_gnn_W_ih"].T, "bih": g["L0_gnn_b_ih"], "wht": g["L0_gnn_W_hh"].T, "bhh": g["L0_gnn_b_hh"],
    }
    arrays = {k + "_dram": np.ascontiguousarray(v) for k, v in arrays.items()}
    args = [nc.dram_tensor(k, v.shape, mybir.dt.from_np(v.dtype), kind="ExternalInput").ap() for k, v in arrays.items()]
    out = nc.dram_tensor("out_0_dram", (N, HID), F32, kind="ExternalOutput").ap()
    gnn_program(nc, *args, out)
    r = run_bass_kernel_spmd(nc, [arrays], core_ids=[0])
    return r.results[0]["out_0_dram"]
```
